# Optimizing a Trainium2 kernel written in Bass

```python
import numpy as np
import jax
import jax.numpy as jnp

def _softmax(x, axis=-1):
    return jax.nn.softmax(x, axis=axis)

def _gelu(x):
    return jax.nn.gelu(x, approximate=True)

def _silu(x):
    return jax.nn.silu(x)

def _sigmoid(x):
    return jax.nn.sigmoid(x)

def _layernorm(x, axis=-1, eps=1e-05):
    m = jnp.mean(x, axis=axis, keepdims=True)
    v = jnp.var(x, axis=axis, keepdims=True)
    return (x - m) / jnp.sqrt(v + eps)

def _scatter_add(tgt, idx, src, axis=0):
    return tgt.at[idx].add(src)

def _segment_sum(src, seg, n):
    return jax.ops.segment_sum(src, seg, n)
kernel_name = 'mk_audio_tower_d4_tok_audfeat512_r4_08429e'

def setup_inputs(seed: int=0):
    np.random.seed(seed)
    _w = jnp.asarray

    def _rec_inputs():
        import jax
        import jax.numpy as jnp
        _rk = jax.random.key(seed)
        x = -0.00190633 + 1.00279 * jax.random.normal(jax.random.fold_in(_rk, 1), (128, 64, 7), jnp.float32)
        return x
    x = _rec_inputs()

    def _L0_tok_setup():
        import jax, jax.numpy as jnp
        import numpy as np
        SIG_DEPTH = 4

        def _outer(a, b):
            return (a[:, :, None] * b[:, None, :]).reshape(a.shape[0], -1)
        key = jax.random.key(seed)
        k1, k2 = jax.random.split(key)
        B, L, Cin = (64, 64, 7)
        out_dim = 128
        C = Cin + 1
        sig_channels = sum((C ** k for k in range(1, SIG_DEPTH + 1)))
        inp = jax.random.normal(k1, (B, L, Cin), dtype=jnp.float32)
        W = jax.random.normal(k2, (out_dim, sig_channels), dtype=jnp.float32) * 0.02
        b = jnp.zeros((out_dim,), dtype=jnp.float32)
        return {'inp': inp, 'W': W, 'b': b}
    _L0_tok_all = _L0_tok_setup()
    _L0_tok_in = {k: v for k, v in _L0_tok_all.items() if k in ('W', 'b')}
    del _L0_tok_all

    def _L0_attn_setup():
        import jax, jax.numpy as jnp
        import numpy as np
        B, S, D, H = (4, 512, 128, 8)
        KD = D // H
        FFN = 4 * D

        def _ln(x, g, b, eps):
            mu = x.mean(-1, keepdims=True)
            var = ((x - mu) ** 2).mean(-1, keepdims=True)
            return (x - mu) / jnp.sqrt(var + eps) * g + b
        key = jax.random.key(seed)
        ks = jax.random.split(key, 8)

        def lin(k, o, i, scale=0.02):
            k1, k2 = jax.random.split(k)
            return (jax.random.normal(k1, (o, i), jnp.float32) * scale, jax.random.normal(k2, (o,), jnp.float32) * scale)
        wq, bq = lin(ks[0], D, D)
        wk, bk = lin(ks[1], D, D)
        wv, bv = lin(ks[2], D, D)
        wg, bg = lin(ks[3], D, D)
        wo, bo = lin(ks[4], D, D)
        fc1_w, fc1_b = lin(ks[5], FFN, D)
        fc2_w, fc2_b = lin(ks[6], D, FFN)
        return {'src': jax.random.normal(ks[7], (B, S, D), jnp.float32), 'mask': jnp.zeros((S, S), jnp.bool_), 'padding_mask': jnp.zeros((B, S), jnp.bool_), 'wq': wq, 'bq': bq, 'wk': wk, 'bk': bk, 'wv': wv, 'bv': bv, 'wg': wg, 'bg': bg, 'wo': wo, 'bo': bo, 'fc1_w': fc1_w, 'fc1_b': fc1_b, 'fc2_w': fc2_w, 'fc2_b': fc2_b, 'ln_ffn_g': jnp.ones((FFN,), jnp.float32), 'ln_ffn_b': jnp.zeros((FFN,), jnp.float32), 'n0_g': jnp.ones((D,), jnp.float32), 'n0_b': jnp.zeros((D,), jnp.float32), 'n1_g': jnp.ones((D,), jnp.float32), 'n1_b': jnp.zeros((D,), jnp.float32)}
    _L0_attn_all = _L0_attn_setup()
    _L0_attn_in = {k: v for k, v in _L0_attn_all.items() if k in ('mask', 'padding_mask', 'wq', 'bq', 'wk', 'bk', 'wv', 'bv', 'wg', 'bg', 'wo', 'bo', 'fc1_w', 'fc1_b', 'fc2_w', 'fc2_b', 'ln_ffn_g', 'ln_ffn_b', 'n0_g', 'n0_b', 'n1_g', 'n1_b')}
    del _L0_attn_all

    def _L0_ffn_setup():
        import jax, jax.numpy as jnp
        import numpy as np
        TOP_K = 2

        def quick_gelu(x):
            return x * jax.nn.sigmoid(1.702 * x)
        key = jax.random.key(seed)
        ks = jax.random.split(key, 6)
        B, S, H, I, E = (8, 1024, 128, 256, 8)
        s_h = 1.0 / np.sqrt(H).astype(np.float32)
        s_i = 1.0 / np.sqrt(I).astype(np.float32)
        return {'hidden_states': jax.random.normal(ks[0], (B, S, H), jnp.float32), 'router_w': jax.random.normal(ks[1], (H, E), jnp.float32) * s_h, 'router_b': jnp.zeros((E,), jnp.float32), 'gate_up_proj': jax.random.normal(ks[2], (E, H, 2 * I), jnp.float32) * s_h, 'gate_up_proj_bias': jnp.zeros((E, 2 * I), jnp.float32), 'down_proj': jax.random.normal(ks[3], (E, I, H), jnp.float32) * s_i, 'down_proj_bias': jnp.zeros((E, H), jnp.float32)}
    _L0_ffn_all = _L0_ffn_setup()
    _L0_ffn_in = {k: v for k, v in _L0_ffn_all.items() if k in ('router_w', 'router_b', 'gate_up_proj', 'gate_up_proj_bias', 'down_proj', 'down_proj_bias')}
    del _L0_ffn_all

    def _L1_attn_setup():
        import jax, jax.numpy as jnp
        import numpy as np
        D_MODEL = 128
        N_HEADS = 8
        DH = D_MODEL // N_HEADS
        Q_PROJ = D_MODEL // 2
        KV_PROJ = 2 * D_MODEL // 3
        ROPE_DIM = D_MODEL // 8
        R = ROPE_DIM // N_HEADS
        THETA = 10000.0
        EPS = 1e-05
        B, S = (2, 512)

        def layernorm(x, g, b):
            m = jnp.mean(x, axis=-1, keepdims=True)
            v = jnp.var(x, axis=-1, keepdims=True)
            return (x - m) * jax.lax.rsqrt(v + EPS) * g + b

        def rope_cos_sin(seq_len, dtype):
            inv_freq = THETA ** (-jnp.arange(0, R, 2, dtype=jnp.float32) / R)
            ang = jnp.arange(seq_len, dtype=jnp.float32)[:, None] * inv_freq
            cos = jnp.concatenate([jnp.cos(ang), jnp.cos(ang)], axis=-1)
            sin = jnp.concatenate([jnp.sin(ang), jnp.sin(ang)], axis=-1)
            return (cos.astype(dtype), sin.astype(dtype))

        def apply_rope(x, cos, sin):
            x1, x2 = jnp.split(x, 2, axis=-1)
            rot = jnp.concatenate([-x2, x1], axis=-1)
            return x * cos + rot * sin

        def _reference_tuple_inner(x, W_dq, W_uq, W_qr, W_dkv, W_ukv, W_kr, W_o, q_ln_g, q_ln_b, kv_ln_g, kv_ln_b):
            b, s, d = x.shape
            cq = layernorm(x @ W_dq, q_ln_g, q_ln_b)
            Q = (cq @ W_uq).reshape(b, s, N_HEADS, DH).transpose(0, 2, 1, 3)
            Qr = (cq @ W_qr).reshape(b, s, N_HEADS, R).transpose(0, 2, 1, 3)
            cos, sin = rope_cos_sin(s, x.dtype)
            Qr = apply_rope(Qr, cos, sin)
            q = jnp.concatenate([Q, Qr], axis=-1)
            ckv = layernorm(x @ W_dkv, kv_ln_g, kv_ln_b)
            KV = ckv @ W_ukv
            K, V = (KV[..., :D_MODEL], KV[..., D_MODEL:])
            K = K.reshape(b, s, N_HEADS, DH).transpose(0, 2, 1, 3)
            Kr = (x @ W_kr).reshape(b, s, N_HEADS, R).transpose(0, 2, 1, 3)
            Kr = apply_rope(Kr, cos, sin)
            k = jnp.concatenate([K, Kr], axis=-1)
            v = V.reshape(b, s, N_HEADS, DH).transpose(0, 2, 1, 3)
            scale = 1.0 / jnp.sqrt(jnp.asarray(DH + R, x.dtype))
            scores = jnp.einsum('bhqd,bhkd->bhqk', q, k) * scale
            mask = jnp.tril(jnp.ones((s, s), dtype=bool))
            scores = jnp.where(mask, scores, jnp.finfo(scores.dtype).min)
            attn = jax.nn.softmax(scores, axis=-1)
            out = jnp.einsum('bhqk,bhkd->bhqd', attn, v)
            out = out.transpose(0, 2, 1, 3).reshape(b, s, d)
            return (out @ W_o.T, ckv)
        key = jax.random.key(seed)
        ks = jax.random.split(key, 9)
        p = lambda k, shape: 0.01 * jax.random.normal(k, shape, jnp.float32)
        return {'x': jax.random.normal(ks[0], (B, S, D_MODEL), jnp.float32), 'W_dq': p(ks[1], (D_MODEL, Q_PROJ)), 'W_uq': p(ks[2], (Q_PROJ, D_MODEL)), 'W_qr': p(ks[3], (Q_PROJ, ROPE_DIM)), 'W_dkv': p(ks[4], (D_MODEL, KV_PROJ)), 'W_ukv': p(ks[5], (KV_PROJ, 2 * D_MODEL)), 'W_kr': p(ks[6], (D_MODEL, ROPE_DIM)), 'W_o': p(ks[7], (D_MODEL, D_MODEL)), 'q_ln_g': jnp.ones((Q_PROJ,), jnp.float32), 'q_ln_b': jnp.zeros((Q_PROJ,), jnp.float32), 'kv_ln_g': jnp.ones((KV_PROJ,), jnp.float32), 'kv_ln_b': jnp.zeros((KV_PROJ,), jnp.float32)}
    _L1_attn_all = _L1_attn_setup()
    _L1_attn_in = {k: v for k, v in _L1_attn_all.items() if k in ('W_dq', 'W_uq', 'W_qr', 'W_dkv', 'W_ukv', 'W_kr', 'W_o', 'q_ln_g', 'q_ln_b', 'kv_ln_g', 'kv_ln_b')}
    del _L1_attn_all

    def _L1_ffn_setup():
        import jax, jax.numpy as jnp
        import numpy as np
        B, S, H, E, K = (8, 1024, 128, 8, 2)
        key = jax.random.key(seed)
        ks = jax.random.split(key, 7)
        s_h = 1.0 / np.sqrt(H)
        s_2h = 1.0 / np.sqrt(2 * H)
        return {'x': jax.random.normal(ks[0], (B, S, H), dtype=jnp.float32), 'gate_w': jax.random.uniform(ks[1], (H, E), minval=-s_h, maxval=s_h, dtype=jnp.float32), 'gate_b': jax.random.uniform(ks[2], (E,), minval=-s_h, maxval=s_h, dtype=jnp.float32), 'w1': jax.random.uniform(ks[3], (E, H, 2 * H), minval=-s_h, maxval=s_h, dtype=jnp.float32), 'b1': jax.random.uniform(ks[4], (E, 2 * H), minval=-s_h, maxval=s_h, dtype=jnp.float32), 'w2': jax.random.uniform(ks[5], (E, 2 * H, H), minval=-s_2h, maxval=s_2h, dtype=jnp.float32), 'b2': jax.random.uniform(ks[6], (E, H), minval=-s_2h, maxval=s_2h, dtype=jnp.float32)}
    _L1_ffn_all = _L1_ffn_setup()
    _L1_ffn_in = {k: v for k, v in _L1_ffn_all.items() if k in ('gate_w', 'gate_b', 'w1', 'b1', 'w2', 'b2')}
    del _L1_ffn_all

    def _L2_attn_setup():
        import jax, jax.numpy as jnp
        import numpy as np
        B, T, HID, H = (4, 512, 128, 4)
        DK, DV = (64, 128)
        GATE_LOW_RANK = 16
        GATE_LOGIT_NORM = 16.0
        RMS_EPS = 1e-05
        key = jax.random.key(seed)
        ks = jax.random.split(key, 9)
        s = 0.02
        f = jnp.float32
        return {'x': jax.random.normal(ks[0], (B, T, HID), f), 'Wq': jax.random.normal(ks[1], (HID, H * DK), f) * s, 'Wk': jax.random.normal(ks[2], (HID, H * DK), f) * s, 'Wv': jax.random.normal(ks[3], (HID, H * DV), f) * s, 'Wg': jax.random.normal(ks[4], (HID, H * DV), f) * s, 'Wo': jax.random.normal(ks[5], (H * DV, HID), f) * s, 'Wgk1': jax.random.normal(ks[6], (HID, GATE_LOW_RANK), f) * s, 'Wgk2': jax.random.normal(ks[7], (GATE_LOW_RANK, H * DK), f) * s, 'bgk2': jnp.zeros((H * DK,), f), 'rms_w': jnp.ones((DV,), f)}
    _L2_attn_all = _L2_attn_setup()
    _L2_attn_in = {k: v for k, v in _L2_attn_all.items() if k in ('Wq', 'Wk', 'Wv', 'Wg', 'Wo', 'Wgk1', 'Wgk2', 'bgk2', 'rms_w')}
    del _L2_attn_all

    def _L2_ffn_setup():
        import jax, jax.numpy as jnp
        import numpy as np
        from jax import lax
        N, M, DIM, HEADS, TOPK = (4, 512, 128, 8, 16)

        def _split_heads(t, h):
            n, m, c = t.shape
            return t.reshape(n, m, h, c // h).transpose(0, 2, 1, 3).reshape(n * h, m, c // h)
        key = jax.random.key(seed)
        ks = jax.random.split(key, 7)
        f = lambda k, s, sc=1.0: jax.random.normal(k, s, dtype=jnp.float32) * sc
        return {'x': f(ks[0], (N, M, DIM)), 'pos_w': f(ks[1], (DIM, 1, 3), 0.1), 'pos_b': f(ks[2], (DIM,), 0.02), 'qkv_w': f(ks[3], (3 * DIM, DIM), 0.02), 'qkv_b': f(ks[4], (3 * DIM,), 0.02), 'wo_w': f(ks[5], (DIM, DIM), 0.02), 'wo_b': f(ks[6], (DIM,), 0.02)}
    _L2_ffn_all = _L2_ffn_setup()
    _L2_ffn_in = {k: v for k, v in _L2_ffn_all.items() if k in ('pos_w', 'pos_b', 'qkv_w', 'qkv_b', 'wo_w', 'wo_b')}
    del _L2_ffn_all

    def _L3_attn_setup():
        import jax, jax.numpy as jnp
        import numpy as np
        B, N, C = (2, 512, 128)
        HEADS, WINDOW, R = (8, 64, 8)
        LORA_SCALE = 2.0 / R
        key = jax.random.key(seed)
        ks = jax.random.split(key, 8)

        def w(k, shp, sc=0.02):
            return jax.random.normal(k, shp, jnp.float32) * sc
        return {'x': jax.random.normal(ks[0], (B, N, C), jnp.float32), 'w_qkv': w(ks[1], (C, 3 * C)), 'lora_A_qkv': w(ks[2], (C, R), 0.01), 'lora_B_qkv': w(ks[3], (R, 3 * C), 0.01), 'w_out': w(ks[4], (C, C)), 'b_out': jnp.zeros((C,), jnp.float32), 'lora_A_out': w(ks[5], (C, R), 0.01), 'lora_B_out': w(ks[6], (R, C), 0.01)}
    _L3_attn_all = _L3_attn_setup()
    _L3_attn_in = {k: v for k, v in _L3_attn_all.items() if k in ('w_qkv', 'lora_A_qkv', 'lora_B_qkv', 'w_out', 'b_out', 'lora_A_out', 'lora_B_out')}
    del _L3_attn_all

    def _L3_ffn_setup():
        import jax, jax.numpy as jnp
        import numpy as np
        from functools import partial
        EPS = 1e-05
        ROPE_THETA = 10000.0
        TOP_K = 2

        def rmsnorm(x, w):
            var = jnp.mean(x * x, axis=-1, keepdims=True)
            return x * jax.lax.rsqrt(var + EPS) * w

        def apply_rope(x):
            B, S, H, dh = x.shape
            inv_freq = 1.0 / ROPE_THETA ** (jnp.arange(0, dh, 2, dtype=jnp.float32) / dh)
            ang = jnp.arange(S, dtype=jnp.float32)[:, None] * inv_freq[None, :]
            cos = jnp.cos(ang)[None, :, None, :]
            sin = jnp.sin(ang)[None, :, None, :]
            x1 = x[..., 0::2]
            x2 = x[..., 1::2]
            r1 = x1 * cos - x2 * sin
            r2 = x1 * sin + x2 * cos
            return jnp.stack([r1, r2], axis=-1).reshape(x.shape)

        def mha_rope(xn, wq, wk, wv, wo, num_heads):
            B, S, D = xn.shape
            dh = D // num_heads
            q = (xn @ wq).reshape(B, S, num_heads, dh)
            k = (xn @ wk).reshape(B, S, num_heads, dh)
            v = (xn @ wv).reshape(B, S, num_heads, dh)
            q = apply_rope(q)
            k = apply_rope(k)
            scores = jnp.einsum('bqhd,bkhd->bhqk', q, k) / jnp.sqrt(jnp.float32(dh))
            causal = jnp.tril(jnp.ones((S, S), dtype=bool))
            scores = jnp.where(causal[None, None], scores, jnp.float32(-1000000000.0))
            attn = jax.nn.softmax(scores, axis=-1)
            out = jnp.einsum('bhqk,bkhd->bqhd', attn, v).reshape(B, S, D)
            return out @ wo

        def moe_ffn(hn, router_w, w1, w2):
            B, S, D = hn.shape
            E = router_w.shape[1]
            t = hn.reshape(B * S, D)
            T = t.shape[0]
            logits = t @ router_w
            probs = jax.nn.softmax(logits, axis=-1)
            vals, idx = jax.lax.top_k(probs, TOP_K)
            gates = vals / jnp.sum(vals, axis=-1, keepdims=True)
            gates_dense = jnp.zeros((T, E), dtype=t.dtype).at[jnp.arange(T)[:, None], idx].add(gates)
            out = jnp.zeros_like(t)
            for e in range(E):
                ge = gates_dense[:, e:e + 1]
                h = jax.nn.gelu(t @ w1[e], approximate=False)
                out = out + ge * (h @ w2[e])
            return out.reshape(B, S, D)
        key = jax.random.key(seed)
        B, S, D, H, E = (4, 512, 128, 8, 8)
        Hf = 4 * D
        ks = jax.random.split(key, 10)
        s = 0.02
        return {'x': jax.random.normal(ks[0], (B, S, D), dtype=jnp.float32), 'attn_norm_w': jnp.ones((D,), dtype=jnp.float32), 'wq': jax.random.normal(ks[1], (D, D), dtype=jnp.float32) * s, 'wk': jax.random.normal(ks[2], (D, D), dtype=jnp.float32) * s, 'wv': jax.random.normal(ks[3], (D, D), dtype=jnp.float32) * s, 'wo': jax.random.normal(ks[4], (D, D), dtype=jnp.float32) * s, 'ffn_norm_w': jnp.ones((D,), dtype=jnp.float32), 'router_w': jax.random.normal(ks[5], (D, E), dtype=jnp.float32) * s, 'w1': jax.random.normal(ks[6], (E, D, Hf), dtype=jnp.float32) * s, 'w2': jax.random.normal(ks[7], (E, Hf, D), dtype=jnp.float32) * s}
    _L3_ffn_all = _L3_ffn_setup()
    _L3_ffn_in = {k: v for k, v in _L3_ffn_all.items() if k in ('attn_norm_w', 'wq', 'wk', 'wv', 'wo', 'ffn_norm_w', 'router_w', 'w1', 'w2')}
    del _L3_ffn_all
    return {'x': x, 'L0_tok_W': _L0_tok_in['W'], 'L0_tok_b': _L0_tok_in['b'], 'L0_attn_mask': _L0_attn_in['mask'], 'L0_attn_padding_mask': _L0_attn_in['padding_mask'], 'L0_attn_wq': _L0_attn_in['wq'], 'L0_attn_bq': _L0_attn_in['bq'], 'L0_attn_wk': _L0_attn_in['wk'], 'L0_attn_bk': _L0_attn_in['bk'], 'L0_attn_wv': _L0_attn_in['wv'], 'L0_attn_bv': _L0_attn_in['bv'], 'L0_attn_wg': _L0_attn_in['wg'], 'L0_attn_bg': _L0_attn_in['bg'], 'L0_attn_wo': _L0_attn_in['wo'], 'L0_attn_bo': _L0_attn_in['bo'], 'L0_attn_fc1_w': _L0_attn_in['fc1_w'], 'L0_attn_fc1_b': _L0_attn_in['fc1_b'], 'L0_attn_fc2_w': _L0_attn_in['fc2_w'], 'L0_attn_fc2_b': _L0_attn_in['fc2_b'], 'L0_attn_ln_ffn_g': _L0_attn_in['ln_ffn_g'], 'L0_attn_ln_ffn_b': _L0_attn_in['ln_ffn_b'], 'L0_attn_n0_g': _L0_attn_in['n0_g'], 'L0_attn_n0_b': _L0_attn_in['n0_b'], 'L0_attn_n1_g': _L0_attn_in['n1_g'], 'L0_attn_n1_b': _L0_attn_in['n1_b'], 'L0_ffn_router_w': _L0_ffn_in['router_w'], 'L0_ffn_router_b': _L0_ffn_in['router_b'], 'L0_ffn_gate_up_proj': _L0_ffn_in['gate_up_proj'], 'L0_ffn_gate_up_proj_bias': _L0_ffn_in['gate_up_proj_bias'], 'L0_ffn_down_proj': _L0_ffn_in['down_proj'], 'L0_ffn_down_proj_bias': _L0_ffn_in['down_proj_bias'], 'L1_attn_W_dq': _L1_attn_in['W_dq'], 'L1_attn_W_uq': _L1_attn_in['W_uq'], 'L1_attn_W_qr': _L1_attn_in['W_qr'], 'L1_attn_W_dkv': _L1_attn_in['W_dkv'], 'L1_attn_W_ukv': _L1_attn_in['W_ukv'], 'L1_attn_W_kr': _L1_attn_in['W_kr'], 'L1_attn_W_o': _L1_attn_in['W_o'], 'L1_attn_q_ln_g': _L1_attn_in['q_ln_g'], 'L1_attn_q_ln_b': _L1_attn_in['q_ln_b'], 'L1_attn_kv_ln_g': _L1_attn_in['kv_ln_g'], 'L1_attn_kv_ln_b': _L1_attn_in['kv_ln_b'], 'L1_ffn_gate_w': _L1_ffn_in['gate_w'], 'L1_ffn_gate_b': _L1_ffn_in['gate_b'], 'L1_ffn_w1': _L1_ffn_in['w1'], 'L1_ffn_b1': _L1_ffn_in['b1'], 'L1_ffn_w2': _L1_ffn_in['w2'], 'L1_ffn_b2': _L1_ffn_in['b2'], 'L2_attn_Wq': _L2_attn_in['Wq'], 'L2_attn_Wk': _L2_attn_in['Wk'], 'L2_attn_Wv': _L2_attn_in['Wv'], 'L2_attn_Wg': _L2_attn_in['Wg'], 'L2_attn_Wo': _L2_attn_in['Wo'], 'L2_attn_Wgk1': _L2_attn_in['Wgk1'], 'L2_attn_Wgk2': _L2_attn_in['Wgk2'], 'L2_attn_bgk2': _L2_attn_in['bgk2'], 'L2_attn_rms_w': _L2_attn_in['rms_w'], 'L2_ffn_pos_w': _L2_ffn_in['pos_w'], 'L2_ffn_pos_b': _L2_ffn_in['pos_b'], 'L2_ffn_qkv_w': _L2_ffn_in['qkv_w'], 'L2_ffn_qkv_b': _L2_ffn_in['qkv_b'], 'L2_ffn_wo_w': _L2_ffn_in['wo_w'], 'L2_ffn_wo_b': _L2_ffn_in['wo_b'], 'L3_attn_w_qkv': _L3_attn_in['w_qkv'], 'L3_attn_lora_A_qkv': _L3_attn_in['lora_A_qkv'], 'L3_attn_lora_B_qkv': _L3_attn_in['lora_B_qkv'], 'L3_attn_w_out': _L3_attn_in['w_out'], 'L3_attn_b_out': _L3_attn_in['b_out'], 'L3_attn_lora_A_out': _L3_attn_in['lora_A_out'], 'L3_attn_lora_B_out': _L3_attn_in['lora_B_out'], 'L3_ffn_attn_norm_w': _L3_ffn_in['attn_norm_w'], 'L3_ffn_wq': _L3_ffn_in['wq'], 'L3_ffn_wk': _L3_ffn_in['wk'], 'L3_ffn_wv': _L3_ffn_in['wv'], 'L3_ffn_wo': _L3_ffn_in['wo'], 'L3_ffn_ffn_norm_w': _L3_ffn_in['ffn_norm_w'], 'L3_ffn_router_w': _L3_ffn_in['router_w'], 'L3_ffn_w1': _L3_ffn_in['w1'], 'L3_ffn_w2': _L3_ffn_in['w2']}

def reference(x, L0_tok_W, L0_tok_b, L0_attn_mask, L0_attn_padding_mask, L0_attn_wq, L0_attn_bq, L0_attn_wk, L0_attn_bk, L0_attn_wv, L0_attn_bv, L0_attn_wg, L0_attn_bg, L0_attn_wo, L0_attn_bo, L0_attn_fc1_w, L0_attn_fc1_b, L0_attn_fc2_w, L0_attn_fc2_b, L0_attn_ln_ffn_g, L0_attn_ln_ffn_b, L0_attn_n0_g, L0_attn_n0_b, L0_attn_n1_g, L0_attn_n1_b, L0_ffn_router_w, L0_ffn_router_b, L0_ffn_gate_up_proj, L0_ffn_gate_up_proj_bias, L0_ffn_down_proj, L0_ffn_down_proj_bias, L1_attn_W_dq, L1_attn_W_uq, L1_attn_W_qr, L1_attn_W_dkv, L1_attn_W_ukv, L1_attn_W_kr, L1_attn_W_o, L1_attn_q_ln_g, L1_attn_q_ln_b, L1_attn_kv_ln_g, L1_attn_kv_ln_b, L1_ffn_gate_w, L1_ffn_gate_b, L1_ffn_w1, L1_ffn_b1, L1_ffn_w2, L1_ffn_b2, L2_attn_Wq, L2_attn_Wk, L2_attn_Wv, L2_attn_Wg, L2_attn_Wo, L2_attn_Wgk1, L2_attn_Wgk2, L2_attn_bgk2, L2_attn_rms_w, L2_ffn_pos_w, L2_ffn_pos_b, L2_ffn_qkv_w, L2_ffn_qkv_b, L2_ffn_wo_w, L2_ffn_wo_b, L3_attn_w_qkv, L3_attn_lora_A_qkv, L3_attn_lora_B_qkv, L3_attn_w_out, L3_attn_b_out, L3_attn_lora_A_out, L3_attn_lora_B_out, L3_ffn_attn_norm_w, L3_ffn_wq, L3_ffn_wk, L3_ffn_wv, L3_ffn_wo, L3_ffn_ffn_norm_w, L3_ffn_router_w, L3_ffn_w1, L3_ffn_w2):
    import jax
    import jax.numpy as jnp

    def _L0_tok_ref(inp, W, b):
        import jax, jax.numpy as jnp
        import numpy as np
        SIG_DEPTH = 4

        def _outer(a, b):
            return (a[:, :, None] * b[:, None, :]).reshape(a.shape[0], -1)
        B, L, Cin = inp.shape
        t = jnp.broadcast_to(jnp.linspace(0.0, 1.0, L, dtype=inp.dtype)[None, :, None], (B, L, 1))
        x = jnp.concatenate([t, inp], axis=-1)
        C = Cin + 1
        d = SIG_DEPTH
        dx = jnp.transpose(x[:, 1:] - x[:, :-1], (1, 0, 2))
        init = tuple((jnp.zeros((B, C ** (k + 1)), x.dtype) for k in range(d)))

        def step(levels, v):
            e = [v]
            for k in range(1, d):
                e.append(_outer(e[-1], v) / (k + 1))
            new = []
            for k in range(d):
                acc = levels[k] + e[k]
                for i in range(k):
                    acc = acc + _outer(levels[i], e[k - 1 - i])
                new.append(acc)
            sig = jnp.concatenate(new, axis=-1)
            return (tuple(new), sig)
        _, sigs = jax.lax.scan(step, init, dx)
        sigs = jnp.transpose(sigs, (1, 0, 2))
        return sigs @ W.T + b

    def _L0_attn_ref(src, mask, padding_mask, wq, bq, wk, bk, wv, bv, wg, bg, wo, bo, fc1_w, fc1_b, fc2_w, fc2_b, ln_ffn_g, ln_ffn_b, n0_g, n0_b, n1_g, n1_b):
        import jax, jax.numpy as jnp
        import numpy as np
        B, S, D, H = (4, 512, 128, 8)
        KD = D // H
        FFN = 4 * D

        def _ln(x, g, b, eps):
            mu = x.mean(-1, keepdims=True)
            var = ((x - mu) ** 2).mean(-1, keepdims=True)
            return (x - mu) / jnp.sqrt(var + eps) * g + b
        b, s, d = src.shape
        idx = jnp.arange(s)
        diff = (idx[:, None] - idx[None, :]).astype(src.dtype)
        decay = jnp.log(1.0 - 2.0 ** (-5.0 - jnp.arange(H, dtype=src.dtype)))
        dm = jnp.where(diff[None] >= 0, jnp.exp(diff[None] * decay[:, None, None]), 0.0)
        dm = dm / jnp.sqrt(dm.sum(-1, keepdims=True))
        q = (src @ wq.T + bq).reshape(b, s, H, KD).transpose(0, 2, 1, 3)
        k = ((src @ wk.T + bk) * KD ** (-0.5)).reshape(b, s, H, KD).transpose(0, 2, 1, 3)
        v = src @ wv.T + bv
        g = src @ wg.T + bg
        qk = jnp.einsum('bhid,bhjd->bhij', q, k) + dm[None]
        den = jnp.maximum(jnp.abs(jax.lax.stop_gradient(qk).sum(-1, keepdims=True)), 1.0)
        qk = qk / den
        vr = v.reshape(b, s, H, KD).transpose(0, 2, 1, 3)
        o = jnp.einsum('bhij,bhjd->bhid', qk, vr).transpose(0, 2, 1, 3)
        mu = o.mean(-1, keepdims=True)
        o = (o - mu) / jnp.sqrt(((o - mu) ** 2).mean(-1, keepdims=True) + 1e-06)
        o = jax.nn.silu(g) * o.reshape(b, s, d)
        o = o @ wo.T + bo
        x = _ln(src + o, n0_g, n0_b, 1e-05)
        h = jax.nn.gelu(x @ fc1_w.T + fc1_b, approximate=False)
        h = _ln(h, ln_ffn_g, ln_ffn_b, 1e-06)
        h = h @ fc2_w.T + fc2_b
        return _ln(x + h, n1_g, n1_b, 1e-05)

    def _L0_ffn_ref(hidden_states, router_w, router_b, gate_up_proj, gate_up_proj_bias, down_proj, down_proj_bias):
        import jax, jax.numpy as jnp
        import numpy as np
        TOP_K = 2

        def quick_gelu(x):
            return x * jax.nn.sigmoid(1.702 * x)
        B, S, H = hidden_states.shape
        E = router_b.shape[0]
        x = hidden_states.reshape(-1, H)
        T = x.shape[0]
        logits = x @ router_w + router_b
        top_w, sel = jax.lax.top_k(logits, TOP_K)
        top_w = jax.nn.softmax(top_w, axis=-1)
        tok_w = jnp.zeros((T, E), x.dtype).at[jnp.arange(T)[:, None], sel].add(top_w)

        def body(acc, params):
            Wgu, bgu, Wd, bd, w_e = params
            gu = x @ Wgu + bgu
            gate, up = jnp.split(gu, 2, axis=-1)
            act = (up + 1.0) * quick_gelu(gate)
            out = act @ Wd + bd
            return (acc + out * w_e[:, None], None)
        acc0 = jnp.zeros((T, H), x.dtype)
        acc, _ = jax.lax.scan(body, acc0, (gate_up_proj, gate_up_proj_bias, down_proj, down_proj_bias, tok_w.T))
        return acc.reshape(B, S, H)

    def _L1_attn_ref(x, W_dq, W_uq, W_qr, W_dkv, W_ukv, W_kr, W_o, q_ln_g, q_ln_b, kv_ln_g, kv_ln_b):
        import jax, jax.numpy as jnp
        import numpy as np
        D_MODEL = 128
        N_HEADS = 8
        DH = D_MODEL // N_HEADS
        Q_PROJ = D_MODEL // 2
        KV_PROJ = 2 * D_MODEL // 3
        ROPE_DIM = D_MODEL // 8
        R = ROPE_DIM // N_HEADS
        THETA = 10000.0
        EPS = 1e-05
        B, S = (2, 512)

        def layernorm(x, g, b):
            m = jnp.mean(x, axis=-1, keepdims=True)
            v = jnp.var(x, axis=-1, keepdims=True)
            return (x - m) * jax.lax.rsqrt(v + EPS) * g + b

        def rope_cos_sin(seq_len, dtype):
            inv_freq = THETA ** (-jnp.arange(0, R, 2, dtype=jnp.float32) / R)
            ang = jnp.arange(seq_len, dtype=jnp.float32)[:, None] * inv_freq
            cos = jnp.concatenate([jnp.cos(ang), jnp.cos(ang)], axis=-1)
            sin = jnp.concatenate([jnp.sin(ang), jnp.sin(ang)], axis=-1)
            return (cos.astype(dtype), sin.astype(dtype))

        def apply_rope(x, cos, sin):
            x1, x2 = jnp.split(x, 2, axis=-1)
            rot = jnp.concatenate([-x2, x1], axis=-1)
            return x * cos + rot * sin

        def _reference_tuple_inner(x, W_dq, W_uq, W_qr, W_dkv, W_ukv, W_kr, W_o, q_ln_g, q_ln_b, kv_ln_g, kv_ln_b):
            b, s, d = x.shape
            cq = layernorm(x @ W_dq, q_ln_g, q_ln_b)
            Q = (cq @ W_uq).reshape(b, s, N_HEADS, DH).transpose(0, 2, 1, 3)
            Qr = (cq @ W_qr).reshape(b, s, N_HEADS, R).transpose(0, 2, 1, 3)
            cos, sin = rope_cos_sin(s, x.dtype)
            Qr = apply_rope(Qr, cos, sin)
            q = jnp.concatenate([Q, Qr], axis=-1)
            ckv = layernorm(x @ W_dkv, kv_ln_g, kv_ln_b)
            KV = ckv @ W_ukv
            K, V = (KV[..., :D_MODEL], KV[..., D_MODEL:])
            K = K.reshape(b, s, N_HEADS, DH).transpose(0, 2, 1, 3)
            Kr = (x @ W_kr).reshape(b, s, N_HEADS, R).transpose(0, 2, 1, 3)
            Kr = apply_rope(Kr, cos, sin)
            k = jnp.concatenate([K, Kr], axis=-1)
            v = V.reshape(b, s, N_HEADS, DH).transpose(0, 2, 1, 3)
            scale = 1.0 / jnp.sqrt(jnp.asarray(DH + R, x.dtype))
            scores = jnp.einsum('bhqd,bhkd->bhqk', q, k) * scale
            mask = jnp.tril(jnp.ones((s, s), dtype=bool))
            scores = jnp.where(mask, scores, jnp.finfo(scores.dtype).min)
            attn = jax.nn.softmax(scores, axis=-1)
            out = jnp.einsum('bhqk,bhkd->bhqd', attn, v)
            out = out.transpose(0, 2, 1, 3).reshape(b, s, d)
            return (out @ W_o.T, ckv)
        return _reference_tuple_inner(x, W_dq, W_uq, W_qr, W_dkv, W_ukv, W_kr, W_o, q_ln_g, q_ln_b, kv_ln_g, kv_ln_b)[0]

    def _L1_ffn_ref(x, gate_w, gate_b, w1, b1, w2, b2):
        import jax, jax.numpy as jnp
        import numpy as np
        B, S, H, E, K = (8, 1024, 128, 8, 2)
        logits = jnp.einsum('bsh,he->bse', x, gate_w) + gate_b
        topk_vals, topk_idx = jax.lax.top_k(logits, K)
        topk_weights = jax.nn.softmax(topk_vals, axis=-1)
        mask = jax.nn.one_hot(topk_idx, E, dtype=topk_weights.dtype)
        weights = jnp.einsum('bske,bsk->bse', mask, topk_weights)
        h = jax.nn.relu(jnp.einsum('bsh,ehf->bsef', x, w1) + b1)
        expert_out = jnp.einsum('bsef,efh->bseh', h, w2) + b2
        return jnp.einsum('bseh,bse->bsh', expert_out, weights)

    def _L2_attn_ref(x, Wq, Wk, Wv, Wg, Wo, Wgk1, Wgk2, bgk2, rms_w):
        import jax, jax.numpy as jnp
        import numpy as np
        B, T, HID, H = (4, 512, 128, 4)
        DK, DV = (64, 128)
        GATE_LOW_RANK = 16
        GATE_LOGIT_NORM = 16.0
        RMS_EPS = 1e-05
        b, t, _ = x.shape
        q = (x @ Wq).reshape(b, t, H, DK) * DK ** (-0.5)
        k = (x @ Wk).reshape(b, t, H, DK)
        v = (x @ Wv).reshape(b, t, H, DV)
        gk = jax.nn.log_sigmoid(x @ Wgk1 @ Wgk2 + bgk2).reshape(b, t, H, DK) / GATE_LOGIT_NORM

        def step(S, inp):
            qt, kt, vt, gt = inp
            S = jnp.exp(gt)[..., None] * S + kt[..., None] * vt[..., None, :]
            ot = jnp.einsum('bhk,bhkv->bhv', qt, S)
            return (S, ot)
        S0 = jnp.zeros((b, H, DK, DV), x.dtype)
        xs = tuple((jnp.moveaxis(a, 1, 0) for a in (q, k, v, gk)))
        _, o = jax.lax.scan(step, S0, xs)
        o = jnp.moveaxis(o, 0, 1)
        o = o * jax.lax.rsqrt(jnp.mean(o * o, axis=-1, keepdims=True) + RMS_EPS) * rms_w
        g = (x @ Wg).reshape(b, t, H, DV)
        o = o * g * jax.nn.sigmoid(g)
        return o.reshape(b, t, H * DV) @ Wo

    def _L2_ffn_ref(x, pos_w, pos_b, qkv_w, qkv_b, wo_w, wo_b):
        import jax, jax.numpy as jnp
        import numpy as np
        from jax import lax
        N, M, DIM, HEADS, TOPK = (4, 512, 128, 8, 16)

        def _split_heads(t, h):
            n, m, c = t.shape
            return t.reshape(n, m, h, c // h).transpose(0, 2, 1, 3).reshape(n * h, m, c // h)
        n, m, c = x.shape
        h = HEADS
        scale = c ** (-0.5)
        pos = lax.conv_general_dilated(x.transpose(0, 2, 1), pos_w, window_strides=(1,), padding=[(1, 1)], feature_group_count=c, dimension_numbers=('NCH', 'OIH', 'NCH'))
        x = x + (pos + pos_b[None, :, None]).transpose(0, 2, 1)
        qkv = x @ qkv_w.T + qkv_b
        q, k, v = jnp.split(qkv, [c, 2 * c], axis=-1)
        q = _split_heads(q, h)
        k = _split_heads(k, h)
        v = _split_heads(v, h)
        qd = lax.stop_gradient(q)
        kd = lax.stop_gradient(k)
        logits = jnp.einsum('bmd,bpd->bmp', qd * scale, kd)
        _, idx = lax.top_k(logits, TOPK)
        gather = jax.vmap(lambda t, i: t[i])
        k_sel = gather(k, idx)
        v_sel = gather(v, idx)
        attn = jax.nn.softmax(jnp.einsum('bmd,bmkd->bmk', q * scale, k_sel), axis=-1)
        out = jnp.einsum('bmk,bmkd->bmd', attn, v_sel)
        d = c // h
        out = out.reshape(n, h, m, d).transpose(0, 2, 1, 3).reshape(n, m, c)
        return out @ wo_w.T + wo_b

    def _L3_attn_ref(x, w_qkv, lora_A_qkv, lora_B_qkv, w_out, b_out, lora_A_out, lora_B_out):
        import jax, jax.numpy as jnp
        import numpy as np
        B, N, C = (2, 512, 128)
        HEADS, WINDOW, R = (8, 64, 8)
        LORA_SCALE = 2.0 / R
        b, n, c = x.shape
        dh = c // HEADS
        scale = dh ** (-0.5)
        qkv = x @ w_qkv + x @ lora_A_qkv @ lora_B_qkv * LORA_SCALE
        qkv = qkv.reshape(b, n, 3, HEADS, dh)
        q = jnp.transpose(qkv[:, :, 0], (0, 2, 1, 3))
        k = jnp.transpose(qkv[:, :, 1], (0, 2, 1, 3))
        v = jnp.transpose(qkv[:, :, 2], (0, 2, 1, 3))
        scores = jnp.einsum('bhid,bhjd->bhij', q, k) * scale
        i = jnp.arange(n)[:, None]
        j = jnp.arange(n)[None, :]
        valid = (j <= i) & (jnp.abs(i - j) <= WINDOW)
        scores = jnp.where(valid[None, None], scores, -jnp.inf)
        attn = jax.nn.softmax(scores, axis=-1)
        out_local = jnp.einsum('bhij,bhjd->bhid', attn, v)
        kg = k[:, :, ::WINDOW, :]
        vg = v[:, :, ::WINDOW, :]
        sg = jnp.einsum('bhid,bhjd->bhij', q, kg) * scale
        ag = jax.nn.softmax(sg, axis=-1)
        out_global = jnp.einsum('bhij,bhjd->bhid', ag, vg)
        out = (out_local + out_global).transpose(0, 2, 1, 3).reshape(b, n, c)
        return out @ w_out + b_out + out @ lora_A_out @ lora_B_out * LORA_SCALE

    def _L3_ffn_ref(x, attn_norm_w, wq, wk, wv, wo, ffn_norm_w, router_w, w1, w2):
        import jax, jax.numpy as jnp
        import numpy as np
        from functools import partial
        EPS = 1e-05
        ROPE_THETA = 10000.0
        TOP_K = 2

        def rmsnorm(x, w):
            var = jnp.mean(x * x, axis=-1, keepdims=True)
            return x * jax.lax.rsqrt(var + EPS) * w

        def apply_rope(x):
            B, S, H, dh = x.shape
            inv_freq = 1.0 / ROPE_THETA ** (jnp.arange(0, dh, 2, dtype=jnp.float32) / dh)
            ang = jnp.arange(S, dtype=jnp.float32)[:, None] * inv_freq[None, :]
            cos = jnp.cos(ang)[None, :, None, :]
            sin = jnp.sin(ang)[None, :, None, :]
            x1 = x[..., 0::2]
            x2 = x[..., 1::2]
            r1 = x1 * cos - x2 * sin
            r2 = x1 * sin + x2 * cos
            return jnp.stack([r1, r2], axis=-1).reshape(x.shape)

        def mha_rope(xn, wq, wk, wv, wo, num_heads):
            B, S, D = xn.shape
            dh = D // num_heads
            q = (xn @ wq).reshape(B, S, num_heads, dh)
            k = (xn @ wk).reshape(B, S, num_heads, dh)
            v = (xn @ wv).reshape(B, S, num_heads, dh)
            q = apply_rope(q)
            k = apply_rope(k)
            scores = jnp.einsum('bqhd,bkhd->bhqk', q, k) / jnp.sqrt(jnp.float32(dh))
            causal = jnp.tril(jnp.ones((S, S), dtype=bool))
            scores = jnp.where(causal[None, None], scores, jnp.float32(-1000000000.0))
            attn = jax.nn.softmax(scores, axis=-1)
            out = jnp.einsum('bhqk,bkhd->bqhd', attn, v).reshape(B, S, D)
            return out @ wo

        def moe_ffn(hn, router_w, w1, w2):
            B, S, D = hn.shape
            E = router_w.shape[1]
            t = hn.reshape(B * S, D)
            T = t.shape[0]
            logits = t @ router_w
            probs = jax.nn.softmax(logits, axis=-1)
            vals, idx = jax.lax.top_k(probs, TOP_K)
            gates = vals / jnp.sum(vals, axis=-1, keepdims=True)
            gates_dense = jnp.zeros((T, E), dtype=t.dtype).at[jnp.arange(T)[:, None], idx].add(gates)
            out = jnp.zeros_like(t)
            for e in range(E):
                ge = gates_dense[:, e:e + 1]
                h = jax.nn.gelu(t @ w1[e], approximate=False)
                out = out + ge * (h @ w2[e])
            return out.reshape(B, S, D)
        num_heads = 8
        h = x + mha_rope(rmsnorm(x, attn_norm_w), wq, wk, wv, wo, num_heads)
        out = h + moe_ffn(rmsnorm(h, ffn_norm_w), router_w, w1, w2)
        return out
    h = _L0_tok_ref(x, L0_tok_W, L0_tok_b)
    h = h + _L0_attn_ref(_layernorm(h, axis=-1), L0_attn_mask, L0_attn_padding_mask, L0_attn_wq, L0_attn_bq, L0_attn_wk, L0_attn_bk, L0_attn_wv, L0_attn_bv, L0_attn_wg, L0_attn_bg, L0_attn_wo, L0_attn_bo, L0_attn_fc1_w, L0_attn_fc1_b, L0_attn_fc2_w, L0_attn_fc2_b, L0_attn_ln_ffn_g, L0_attn_ln_ffn_b, L0_attn_n0_g, L0_attn_n0_b, L0_attn_n1_g, L0_attn_n1_b)
    h = h + _L0_ffn_ref(_layernorm(h, axis=-1), L0_ffn_router_w, L0_ffn_router_b, L0_ffn_gate_up_proj, L0_ffn_gate_up_proj_bias, L0_ffn_down_proj, L0_ffn_down_proj_bias)
    h = h + _L1_attn_ref(_layernorm(h, axis=-1), L1_attn_W_dq, L1_attn_W_uq, L1_attn_W_qr, L1_attn_W_dkv, L1_attn_W_ukv, L1_attn_W_kr, L1_attn_W_o, L1_attn_q_ln_g, L1_attn_q_ln_b, L1_attn_kv_ln_g, L1_attn_kv_ln_b)
    h = h + _L1_ffn_ref(_layernorm(h, axis=-1), L1_ffn_gate_w, L1_ffn_gate_b, L1_ffn_w1, L1_ffn_b1, L1_ffn_w2, L1_ffn_b2)
    h = h + _L2_attn_ref(_layernorm(h, axis=-1), L2_attn_Wq, L2_attn_Wk, L2_attn_Wv, L2_attn_Wg, L2_attn_Wo, L2_attn_Wgk1, L2_attn_Wgk2, L2_attn_bgk2, L2_attn_rms_w)
    h = h + _L2_ffn_ref(_layernorm(h, axis=-1), L2_ffn_pos_w, L2_ffn_pos_b, L2_ffn_qkv_w, L2_ffn_qkv_b, L2_ffn_wo_w, L2_ffn_wo_b)
    h = h + _L3_attn_ref(_layernorm(h, axis=-1), L3_attn_w_qkv, L3_attn_lora_A_qkv, L3_attn_lora_B_qkv, L3_attn_w_out, L3_attn_b_out, L3_attn_lora_A_out, L3_attn_lora_B_out)
    h = h + _L3_ffn_ref(_layernorm(h, axis=-1), L3_ffn_attn_norm_w, L3_ffn_wq, L3_ffn_wk, L3_ffn_wv, L3_ffn_wo, L3_ffn_ffn_norm_w, L3_ffn_router_w, L3_ffn_w1, L3_ffn_w2)
    return h

_drawn_inputs = setup_inputs


def setup_inputs(seed=0):
    import zlib

    import numpy as np

    out = dict(_drawn_inputs(seed))
    spreads = {'L0_tok_b': (0.0, 0.462),
     'L0_attn_ln_ffn_g': (1.0, 0.6),
     'L0_attn_ln_ffn_b': (0.0, 0.8),
     'L0_attn_n0_g': (1.0, 0.6),
     'L0_attn_n0_b': (0.0, 0.8),
     'L0_attn_n1_g': (1.0, 0.6),
     'L0_attn_n1_b': (0.0, 0.8),
     'L0_ffn_router_b': (0.0, 0.787),
     'L0_ffn_gate_up_proj_bias': (0.0, 0.8),
     'L0_ffn_down_proj_bias': (0.0, 0.8),
     'L1_attn_q_ln_g': (1.0, 0.6),
     'L1_attn_q_ln_b': (0.0, 0.8),
     'L1_attn_kv_ln_g': (1.0, 0.6),
     'L1_attn_kv_ln_b': (0.0, 0.8),
     'L2_attn_bgk2': (0.0, 0.8),
     'L2_attn_rms_w': (1.0, 0.6),
     'L3_attn_b_out': (0.0, 0.8),
     'L3_ffn_attn_norm_w': (1.0, 0.6),
     'L3_ffn_ffn_norm_w': (1.0, 0.6)}
    factors = {'L0_attn_wq': 8.0,
     'L0_attn_bq': 8.0,
     'L0_attn_wk': 8.0,
     'L0_attn_bk': 8.0,
     'L0_attn_wv': 8.0,
     'L0_attn_bv': 8.0,
     'L0_attn_wg': 8.0,
     'L0_attn_bg': 8.0,
     'L0_attn_wo': 8.0,
     'L0_attn_bo': 8.0,
     'L0_attn_fc1_b': 8.0,
     'L0_attn_fc2_b': 8.0,
     'L1_attn_W_dq': 8.0,
     'L1_attn_W_uq': 8.0,
     'L1_attn_W_qr': 8.0,
     'L1_attn_W_dkv': 8.0,
     'L1_attn_W_ukv': 8.0,
     'L1_attn_W_kr': 8.0,
     'L1_attn_W_o': 8.0,
     'L1_ffn_gate_w': 4.979,
     'L1_ffn_gate_b': 8.0,
     'L1_ffn_w1': 5.346,
     'L1_ffn_b1': 8.0,
     'L1_ffn_w2': 4.451,
     'L1_ffn_b2': 8.0,
     'L2_attn_Wq': 8.0,
     'L2_attn_Wk': 8.0,
     'L2_attn_Wv': 8.0,
     'L2_attn_Wg': 8.0,
     'L2_attn_Wo': 8.0,
     'L2_attn_Wgk1': 8.0,
     'L2_attn_Wgk2': 8.0,
     'L2_ffn_pos_w': 8.0,
     'L2_ffn_pos_b': 8.0,
     'L2_ffn_qkv_w': 8.0,
     'L2_ffn_qkv_b': 8.0,
     'L2_ffn_wo_w': 8.0,
     'L2_ffn_wo_b': 8.0,
     'L3_attn_w_qkv': 8.0,
     'L3_attn_lora_A_qkv': 21.406,
     'L3_attn_lora_B_qkv': 8.0,
     'L3_attn_w_out': 8.0,
     'L3_attn_lora_A_out': 23.902,
     'L3_attn_lora_B_out': 8.0,
     'L3_ffn_wq': 8.0,
     'L3_ffn_wk': 8.0,
     'L3_ffn_wv': 8.0,
     'L3_ffn_wo': 8.0,
     'L3_ffn_router_w': 8.0,
     'L3_ffn_w1': 8.0,
     'L3_ffn_w2': 8.0}
    for name, (base, spread) in spreads.items():
        noise = np.random.default_rng([zlib.crc32(name.encode()), seed]).standard_normal(out[name].shape)
        drawn = base * np.exp(spread * noise) if base else spread * noise
        out[name] = jnp.asarray(drawn.astype(out[name].dtype))
    for name, factor in factors.items():
        out[name] = (out[name] * factor).astype(out[name].dtype)
    return out
```

```python
from contextlib import ExitStack

import concourse.bass as bass
from concourse import mybir

ALU = mybir.AluOpType
ACT = mybir.ActivationFunctionType
AX = mybir.AxisListType
F32 = mybir.dt.float32
I32 = mybir.dt.int32

P = 128
D = 128
HEADS = 8
DH = D // HEADS
TOK = 63
SEQ = 64
GT = 4
GTOK = GT * P
SLOTS = 2
EXPERTS = 8
NEG = -3.0e38
PICKED = -3.3e38
FFN = 4 * D
QP, KVP = 64, 85
GH, GK, GV, GR = 4, 64, 128, 16

LAYOUT = {
    "const": [("ident", P), ("ones", P), ("dm", HEADS * SEQ), ("causal", SEQ), ("keys", SEQ), ("upper", SEQ),
              ("restart", GTOK), ("mla_cos", SEQ), ("mla_sin", SEQ), ("rope_cos", SEQ), ("rope_sin", SEQ)],
    "L0A": [("qk", 4 * D), ("v", D), ("g", D), ("wo", D), ("fc1", FFN), ("fc2", 4 * 129), ("qkb", 4), ("bv", 64),
            ("bg", D), ("bo", D), ("n0g", D), ("n0b", D), ("n1g", D), ("n1b", D), ("fc1b", 4), ("fc2b", D),
            ("fg", 4), ("fb", 4)],
    "L1A": [("down", QP + KVP), ("qa", 2 * D), ("qb", 2 * D), ("kn", 2 * D), ("ka", 2 * D), ("kb", 2 * D), ("v", D),
            ("wo", D), ("qg", 1), ("qbias", 1), ("kg", 1), ("kbias", 1)],
    "L2A": [("qk", 4 * D), ("gk1", GR), ("gk2", 2 * D), ("gkb", 2), ("v", GH * GV), ("g", GH * GV), ("wo", GH * D),
            ("rms", 1)],
    "L2F": [("qk", 4 * D), ("v", D), ("wo", D), ("conv", 3), ("convb", 1), ("qkb", 4), ("bv", 1), ("bo", D)],
    "L3A": [("qk", 4 * D), ("v", D), ("wo", D), ("la", D), ("lbqk", 4 * D), ("lbv", D), ("loa", D), ("lob", D),
            ("bo", D)],
    "L3F": [("qk", 4 * D), ("qkr", 4 * D), ("v", D), ("wo", D), ("nw", 1)],
}
LINKS = {"L0A": 90, "L1A": 33, "L2A": 31, "L2F": 25, "L3A": 18, "L3F": 37}
ATTN_STAGES = ("L0A", "L1A", "L2A", "L2F", "L3A", "L3F")


def columns(stage):
    at, out = 0, {}
    for name, n in LAYOUT[stage]:
        out[name] = (at, n)
        at += n
    return out, at


class Net:
    pass


class Link:

    def __init__(self, eng, sem, base, per_group):
        self.eng, self.sem, self.base, self.per_group = eng, sem, base, per_group

    def group(self, t):
        self.first, self.k = self.base + t * self.per_group, 0

    def __call__(self, ins, own=None):
        self.k += 1
        ins.then_inc(self.sem, 1)
        self.eng.wait_ge(self.sem, self.first + self.k)
        if own is not None:
            self.eng.sem_inc(own, 1)

    def end(self):
        assert self.k == self.per_group, ("links in a group:", self.k)


def slot_links(eng, sems, base, per_group):
    return [Link(eng, sems[s], base, per_group) for s in range(SLOTS)]


def pairs(eng, groups, body):
    with eng.Fori(0, groups // SLOTS) as i:
        running = [body(i * SLOTS + s, s, i) for s in range(SLOTS)]
        while running:
            running = [r for r in running if next(r, "ended") != "ended"]



RSQRT_LINKS = 12


def rsqrt_dve(g, v, link, s, width, src, eps, scale=1.0):
    a, y, q = g.ra[s][:, 0:width], g.rs[s][:, 0:width], g.rq[s][:, 0:width]
    link(v.tensor_scalar(a, src, scale, eps, ALU.mult, ALU.add))
    link(v.tensor_scalar(y.bitcast(I32), a.bitcast(I32), 1, None, ALU.arith_shift_right))
    link(v.tensor_scalar(y.bitcast(I32), y.bitcast(I32), -1.0, float(0x5F3759DF), ALU.mult, ALU.add))
    for _ in range(3):
        link(v.tensor_tensor(q, y, y, ALU.mult))
        link(v.scalar_tensor_tensor(q, q, -0.5, a, ALU.mult, ALU.mult))
        link(v.scalar_tensor_tensor(y, q, 1.5, y, ALU.add, ALU.mult))


NORM_LINKS = RSQRT_LINKS + 2


def norm_dve(g, v, link, s, parts, eps):
    for i, part in enumerate(parts):
        ins = v.bn_stats(g.stats[s][:, i, :], part)
    link(ins, g.wait_carrier)
    for i in range(len(parts)):
        ins = v.bn_aggr(g.mv[s][:, i, :], g.stats[s][:, i, :])
    link(ins)
    rsqrt_dve(g, v, link, s, len(parts), g.mv[s][:, 0:len(parts), 1], eps)


def normalise_dve(g, v, s, parts, outs):
    for i, (part, out) in enumerate(zip(parts, outs)):
        ins = v.tensor_scalar(out, part, g.mv[s][:, i, 0:1], g.rs[s][:, i:i + 1], ALU.subtract, ALU.mult)
    return ins


FRONT_LINKS = NORM_LINKS


def front_dve(g, v, link, s, t, n):
    v.wait_ge(g.const_loaded, 16)
    v.wait_ge(g.slot_free, n)
    norm_dve(g, v, link, s, [g.h[:, bass.ds(t * GT + i, 1), :] for i in range(GT)], 1e-5)
    for i in range(GT):
        ins = v.tensor_scalar(g.xn[s][:, i:i + 1, :], g.h[:, bass.ds(t * GT + i, 1), :],
                              g.mv[s][:, i, 0:1], g.rs[s][:, i:i + 1], ALU.subtract, ALU.mult)
    ins.then_inc(g.xn_ready, 1)



def front_pe(g, pe, s, n):
    pe.wait_ge(g.const_loaded, 16)
    pe.wait_ge(g.xn_ready, n)
    for i in range(GT):
        ins = pe.transpose(g.ps[s][:, 0, i * P:(i + 1) * P], g.xn[s][:, i, :], g.c("ident"))
    ins.then_inc(g.xn_transposed, 1)


def front_act(g, a, s, n):
    a.wait_ge(g.xn_transposed, n)
    a.activation(g.xT[s][:, :], g.ps[s][:, 0, :], ACT.Copy).then_inc(g.xT_ready, 1)


def project_qk_pe(g, pe, s, w, first=0, count=4):
    for i in range(first, first + count):
        ins = pe.matmul(g.ps[s][:, i, :], w[:, i * D:(i + 1) * D], g.xT[s][:, :], start=True, stop=True)
    return ins


def values_pe(g, pe, s, w, xT, k=P):
    for q in range(2 * GT):
        for par in range(2):
            ins = pe.matmul(g.ps[s][64 * par:64 * par + 64, 0, q * 64:(q + 1) * 64], xT[0:k, q * SEQ:(q + 1) * SEQ],
                            w[0:k, par * 64:(par + 1) * 64], start=True, stop=True)
    return ins


def scores_pe(g, pe, s):
    for hh in range(2):
        for sq in range(2):
            for tile in range(GT):
                for r in range(4):
                    rows, cols = slice(32 * r, 32 * r + 32), slice(tile * P + sq * SEQ, tile * P + sq * SEQ + SEQ)
                    at = tile * P + hh * SEQ
                    ins = pe.matmul(g.ps[s][64 * sq:64 * sq + 64, r, at:at + SEQ],
                                    g.qk[s][rows, hh, cols], g.qk[s][rows, 2 + hh, cols], start=True, stop=True)
    return ins


def turn_probs_pe(g, pe, s):
    for r in range(4):
        for tile in range(GT):
            c = r * 512 + tile * P
            ins = pe.transpose(g.ps[s][:, r, tile * P:(tile + 1) * P], g.pr[s][:, c:c + P], g.c("ident"))
    return ins


def weigh_values_pe(g, pe, s):
    for sq in range(2):
        for r in range(4):
            for tile in range(GT):
                for par in range(2):
                    c, p = (tile * 4 + r) * (DH + 1), r * 512 + tile * P + sq * SEQ
                    keys = slice(64 * par, 64 * par + TOK)
                    ins = pe.matmul(g.ps[s][64 * sq:64 * sq + 64, par, c:c + DH + 1], g.pt[s][keys, p:p + SEQ],
                                    g.v2[s][keys, 2 * tile + sq, r, :], start=True, stop=True)
    return ins


def turn_out_pe(g, pe, s, src):
    for i in range(GT):
        ins = pe.transpose(g.ps[s][:, 2, i * P:(i + 1) * P], src(i), g.c("ident"))
    return ins


def o_tile(g, s):
    return lambda i: g.o[s][:, i, :]


def project_out_pe(g, pe, s, w):
    for i in range(GT):
        ins = pe.matmul(g.ps[s][:, 3, i * P:(i + 1) * P], g.oT[s][:, i * P:(i + 1) * P], w, start=True, stop=True)
    return ins


def attend_pe(g, pe, s, k, ready, wo):
    for sem, n in ready:
        pe.wait_ge(sem, n)
    scores_pe(g, pe, s).then_inc(g.scores_done, 1)
    yield
    pe.wait_ge(g.probs_ready, k)
    turn_probs_pe(g, pe, s).then_inc(g.probs_turned, 1)
    yield
    pe.wait_ge(g.const_loaded, 16)
    pe.wait_ge(g.pt_ready_a, k)
    pe.wait_ge(g.pt_ready_v, k)
    weigh_values_pe(g, pe, s).then_inc(g.values_weighed, 1)
    yield
    pe.wait_ge(g.o_ready, k)
    turn_out_pe(g, pe, s, o_tile(g, s)).then_inc(g.o_turned, 1)
    yield
    pe.wait_ge(g.oT_ready, k)
    project_out_pe(g, pe, s, wo).then_inc(g.out_done, 1)


def turned_probs_act(g, a, s, k):
    a.wait_ge(g.probs_turned, k)
    a.activation(g.pt[s][:, 0:1024], g.psf[s][:, 0:1024], ACT.Copy).then_inc(g.pt_ready_a, 1)


def turned_probs_dve(g, v, s, k):
    v.wait_ge(g.probs_turned, k)
    v.tensor_copy(g.pt[s][:, 1024:2048], g.psf[s][:, 1024:2048]).then_inc(g.pt_ready_v, 1)


def softmax_dve(g, v, link, s, k, scale, mask):
    v.wait_ge(g.scores_done, k)
    rows = g.pr[s].rearrange("p (r j) -> p r j", j=SEQ)
    link(v.scalar_tensor_tensor(rows, g.psf[s].rearrange("p (r j) -> p r j", j=SEQ), scale,
                                mask.unsqueeze(1).to_broadcast([P, 32, SEQ]), ALU.mult, ALU.add))
    link(v.tensor_reduce(g.rm[s][:, 0:32], rows, AX.X, ALU.max))
    v.tensor_tensor(rows, rows, g.rm[s][:, 0:32].unsqueeze(2).to_broadcast([P, 32, SEQ]),
                    ALU.subtract).then_inc(g.centred_ready, 1)


SOFTMAX_LINKS = 2


def scale_heads_dve(g, v, s):
    for a in range(2):
        ins = v.tensor_tensor(
            g.o[s][:, :, 64 * a:64 * a + 64].rearrange("p t (r e) -> p t r e", e=DH),
            g.ps[s][:, a, 0:16 * (DH + 1)].rearrange("p (t r e) -> p t r e", t=GT, e=DH + 1)[:, :, :, 0:DH],
            g.rm[s][:, 16 * a:16 * a + 16].rearrange("p (t r) -> p t r", t=GT).unsqueeze(3).to_broadcast([P, GT, 4, DH]),
            ALU.mult)
    return ins


def divide_dve(g, v, link, s, k):
    v.wait_ge(g.values_weighed, k)
    link(v.reciprocal(g.rm[s][:, 0:32].rearrange("p (a b) -> p a b", a=2), g.heads(s)[:, :, :, DH]))
    scale_heads_dve(g, v, s).then_inc(g.o_ready, 1)


DIVIDE_LINKS = 1


def add_out_dve(g, v, s, t, k, bias=None, link=None):
    v.wait_ge(g.out_done, k)
    out = g.ps[s][:, 3, :].rearrange("p (t d) -> p t d", d=D)
    if bias is not None:
        link(v.tensor_tensor(g.t2[s][:, :, :], out, bias.unsqueeze(1).to_broadcast([P, GT, D]), ALU.add))
        out = g.t2[s][:, :, :]
    h = g.h[:, bass.ds(t * GT, GT), :]
    v.tensor_tensor(h, out, h, ALU.add).then_inc(g.slot_free, 1)



def l0a_fold_dve(g, v):
    v.wait_ge(g.attn_loaded[0], 16)
    v.wait_ge(g.slot_free, g.n0["L0A"] + SLOTS)
    fc2 = g.w("L0A", "fc2").rearrange("p (k d) -> p k d", d=129)
    for k in range(4):
        ins = v.tensor_scalar(g.pr[0][:, k * P:(k + 1) * P], g.c("ones"), g.w("L0A", "fb")[:, k:k + 1], None, ALU.mult)
    ins.then_inc(g.fold_dve, 1)
    v.wait_ge(g.fold_pe, 1)
    b = g.w("L0A", "fc2b")
    v.tensor_tensor(b, b, g.ps[0][:, 0, 0:D], ALU.add).then_inc(g.fold_dve, 1)
    for k in range(4):
        ins = v.tensor_scalar(fc2[:, k, 0:D], fc2[:, k, 0:D], g.w("L0A", "fg")[:, k:k + 1], None, ALU.mult)
    ins.then_inc(g.fold_dve, 1)
    v.wait_ge(g.fold_pe, 2)
    v.tensor_copy(g.cs[:, :], g.ps[0][:, 1, 0:D]).then_inc(g.fold_dve, 1)
    v.wait_ge(g.fold_dve, 4)


def l0a_fold_pe(g, pe):
    fc2 = g.w("L0A", "fc2").rearrange("p (k d) -> p k d", d=129)
    pe.wait_ge(g.fold_dve, 1)
    for k in range(4):
        ins = pe.matmul(g.ps[0][:, 0, 0:D], g.pr[0][:, k * P:(k + 1) * P], fc2[:, k, 0:D], start=(k == 0), stop=(k == 3))
    ins.then_inc(g.fold_pe, 1)
    pe.wait_ge(g.fold_dve, 3)
    for k in range(4):
        ins = pe.matmul(g.ps[0][:, 1, 0:D], g.c("ones"), fc2[:, k, 0:D], start=(k == 0), stop=(k == 3))
    ins.then_inc(g.fold_pe, 1)
    pe.wait_ge(g.fold_dve, 4)


def l0a_pe(g, pe):
    w = lambda name: g.w("L0A", name)
    fc2 = w("fc2").rearrange("p (k d) -> p k d", d=129)
    l0a_fold_pe(g, pe)

    def group(t, s, i):
        n = g.n0["L0A"] + t + 1
        k = t + 1
        front_pe(g, pe, s, n)
        yield
        pe.wait_ge(g.xT_ready, n)
        project_qk_pe(g, pe, s, w("qk")).then_inc(g.r_qk_done, 1)
        yield
        pe.wait_ge(g.r_q_ready, k)
        values_pe(g, pe, s, w("v"), g.xT[s]).then_inc(g.r_v_done, 1)
        for i in range(GT):
            ins = pe.matmul(g.ps[s][:, 1, i * P:(i + 1) * P], g.xT[s][:, i * P:(i + 1) * P], w("g"), start=True, stop=True)
        ins.then_inc(g.r_g_done, 1)
        yield
        pe.wait_ge(g.r_g_ready, k)
        pe.wait_ge(g.r_k_ready, k)
        scores_pe(g, pe, s).then_inc(g.scores_done, 1)
        yield
        pe.wait_ge(g.probs_ready, k)
        turn_probs_pe(g, pe, s).then_inc(g.probs_turned, 1)
        yield
        pe.wait_ge(g.const_loaded, 16)
        pe.wait_ge(g.pt_ready_a, k)
        pe.wait_ge(g.pt_ready_v, k)
        weigh_values_pe(g, pe, s).then_inc(g.values_weighed, 1)
        yield
        pe.wait_ge(g.o_ready, k)
        turn_out_pe(g, pe, s, o_tile(g, s)).then_inc(g.o_turned, 1)
        yield
        pe.wait_ge(g.oT_ready, k)
        project_out_pe(g, pe, s, w("wo")).then_inc(g.out_done, 1)
        yield
        pe.wait_ge(g.r_x1_ready, k)
        turn_out_pe(g, pe, s, lambda i: g.o[s][:, i, :]).then_inc(g.r_x1_turned, 1)
        yield
        pe.wait_ge(g.r_x1T_ready, k)
        for i in range(4):
            ins = pe.matmul(g.ps[s][:, i, :], w("fc1")[:, i * D:(i + 1) * D], g.xT[s][:, :], start=True, stop=True)
        ins.then_inc(g.r_fc1_done, 1)
        yield
        pe.wait_ge(g.r_z_ready, k)
        for i in range(GT):
            cols = slice(i * P, (i + 1) * P)
            for c in range(4):
                pe.matmul(g.psf[s][:, 256 * i:256 * i + 129], g.pr[s][:, c * 512 + i * P:c * 512 + (i + 1) * P],
                          fc2[:, c, :], start=(c == 0), stop=(c == 3))
            for c in range(4):
                ins = pe.matmul(g.psf[s][:, 256 * i + 129:256 * i + 130], g.pt[s][:, c * 512 + i * P:c * 512 + (i + 1) * P],
                                g.c("ones")[:, 0:1], start=(c == 0), stop=(c == 3))
        ins.then_inc(g.r_fc2_done, 1)

    pairs(pe, g.groups, group)


def l0a_act(g, a):
    w = lambda name: g.w("L0A", name)

    def group(t, s, i):
        n = g.n0["L0A"] + t + 1
        k = t + 1
        front_act(g, a, s, n)
        yield
        a.wait_ge(g.r_qk_done, k)
        for i in range(2):
            ins = a.activation(g.qk[s][:, i, :], g.ps[s][:, i, :], ACT.Identity, bias=w("qkb")[:, i:i + 1])
        ins.then_inc(g.r_q_ready, 1)
        yield
        a.wait_ge(g.r_g_ready, k)
        a.activation(g.t2[s][:, :, :], g.t2[s][:, :, :], ACT.Silu).then_inc(g.r_silu_ready, 1)
        yield
        a.wait_ge(g.probs_turned, k)
        a.activation(g.pt[s][:, 0:1024], g.psf[s][:, 0:1024], ACT.Copy).then_inc(g.pt_ready_a, 1)
        yield
        a.wait_ge(g.o_turned, k)
        a.activation(g.oT[s][:, :], g.ps[s][:, 2, :], ACT.Copy).then_inc(g.oT_ready, 1)
        yield
        a.wait_ge(g.r_x1_turned, k)
        a.activation(g.xT[s][:, :], g.ps[s][:, 2, :], ACT.Copy).then_inc(g.r_x1T_ready, 1)
        yield
        a.wait_ge(g.r_fc1_done, k)
        for i in range(4):
            ins = a.activation(g.pr[s][:, i * 512:(i + 1) * 512], g.ps[s][:, i, :], ACT.Gelu, bias=w("fc1b")[:, i:i + 1])
        ins.then_inc(g.r_gelu_ready, 1)
        yield
        a.wait_ge(g.r_gelu_ready, k)
        a.activation(g.pt[s][:, :], g.pr[s][:, :], ACT.Square).then_inc(g.r_z_ready, 1)

    pairs(a, g.groups, group)


def l0a_dve(g, v):
    w = lambda name: g.w("L0A", name)
    l0a_fold_dve(g, v)
    links = slot_links(v, g.slot_link, g.link0["L0A"], LINKS["L0A"])

    def group(t, s, i):
        n = g.n0["L0A"] + t + 1
        k = t + 1
        link = links[s]
        link.group(i)
        row = lambda name: w(name).unsqueeze(1).to_broadcast([P, GT, D])
        o, xn, t2 = g.o[s][:, :, :], g.xn[s][:, :, :], g.t2[s][:, :, :]
        front_dve(g, v, link, s, t, n)
        yield
        v.wait_ge(g.r_qk_done, k)
        for i in range(2, 4):
            ins = v.tensor_scalar(g.qk[s][:, i, :], g.ps[s][:, i, :], w("qkb")[:, i:i + 1], DH ** -0.5, ALU.add, ALU.mult)
        ins.then_inc(g.r_k_ready, 1)
        yield
        v.wait_ge(g.r_v_done, k)
        link(v.tensor_tensor(g.v2[s][:, :, :, 0:DH], g.ps[s][:, 0, :].rearrange("p (q h e) -> p q h e", q=8, e=DH),
                             w("bv").rearrange("p (h e) -> p h e", e=DH).unsqueeze(1).to_broadcast([P, 8, 4, DH]), ALU.add))
        yield
        v.wait_ge(g.r_g_done, k)
        v.tensor_tensor(t2, g.ps[s][:, 1, :].rearrange("p (t d) -> p t d", d=D), row("bg"), ALU.add).then_inc(g.r_g_ready, 1)
        yield
        v.wait_ge(g.scores_done, k)
        split = lambda ap: ap.rearrange("p (r t c) -> p r t c", r=4, t=GT)
        v.tensor_tensor(split(g.pr[s][:, :]), split(g.psf[s]),
                        g.c("dm").rearrange("p (r c) -> p r c", r=4).unsqueeze(2).to_broadcast([P, 4, GT, 2 * SEQ]),
                        ALU.add).then_inc(g.probs_ready, 1)
        yield
        v.wait_ge(g.probs_turned, k)
        v.tensor_copy(g.pt[s][:, 1024:2048], g.psf[s][:, 1024:2048]).then_inc(g.pt_ready_v, 1)
        yield
        v.wait_ge(g.values_weighed, k)
        den = g.rm[s][:, 0:32]
        den4, sums = den.rearrange("p (a b) -> p a b", a=2), g.heads(s)[:, :, :, DH]
        link(v.tensor_scalar(den4, sums, 1.0, None, ALU.max))
        link(v.scalar_tensor_tensor(den4, sums, -1.0, den4, ALU.mult, ALU.max))
        link(v.reciprocal(den, den))
        oh = g.of[s].rearrange("p (r e) -> p r e", e=DH)
        per_head = lambda ap: ap.unsqueeze(2).to_broadcast([P, 32, DH])
        link(scale_heads_dve(g, v, s))
        link(v.tensor_reduce(g.rm[s][:, 0:32], oh, AX.X, ALU.add))
        link(v.scalar_tensor_tensor(oh, per_head(g.rm[s][:, 0:32]), -1.0 / DH, oh, ALU.mult, ALU.add))
        sq = g.pr[s][:, 0:512].rearrange("p (r e) -> p r e", e=DH)
        link(v.tensor_tensor(sq, oh, oh, ALU.mult))
        link(v.tensor_reduce(g.rm[s][:, 0:32], sq, AX.X, ALU.add))
        rsqrt_dve(g, v, link, s, 32, g.rm[s][:, 0:32], 1e-6, 1.0 / DH)
        link(v.tensor_tensor(oh, oh, per_head(g.rs[s][:, 0:32]), ALU.mult))
        yield
        v.wait_ge(g.r_silu_ready, k)
        v.tensor_tensor(o, o, t2, ALU.mult).then_inc(g.o_ready, 1)
        yield
        v.wait_ge(g.out_done, k)
        link(v.tensor_tensor(t2, g.ps[s][:, 3, :].rearrange("p (t d) -> p t d", d=D), row("bo"), ALU.add))
        link(v.tensor_tensor(xn, xn, t2, ALU.add))
        norm_dve(g, v, link, s, [g.xn[s][:, i, :] for i in range(GT)], 1e-5)
        link(normalise_dve(g, v, s, [g.xn[s][:, i, :] for i in range(GT)], [g.xn[s][:, i, :] for i in range(GT)]))
        link(v.tensor_tensor(xn, xn, row("n0g"), ALU.mult))
        v.tensor_tensor(o, xn, row("n0b"), ALU.add).then_inc(g.r_x1_ready, 1)
        yield
        v.wait_ge(g.r_fc2_done, k)
        z = g.psf[s][:, 0:1024].rearrange("p (t c) -> p t c", c=256)
        mean, sq4 = g.rm[s][:, 0:4], g.rm[s][:, 4:8]
        link(v.tensor_scalar(g.rm[s][:, 0:8].rearrange("p (a t) -> p t a", a=2), z[:, :, 128:130], 1.0 / FFN, None, ALU.mult))
        link(v.tensor_tensor(g.rm[s][:, 8:12], mean, mean, ALU.mult))
        link(v.tensor_tensor(sq4, sq4, g.rm[s][:, 8:12], ALU.subtract))
        rsqrt_dve(g, v, link, s, 4, sq4, 1e-6)
        link(v.scalar_tensor_tensor(mean, mean, -1.0, g.rs[s][:, 0:4], ALU.mult, ALU.mult))
        for i in range(GT):
            ins = v.scalar_tensor_tensor(g.t2[s][:, i, :], g.cs[:, :], mean[:, i:i + 1], w("fc2b"), ALU.mult, ALU.add)
        link(ins)
        for i in range(GT):
            ins = v.scalar_tensor_tensor(g.t2[s][:, i, :], z[:, i, 0:D], g.rs[s][:, i:i + 1], g.t2[s][:, i, :], ALU.mult, ALU.add)
        link(ins)
        link(v.tensor_tensor(t2, t2, o, ALU.add))
        norm_dve(g, v, link, s, [g.t2[s][:, i, :] for i in range(GT)], 1e-5)
        link(normalise_dve(g, v, s, [g.t2[s][:, i, :] for i in range(GT)], [g.t2[s][:, i, :] for i in range(GT)]))
        link(v.tensor_tensor(t2, t2, row("n1g"), ALU.mult))
        link(v.tensor_tensor(t2, t2, row("n1b"), ALU.add))
        h = g.h[:, bass.ds(t * GT, GT), :]
        v.tensor_tensor(h, t2, h, ALU.add).then_inc(g.slot_free, 1)
        link.end()

    pairs(v, g.groups, group)



def values_act(g, a, s):
    return a.activation(g.v2[s][:, :, :, 0:DH], g.ps[s][:, 0, :].rearrange("p (q h e) -> p q h e", q=2 * GT, e=DH), ACT.Copy)


def attend_act(g, a, s, k, bias=None, turn_out=True, masked_after=None):
    a.wait_ge(g.centred_ready, k - g.uncentred)
    a.activation(g.pr[s][:, :], g.pr[s][:, :], ACT.Exp).then_inc(masked_after if masked_after is not None else g.probs_ready, 1)
    yield
    turned_probs_act(g, a, s, k)
    if turn_out:
        yield
        a.wait_ge(g.o_turned, k)
        if bias is None:
            ins = a.activation(g.oT[s][:, :], g.ps[s][:, 2, :], ACT.Copy)
        else:
            ins = a.activation(g.oT[s][:, :], g.ps[s][:, 2, :], ACT.Identity, bias=bias)
        ins.then_inc(g.oT_ready, 1)


def rope_dve(g, v, link, s, half, cos, sin):
    split = lambda ap: ap.rearrange("p (q j) -> p q j", j=SEQ)
    both = lambda table: table.unsqueeze(1).to_broadcast([P, 16, SEQ])
    v.tensor_tensor(split(g.pr[s][:, 0:1024]), split(g.psf[s][:, 0:1024]), both(cos), ALU.mult)
    link(v.tensor_tensor(split(g.pr[s][:, 1024:2048]), split(g.psf[s][:, 1024:2048]), both(sin), ALU.mult))
    return v.tensor_tensor(g.qk[s][:, half:half + 2, :].rearrange("p a c -> p (a c)"), g.pr[s][:, 0:1024],
                           g.pr[s][:, 1024:2048], ALU.add)



def l1a_pe(g, pe):
    w = lambda name: g.w("L1A", name)

    def group(t, s, i):
        n, j, k = g.n0["L1A"] + t + 1, t + 1, g.k0["L1A"] + t + 1
        front_pe(g, pe, s, n)
        yield
        pe.wait_ge(g.xT_ready, n)
        for i in range(GT):
            ins = pe.matmul(g.psf[s][:, 256 * i:256 * i + QP + KVP], g.xT[s][:, i * P:(i + 1) * P], w("down"),
                            start=True, stop=True)
        ins.then_inc(g.m_down_done, 1)
        yield
        pe.wait_ge(g.m_latent_ready, j)
        for i in range(GT):
            at = i * (QP + KVP)
            pe.transpose(g.ps[s][0:KVP, 1, i * P:(i + 1) * P], g.pr[s][:, at + QP:at + QP + KVP], g.c("ident"))
            ins = pe.transpose(g.ps[s][0:QP, 0, i * P:(i + 1) * P], g.pr[s][:, at:at + QP], g.c("ident"))
        ins.then_inc(g.m_latent_turned, 1)
        yield
        pe.wait_ge(g.m_latentT_ready, j)
        cq, ckv = g.of[s][0:QP, :], g.oT[s][0:KVP, :]
        for i in range(2):
            pe.matmul(g.ps[s][:, i, :], w("qa")[0:QP, i * D:(i + 1) * D], cq, start=True, stop=True)
            ins = pe.matmul(g.ps[s][:, 2 + i, :], w("qb")[0:QP, i * D:(i + 1) * D], cq, start=True, stop=True)
        ins.then_inc(g.m_q_done, 1)
        yield
        pe.wait_ge(g.m_q_ready, j)
        for i in range(2):
            pe.matmul(g.ps[s][:, i, :], w("kn")[0:KVP, i * D:(i + 1) * D], ckv, start=True, stop=False)
            pe.matmul(g.ps[s][:, i, :], w("ka")[:, i * D:(i + 1) * D], g.xT[s][:, :], start=False, stop=True)
            ins = pe.matmul(g.ps[s][:, 2 + i, :], w("kb")[:, i * D:(i + 1) * D], g.xT[s][:, :], start=True, stop=True)
        ins.then_inc(g.m_k_done, 1)
        yield
        pe.wait_ge(g.m_k_ready, j)
        values_pe(g, pe, s, w("v"), g.oT[s], KVP).then_inc(g.m_v_done, 1)
        yield
        yield from attend_pe(g, pe, s, k, [(g.m_v_ready, j)], w("wo"))

    pairs(pe, g.groups, group)


def l1a_act(g, a):
    w = lambda name: g.w("L1A", name)

    def group(t, s, i):
        n, j, k = g.n0["L1A"] + t + 1, t + 1, g.k0["L1A"] + t + 1
        front_act(g, a, s, n)
        yield
        a.wait_ge(g.m_latent_turned, j)
        a.activation(g.of[s][0:QP, :], g.ps[s][0:QP, 0, :], ACT.Identity, bias=w("qbias")[0:QP, :], scale=w("qg")[0:QP, :])
        a.activation(g.oT[s][0:KVP, :], g.ps[s][0:KVP, 1, :], ACT.Identity, bias=w("kbias")[0:KVP, :],
                     scale=w("kg")[0:KVP, :]).then_inc(g.m_latentT_ready, 1)
        yield
        a.wait_ge(g.m_v_done, j)
        values_act(g, a, s).then_inc(g.m_v_ready, 1)
        yield
        yield from attend_act(g, a, s, k)

    pairs(a, g.groups, group)


def l1a_dve(g, v):
    links = slot_links(v, g.slot_link, g.link0["L1A"], LINKS["L1A"])

    def group(t, s, i):
        n, j, k = g.n0["L1A"] + t + 1, t + 1, g.k0["L1A"] + t + 1
        link = links[s]
        link.group(i)
        front_dve(g, v, link, s, t, n)
        yield
        v.wait_ge(g.const_loaded, 16)
        v.wait_ge(g.m_down_done, j)
        parts = [g.psf[s][:, 256 * i + lo:256 * i + hi] for lo, hi in ((0, QP), (QP, QP + KVP)) for i in range(GT)]
        outs = [g.pr[s][:, 149 * i + lo:149 * i + hi] for lo, hi in ((0, QP), (QP, QP + KVP)) for i in range(GT)]
        norm_dve(g, v, link, s, parts, 1e-5)
        normalise_dve(g, v, s, parts, outs).then_inc(g.m_latent_ready, 1)
        yield
        v.wait_ge(g.m_q_done, j)
        rope_dve(g, v, link, s, 0, g.c("mla_cos"), g.c("mla_sin")).then_inc(g.m_q_ready, 1)
        yield
        v.wait_ge(g.m_q_ready, j)
        v.wait_ge(g.m_k_done, j)
        rope_dve(g, v, link, s, 2, g.c("mla_cos"), g.c("mla_sin")).then_inc(g.m_k_ready, 1)
        yield
        softmax_dve(g, v, link, s, k, float(DH + 2) ** -0.5, g.c("causal"))
        yield
        turned_probs_dve(g, v, s, k)
        yield
        divide_dve(g, v, link, s, k)
        yield
        add_out_dve(g, v, s, t, k)
        link.end()

    pairs(v, g.groups, group)



def l2f_pe(g, pe):
    w = lambda name: g.w("L2F", name)

    def group(t, s, i):
        n, j, k = g.n0["L2F"] + t + 1, t + 1, g.k0["L2F"] + t + 1
        front_pe(g, pe, s, n)
        yield
        pe.wait_ge(g.f_conv_ready, j)
        project_qk_pe(g, pe, s, w("qk")).then_inc(g.f_qk_done, 1)
        yield
        pe.wait_ge(g.f_q_ready, j)
        values_pe(g, pe, s, w("v"), g.xT[s]).then_inc(g.f_v_done, 1)
        yield
        yield from attend_pe(g, pe, s, k, [(g.f_v_ready, j), (g.f_k_ready, j)], w("wo"))

    pairs(pe, g.groups, group)


def l2f_act(g, a):
    w = lambda name: g.w("L2F", name)

    def group(t, s, i):
        n, j, k = g.n0["L2F"] + t + 1, t + 1, g.k0["L2F"] + t + 1
        front_act(g, a, s, n)
        yield
        a.wait_ge(g.f_qk_done, j)
        for i in range(2):
            ins = a.activation(g.qk[s][:, i, :], g.ps[s][:, i, :], ACT.Identity, bias=w("qkb")[:, i:i + 1])
        ins.then_inc(g.f_q_ready, 1)
        for i in range(2, 4):
            ins = a.activation(g.qk[s][:, i, :], g.ps[s][:, i, :], ACT.Identity, bias=w("qkb")[:, i:i + 1])
        ins.then_inc(g.f_k_ready, 1)
        yield
        a.wait_ge(g.f_v_done, j)
        values_act(g, a, s).then_inc(g.f_v_ready, 1)
        yield
        yield from attend_act(g, a, s, k, bias=w("bv"), masked_after=g.f_exp_ready)

    pairs(a, g.groups, group)


def l2f_dve(g, v):
    w = lambda name: g.w("L2F", name)
    links = slot_links(v, g.slot_link, g.link0["L2F"], LINKS["L2F"])

    def group(t, s, i):
        n, j, k = g.n0["L2F"] + t + 1, t + 1, g.k0["L2F"] + t + 1
        link = links[s]
        link.group(i)
        front_dve(g, v, link, s, t, n)
        x, y = g.xT[s], g.t2[s][:, :, :].rearrange("p t d -> p (t d)")
        yield
        v.wait_ge(g.xT_ready, n)
        link(v.memset(x[:, :].rearrange("p (q j) -> p q j", j=SEQ)[:, :, TOK:SEQ], 0.0))
        link(v.scalar_tensor_tensor(y, x[:, :], w("conv")[:, 1:2], x[:, :], ALU.mult, ALU.add))
        link(v.scalar_tensor_tensor(y[:, 1:], x[:, 0:GTOK - 1], w("conv")[:, 0:1], y[:, 1:], ALU.mult, ALU.add))
        link(v.scalar_tensor_tensor(y[:, 0:GTOK - 1], x[:, 1:], w("conv")[:, 2:3], y[:, 0:GTOK - 1], ALU.mult, ALU.add))
        v.tensor_scalar(x[:, :], y, w("convb"), None, ALU.add).then_inc(g.f_conv_ready, 1)
        yield
        v.wait_ge(g.scores_done, k)
        rows = lambda ap: ap.rearrange("p (r j) -> p r j", j=SEQ)
        score, left = rows(g.pr[s][:, :]), rows(g.pt[s][:, :])
        best = g.small[s][:, :].rearrange("p (r e) -> p r e", e=8)
        link(v.scalar_tensor_tensor(score, rows(g.psf[s]), float(D) ** -0.5,
                                    g.c("keys").unsqueeze(1).to_broadcast([P, 32, SEQ]), ALU.mult, ALU.add), g.wait_carrier)
        source = score
        for turn in range(2):
            for r in range(32):
                ins = v.max(best[:, r, :], source[:, r, 0:TOK])
            link(ins, g.wait_carrier)
            if turn == 0:
                v.tensor_copy(g.rm[s][:, 0:32], best[:, :, 0])
            for r in range(32):
                ins = v.match_replace(left[:, r, 0:TOK], best[:, r, :], source[:, r, 0:TOK], PICKED)
            link(ins, g.wait_carrier)
            source = left
        v.tensor_tensor(score, score, g.rm[s][:, 0:32].unsqueeze(2).to_broadcast([P, 32, SEQ]),
                        ALU.subtract).then_inc(g.centred_ready, 1)
        yield
        v.wait_ge(g.f_exp_ready, j)
        v.scalar_tensor_tensor(score[:, :, 0:TOK], left[:, :, 0:TOK], 0.5 * (NEG + PICKED), score[:, :, 0:TOK],
                               ALU.is_lt, ALU.mult).then_inc(g.probs_ready, 1)
        yield
        turned_probs_dve(g, v, s, k)
        yield
        divide_dve(g, v, link, s, k)
        yield
        add_out_dve(g, v, s, t, k, w("bo"), link)
        link.end()

    pairs(v, g.groups, group)



def l3a_fold_pe(g, pe):
    w = lambda name: g.w("L3A", name)
    pe.wait_ge(g.slot_free, g.n0["L3A"] + SLOTS)
    pe.matmul(g.ps[0][:, 0, :], w("la")[0:8, :], w("lbqk")[0:8, :], start=True, stop=True)
    pe.matmul(g.ps[0][:, 1, 0:D], w("la")[0:8, :], w("lbv")[0:8, :], start=True, stop=True)
    pe.matmul(g.ps[0][:, 2, 0:D], w("loa")[0:8, :], w("lob")[0:8, :], start=True, stop=True).then_inc(g.lora_pe, 1)
    pe.wait_ge(g.lora_dve, 1)


def l3a_fold_dve(g, v):
    v.wait_ge(g.lora_pe, 1)
    for bank, name in enumerate(("qk", "v", "wo")):
        w = g.w("L3A", name)
        ins = v.scalar_tensor_tensor(w, g.ps[0][:, bank, 0:w.shape[1]], 0.25, w, ALU.mult, ALU.add)
    ins.then_inc(g.lora_dve, 1)


def l3a_pe(g, pe):
    w = lambda name: g.w("L3A", name)
    l3a_fold_pe(g, pe)

    def group(t, s, i):
        n, j, k = g.n0["L3A"] + t + 1, t + 1, g.k0["L3A"] + t + 1
        front_pe(g, pe, s, n)
        yield
        pe.wait_ge(g.xT_ready, n)
        project_qk_pe(g, pe, s, w("qk")).then_inc(g.w_qk_done, 1)
        yield
        pe.wait_ge(g.w_q_ready, j)
        pe.matmul(g.ps[s][:, 1, 0:2 * GT], w("v"), g.xT[s][:, 0:GTOK:SEQ], start=True, stop=True)
        values_pe(g, pe, s, w("v"), g.xT[s]).then_inc(g.w_v_done, 1)
        yield
        yield from attend_pe(g, pe, s, k, [(g.w_v_ready, j), (g.w_k_ready, j)], w("wo"))

    pairs(pe, g.groups, group)


def l3a_act(g, a):
    def group(t, s, i):
        n, j, k = g.n0["L3A"] + t + 1, t + 1, g.k0["L3A"] + t + 1
        front_act(g, a, s, n)
        yield
        a.wait_ge(g.w_qk_done, j)
        a.activation(g.qk[s][:, 0:2, :], g.ps[s][:, 0:2, :], ACT.Copy).then_inc(g.w_q_ready, 1)
        yield
        a.wait_ge(g.w_v_done, j)
        a.activation(g.small[s][:, 0:2 * GT], g.ps[s][:, 1, 0:2 * GT], ACT.Copy)
        values_act(g, a, s).then_inc(g.w_v_ready, 1)
        yield
        yield from attend_act(g, a, s, k, turn_out=False)

    pairs(a, g.groups, group)


def l3a_dve(g, v):
    w = lambda name: g.w("L3A", name)
    l3a_fold_dve(g, v)
    links = slot_links(v, g.slot_link, g.link0["L3A"], LINKS["L3A"])

    def group(t, s, i):
        n, j, k = g.n0["L3A"] + t + 1, t + 1, g.k0["L3A"] + t + 1
        link = links[s]
        link.group(i)
        front_dve(g, v, link, s, t, n)
        yield
        v.wait_ge(g.w_qk_done, j)
        v.tensor_copy(g.qk[s][:, 2:4, :], g.ps[s][:, 2:4, :]).then_inc(g.w_k_ready, 1)
        yield
        softmax_dve(g, v, link, s, k, DH ** -0.5, g.c("causal"))
        yield
        turned_probs_dve(g, v, s, k)
        yield
        divide_dve(g, v, link, s, k)
        yield
        v.wait_ge(g.o_turned, k)
        split = lambda ap: ap.rearrange("p (q j) -> p q j", j=SEQ)
        v.tensor_tensor(split(g.oT[s][:, :]), split(g.ps[s][:, 2, :]),
                        g.small[s][:, 0:2 * GT].unsqueeze(2).to_broadcast([P, 2 * GT, SEQ]), ALU.add).then_inc(g.oT_ready, 1)
        yield
        add_out_dve(g, v, s, t, k, w("bo"), link)
        link.end()

    pairs(v, g.groups, group)



def rms_dve(g, v, link, s):
    for i in range(GT):
        ins = v.bn_stats(g.stats[s][:, i, :], g.xn[s][:, i, :])
    link(ins, g.wait_carrier)
    for i in range(GT):
        ins = v.bn_aggr(g.mv[s][:, i, :], g.stats[s][:, i, :])
    link(ins)
    link(v.tensor_tensor(g.rm[s][:, 0:GT], g.mv[s][:, 0:GT, 0], g.mv[s][:, 0:GT, 0], ALU.mult))
    link(v.tensor_tensor(g.rm[s][:, 0:GT], g.rm[s][:, 0:GT], g.mv[s][:, 0:GT, 1], ALU.add))
    rsqrt_dve(g, v, link, s, GT, g.rm[s][:, 0:GT], 1e-5)


def l3f_pe(g, pe):
    w = lambda name: g.w("L3F", name)

    def group(t, s, i):
        n, j, k = g.n0["L3F"] + t + 1, t + 1, g.k0["L3F"] + t + 1
        pe.wait_ge(g.const_loaded, 16)
        pe.wait_ge(g.xn_ready, n)
        for i in range(GT):
            ins = pe.transpose(g.ps[s][:, 0, i * P:(i + 1) * P], g.t2[s][:, i, :], g.c("ident"))
        ins.then_inc(g.xn_transposed, 1)
        yield
        pe.wait_ge(g.xT_ready, n)
        for q, done, ready in ((0, g.p_q_done, g.p_q_ready), (2, g.p_k_done, g.p_k_ready)):
            for i in range(2):
                cols = slice((q + i) * D, (q + i + 1) * D)
                pe.matmul(g.ps[s][:, i, :], w("qk")[:, cols], g.xT[s][:, :], start=True, stop=True)
                ins = pe.matmul(g.ps[s][:, 2 + i, :], w("qkr")[:, cols], g.xT[s][:, :], start=True, stop=True)
            ins.then_inc(done, 1)
            yield
            pe.wait_ge(ready, j)
        values_pe(g, pe, s, w("v"), g.xT[s]).then_inc(g.p_v_done, 1)
        yield
        yield from attend_pe(g, pe, s, k, [(g.p_v_ready, j)], w("wo"))

    pairs(pe, g.groups, group)


def l3f_act(g, a):
    w = lambda name: g.w("L3F", name)

    def group(t, s, i):
        n, j, k = g.n0["L3F"] + t + 1, t + 1, g.k0["L3F"] + t + 1
        a.wait_ge(g.xn_transposed, n)
        a.activation(g.xT[s][:, :], g.ps[s][:, 0, :], ACT.Copy, scale=w("nw")).then_inc(g.xT_ready, 1)
        yield
        a.wait_ge(g.p_v_done, j)
        values_act(g, a, s).then_inc(g.p_v_ready, 1)
        yield
        yield from attend_act(g, a, s, k)

    pairs(a, g.groups, group)


def l3f_dve(g, v):
    links = slot_links(v, g.slot_link, g.link0["L3F"], LINKS["L3F"])

    def group(t, s, i):
        n, j, k = g.n0["L3F"] + t + 1, t + 1, g.k0["L3F"] + t + 1
        link = links[s]
        link.group(i)
        v.wait_ge(g.const_loaded, 16)
        v.wait_ge(g.slot_free, n)
        rows = [g.h[:, bass.ds(t * GT + i, 1), :] for i in range(GT)]
        norm_dve(g, v, link, s, rows, 1e-5)
        link(normalise_dve(g, v, s, rows, [g.xn[s][:, i:i + 1, :] for i in range(GT)]))
        rms_dve(g, v, link, s)
        for i in range(GT):
            ins = v.tensor_scalar(g.t2[s][:, i, :], g.xn[s][:, i, :], g.rs[s][:, i:i + 1], None, ALU.mult)
        ins.then_inc(g.xn_ready, 1)
        yield
        v.wait_ge(g.p_q_done, j)
        rope_dve(g, v, link, s, 0, g.c("rope_cos"), g.c("rope_sin")).then_inc(g.p_q_ready, 1)
        yield
        v.wait_ge(g.p_q_ready, j)
        v.wait_ge(g.p_k_done, j)
        rope_dve(g, v, link, s, 2, g.c("rope_cos"), g.c("rope_sin")).then_inc(g.p_k_ready, 1)
        yield
        softmax_dve(g, v, link, s, k, DH ** -0.5, g.c("causal"))
        yield
        turned_probs_dve(g, v, s, k)
        yield
        divide_dve(g, v, link, s, k)
        yield
        v.wait_ge(g.out_done, k)
        link(v.tensor_tensor(g.a[:, bass.ds(t * GT, GT), :], g.ps[s][:, 3, :].rearrange("p (t d) -> p t d", d=D),
                             g.xn[s][:, :, :], ALU.add))
        h = g.h[:, bass.ds(t * GT, GT), :]
        v.tensor_tensor(h, g.a[:, bass.ds(t * GT, GT), :], h, ALU.add).then_inc(g.slot_free, 1)
        link.end()

    pairs(v, g.groups, group)


class Moe:

    def __init__(self, stage, kind, hidden):
        self.stage, self.kind = stage, kind
        self.up = hidden if kind != "swish" else 2 * hidden
        self.chunks = hidden // P
        self.units = self.up // (2 * P)
        self.links = NORM_LINKS + (2 if kind == "gelu" else 0) + 7
        self.cols = {}
        at = 0
        parts = [("up", EXPERTS * self.up), ("down", EXPERTS * self.chunks * D), ("router", EXPERTS)]
        if kind != "gelu":
            parts += [("rb", EXPERTS), ("ub", EXPERTS * self.up // P), ("db", D)]
        if kind == "swish":
            parts += [("sb", EXPERTS * self.up // P)]
        if kind == "gelu":
            parts += [("nw", 1)]
        for name, n in parts:
            self.cols[name] = (at, n)
            at += n
        self.width = at

    def w(self, g, name):
        at, n = self.cols[name]
        return g.w_big[:, at:at + n]


MOE = {"L0M": Moe("L0M", "swish", 256), "L1M": Moe("L1M", "relu", 256), "L3M": Moe("L3M", "gelu", 512)}
W_BIG = max(m.width for m in MOE.values())
ROUTE = 16
SENTINEL = -1.0e38



def moe_acts(g, e, chunk):
    return g.pr[e % 2][:, chunk * GTOK:(chunk + 1) * GTOK]


def moe_pe(stage):
    m = MOE[stage]

    def program(g, pe):
        sem = g.moe[stage]
        up, down = m.w(g, "up"), m.w(g, "down")
        pe.wait_ge(g.slot_free, g.n0[stage] + SLOTS)

        def turn_x(t, s, first=False):
            n = g.n0[stage] + t + 1
            if not first and m.kind != "gelu":
                pe.wait_ge(sem.gatesT_ready, g.m0[stage] + t)
            pe.wait_ge(g.xn_ready, n)
            for i in range(GT):
                ins = pe.transpose(g.ps[1][:, 2, i * P:(i + 1) * P], g.xn[s][:, i, :], g.c("ident"))
            ins.then_inc(g.xn_transposed, 1)

        def logits(t, s, first=False):
            pe.wait_ge(g.xT_ready, g.n0[stage] + t + 1)
            if not first:
                pe.wait_ge(sem.route_centred, g.m0[stage] + t)
            if not first and m.kind != "gelu":
                pe.wait_ge(sem.bias_added, g.m0[stage] + t)
            for i in range(GT):
                ins = pe.matmul(g.ps[1][:, 3, i * EXPERTS:(i + 1) * EXPERTS], g.xT[s][:, i * P:(i + 1) * P],
                                m.w(g, "router"), start=True, stop=True)
            ins.then_inc(sem.logits_done, 1)

        def turn_gates(t, s):
            pe.wait_ge(sem.gates_ready, g.m0[stage] + t + 1)
            for i in range(GT):
                ins = pe.transpose(g.ps[1][0:EXPERTS, 2, i * P:(i + 1) * P], g.gates[s][:, i * EXPERTS:(i + 1) * EXPERTS],
                                   g.c("ident"))
            ins.then_inc(sem.gates_turned, 1)

        def bias(t, s):
            pe.wait_ge(sem.gatesT_ready, g.m0[stage] + t + 1)
            for i in range(GT):
                ins = pe.matmul(g.ps[1][:, 3, i * P:(i + 1) * P], g.oT[s][0:EXPERTS, i * P:(i + 1) * P],
                                m.w(g, "db")[0:EXPERTS, :], start=True, stop=True)
            ins.then_inc(sem.bias_done, 1)

        def unit(t, s, e, u):
            if m.kind == "relu":
                pe.wait_ge(sem.hidden_ready, t * EXPERTS + e + 1)
                pe.wait_ge(sem.hidden_ready_v, t * EXPERTS + e + 1)
            else:
                pe.wait_ge(sem.unit_free, (t * EXPERTS + e) * m.units + u + 1)
            b = 2 * ((e * m.units + u) % 2)
            for i in range(2):
                c = e * m.up + (i * m.chunks + u if m.kind == "swish" else 2 * u + i) * P
                ins = pe.matmul(g.ps[0][:, b + i, :], up[:, c:c + P], g.xT[s][:, :], start=True, stop=True)
            ins.then_inc(sem.unit_done, 1)

        def down_of(t, s, e):
            if m.kind == "relu":
                pe.wait_ge(sem.hidden_ready, t * EXPERTS + e + 3)
                pe.wait_ge(sem.hidden_ready_v, t * EXPERTS + e + 3)
            else:
                pe.wait_ge(sem.unit_free, (t * EXPERTS + e + 1) * m.units + 2)
            pe.wait_ge(sem.down_free, t * EXPERTS + e + 1)
            for i in range(GT):
                for c in range(m.chunks):
                    at = (e * m.chunks + c) * D
                    ins = pe.matmul(g.ps[1][:, e % 2, i * P:(i + 1) * P], moe_acts(g, e, c)[:, i * P:(i + 1) * P],
                                    down[:, at:at + D], start=(c == 0), stop=(c == m.chunks - 1))
            ins.then_inc(sem.down_done, 1)

        def prepare(t, s):
            turn_x(t, s, True)
            logits(t, s, True)
            if m.kind != "gelu":
                turn_gates(t, s)

        def group(t, s, following):
            for e in range(EXPERTS):
                for u in range(m.units):
                    unit(t, s, e, u)
                    if u == 0 and e > 0:
                        down_of(t, s, e - 1)
                if e == 0 and m.kind != "gelu":
                    bias(t, s)
                if following:
                    if e == 3:
                        turn_x(t + 1, 1 - s)
                    if e == 4:
                        logits(t + 1, 1 - s)
                    if e == 6 and m.kind != "gelu":
                        turn_gates(t + 1, 1 - s)
            down_of(t, s, EXPERTS - 1)

        prepare(0, 0)
        moe_groups(pe, g, group)

    return program


def moe_groups(eng, g, group):
    if g.groups > 2:
        with eng.Fori(0, g.groups // 2 - 1) as i:
            group(i * 2, 0, True)
            group(i * 2 + 1, 1, True)
    group(g.groups - 2, 0, True)
    group(g.groups - 1, 1, False)


def moe_act(stage):
    m = MOE[stage]

    def program(g, a):
        sem = g.moe[stage]
        if m.kind == "swish":
            a.wait_ge(sem.bias_scaled, 1)

        def evacuate_x(t, s):
            n = g.n0[stage] + t + 1
            a.wait_ge(g.xn_transposed, n)
            if m.kind == "gelu":
                a.activation(g.xT[s][:, :], g.ps[1][:, 2, :], ACT.Copy, scale=m.w(g, "nw")).then_inc(g.xT_ready, 1)
            else:
                a.activation(g.xT[s][:, :], g.ps[1][:, 2, :], ACT.Copy).then_inc(g.xT_ready, 1)

        def exponentials(t, s):
            a.wait_ge(sem.route_centred, g.m0[stage] + t + 1)
            a.activation(g.gates[s][:, :], g.gates[s][:, :], ACT.Exp).then_inc(sem.route_exp, 1)

        def evacuate_gates(t, s):
            a.wait_ge(sem.gates_turned, g.m0[stage] + t + 1)
            a.activation(g.oT[s][0:EXPERTS, :], g.ps[1][0:EXPERTS, 2, :], ACT.Copy).then_inc(sem.gatesT_ready, 1)

        def unit(t, s, e, u):
            b = 2 * ((e * m.units + u) % 2)
            a.wait_ge(sem.unit_done, (t * EXPERTS + e) * m.units + u + 1)
            if m.kind == "swish":
                at = e * m.up // P + u
                a.activation(g.pt[0][:, (b // 2) * GTOK:(b // 2 + 1) * GTOK], g.ps[0][:, b, :], ACT.Sigmoid, scale=1.702,
                             bias=m.w(g, "sb")[:, at:at + 1]).then_inc(sem.sig_ready, 1)
                return
            if u == 0:
                a.wait_ge(sem.down_done, t * EXPERTS + e + 1)
            if m.kind == "relu":
                at = e * m.up // P
                a.activation(moe_acts(g, e, 0), g.ps[0][:, b, :], ACT.Relu, bias=m.w(g, "ub")[:, at:at + 1])\
                    .then_inc(sem.hidden_ready, 1)
            else:
                ins = a.activation(g.pr[e % 2][:, 2 * u * GTOK:(2 * u + 2) * GTOK],
                                   g.ps[0][:, b:b + 2, :], ACT.Gelu)
                ins.then_inc(sem.unit_free, 1)

        def group(t, s, following):
            for e in range(EXPERTS):
                for u in range(m.units):
                    unit(t, s, e, u)
                if following:
                    if e == 3:
                        evacuate_x(t + 1, 1 - s)
                    if e == 5:
                        exponentials(t + 1, 1 - s)
                    if e == 7 and m.kind != "gelu":
                        evacuate_gates(t + 1, 1 - s)

        evacuate_x(0, 0)
        exponentials(0, 0)
        if m.kind != "gelu":
            evacuate_gates(0, 0)
        moe_groups(a, g, group)

    return program


def moe_dve(stage):
    m = MOE[stage]

    def program(g, v):
        sem = g.moe[stage]
        link = Link(v, g.moe_link, g.link0[stage], m.links)
        v.wait_ge(g.slot_free, g.n0[stage] + SLOTS)
        v.sem_inc(sem.down_free, 2)
        v.sem_inc(sem.down_done, 2)
        if m.kind == "relu":
            v.sem_inc(sem.hidden_ready, 2)
            v.sem_inc(sem.hidden_ready_v, 2)
        else:
            v.sem_inc(sem.unit_free, 2)
        for s in range(SLOTS):
            ins = v.memset(g.small[s][:, 0:192], SENTINEL)
        if m.kind == "swish":
            v.tensor_scalar(m.w(g, "sb"), m.w(g, "ub"), 1.702, None, ALU.mult).then_inc(sem.bias_scaled, 1)
            v.wait_ge(sem.bias_scaled, 1)
            ub = m.w(g, "ub").rearrange("p (e c) -> p e c", e=EXPERTS)[:, :, m.chunks:]
            ins = v.tensor_scalar(ub, ub, 1.0, None, ALU.add)
        ins.then_inc(sem.bias_scaled, 1)
        v.wait_ge(sem.bias_scaled, 2 if m.kind == "swish" else 1)
        source = g.a if m.kind == "gelu" else g.h

        def normalise(t, s):
            v.wait_ge(g.const_loaded, 16)
            rows = [source[:, bass.ds(t * GT + i, 1), :] for i in range(GT)]
            if m.kind != "gelu":
                norm_dve(g, v, link, s, rows, 1e-5)
                ins = normalise_dve(g, v, s, rows, [g.xn[s][:, i:i + 1, :] for i in range(GT)])
            else:
                for i in range(GT):
                    ins = v.bn_stats(g.stats[s][:, i, :], rows[i])
                link(ins, g.wait_carrier)
                for i in range(GT):
                    ins = v.bn_aggr(g.mv[s][:, i, :], g.stats[s][:, i, :])
                link(ins)
                link(v.tensor_tensor(g.rm[s][:, 0:GT], g.mv[s][:, 0:GT, 0], g.mv[s][:, 0:GT, 0], ALU.mult))
                link(v.tensor_tensor(g.rm[s][:, 0:GT], g.rm[s][:, 0:GT], g.mv[s][:, 0:GT, 1], ALU.add))
                rsqrt_dve(g, v, link, s, GT, g.rm[s][:, 0:GT], 1e-5)
                for i in range(GT):
                    ins = v.tensor_scalar(g.xn[s][:, i:i + 1, :], rows[i], g.rs[s][:, i:i + 1], None, ALU.mult)
            ins.then_inc(g.xn_ready, 1)

        def route(t, s):
            lg = g.small[s][:, 0:GT * ROUTE].rearrange("p (t c) -> p t c", t=GT)
            left = g.small[s][:, 64:64 + GT * ROUTE].rearrange("p (t c) -> p t c", t=GT)
            top = g.small[s][:, 128:128 + GT * 8].rearrange("p (t c) -> p t c", t=GT)
            two = g.small[s][:, 160:160 + GT * 8].rearrange("p (t c) -> p t c", t=GT)
            ps = g.ps[1][:, 3, 0:GT * EXPERTS].rearrange("p (t e) -> p t e", t=GT)
            v.wait_ge(sem.logits_done, g.m0[stage] + t + 1)
            if m.kind == "gelu":
                link(v.tensor_copy(lg[:, :, 0:EXPERTS], ps), g.wait_carrier)
            else:
                link(v.tensor_tensor(lg[:, :, 0:EXPERTS], ps, m.w(g, "rb").unsqueeze(1).to_broadcast([P, GT, EXPERTS]), ALU.add),
                     g.wait_carrier)
            for i in range(GT):
                ins = v.max(top[:, i, :], lg[:, i, 0:EXPERTS])
            link(ins)
            link(v.tensor_copy(two[:, :, 0:2], top[:, :, 0:2]), g.wait_carrier)
            for i in range(GT):
                ins = v.match_replace(left[:, i, 0:14], two[:, i, :], lg[:, i, 0:14], PICKED)
            link(ins)
            gates = g.gates[s][:, :].rearrange("p (t e) -> p t e", t=GT)
            v.tensor_tensor(gates, lg[:, :, 0:EXPERTS], top[:, :, 0:1].to_broadcast([P, GT, EXPERTS]),
                            ALU.subtract).then_inc(sem.route_centred, 1)

        def gate(t, s):
            left = g.small[s][:, 64:64 + GT * ROUTE].rearrange("p (t c) -> p t c", t=GT)
            gates = g.gates[s][:, :].rearrange("p (t e) -> p t e", t=GT)
            sums = g.small[s][:, 192:192 + GT]
            v.wait_ge(sem.route_exp, g.m0[stage] + t + 1)
            link(v.scalar_tensor_tensor(gates, left[:, :, 0:EXPERTS], 0.5 * (SENTINEL + PICKED), gates, ALU.is_lt, ALU.mult))
            link(v.tensor_reduce(sums, gates, AX.X, ALU.add))
            link(v.reciprocal(sums, sums))
            v.tensor_tensor(gates, gates, sums.unsqueeze(2).to_broadcast([P, GT, EXPERTS]),
                            ALU.mult).then_inc(sem.gates_ready, 1)
            link.end()

        def unit(t, s, e, u):
            b = 2 * ((e * m.units + u) % 2)
            at = e * m.up // P + u
            if m.kind == "swish":
                sig = g.pt[0][:, (b // 2) * GTOK:(b // 2 + 1) * GTOK]
                v.wait_ge(sem.sig_ready, (t * EXPERTS + e) * m.units + u + 1)
                v.scalar_tensor_tensor(sig, g.ps[0][:, b, :], m.w(g, "ub")[:, at:at + 1], sig,
                                       ALU.add, ALU.mult).then_inc(sem.sig_gated, 1)
                v.wait_ge(sem.sig_gated, (t * EXPERTS + e) * m.units + u + 1)
                if u == 0:
                    v.wait_ge(sem.down_done, t * EXPERTS + e + 1)
                at += m.chunks
                v.scalar_tensor_tensor(moe_acts(g, e, u), g.ps[0][:, b + 1, :], m.w(g, "ub")[:, at:at + 1], sig,
                                       ALU.add, ALU.mult).then_inc(sem.unit_free, 1)
            if m.kind == "relu":
                v.wait_ge(sem.unit_done, t * EXPERTS + e + 1)
                v.wait_ge(sem.down_done, t * EXPERTS + e + 1)
                v.tensor_scalar(moe_acts(g, e, 1), g.ps[0][:, b + 1, :], m.w(g, "ub")[:, at + 1:at + 2], 0.0,
                                ALU.add, ALU.max).then_inc(sem.hidden_ready_v, 1)

        def gather(t, s, e):
            if e == 0:
                v.wait_ge(sem.gates_ready, g.m0[stage] + t + 1)
            if e == 1 and m.kind != "gelu":
                v.wait_ge(sem.bias_added, g.m0[stage] + t + 1)
            v.wait_ge(sem.down_free, t * EXPERTS + e + 2)
            v.wait_ge(sem.down_done, t * EXPERTS + e + 3)
            for i in range(GT):
                row = g.h[:, bass.ds(t * GT + i, 1), :]
                ins = v.scalar_tensor_tensor(row, g.ps[1][:, e % 2:e % 2 + 1, i * P:(i + 1) * P],
                                             g.gates[s][:, i * EXPERTS + e:i * EXPERTS + e + 1], row, ALU.mult, ALU.add)
            ins.then_inc(sem.down_free, 1)

        def add_bias(t, s):
            v.wait_ge(sem.down_free, t * EXPERTS + 3)
            v.wait_ge(sem.bias_done, g.m0[stage] + t + 1)
            h = g.h[:, bass.ds(t * GT, GT), :]
            v.tensor_tensor(h, g.ps[1][:, 3, :].rearrange("p (t d) -> p t d", d=D), h, ALU.add).then_inc(sem.bias_added, 1)

        def group(t, s, following):
            for e in range(EXPERTS):
                for u in range(m.units):
                    unit(t, s, e, u)
                if e == 2 and m.kind != "gelu":
                    add_bias(t, s)
                if following:
                    if e == 1:
                        link.group(t + 1)
                        normalise(t + 1, 1 - s)
                    if e == 4:
                        route(t + 1, 1 - s)
                    if e == 5:
                        gate(t + 1, 1 - s)
                if e > 0:
                    gather(t, s, e - 1)
            gather(t, s, EXPERTS - 1)
            v.wait_ge(sem.down_free, (t + 1) * EXPERTS + 2)
            v.sem_inc(g.slot_free, 1)

        link.group(0)
        normalise(0, 0)
        route(0, 0)
        gate(0, 0)
        moe_groups(v, g, group)

    return program


MOE_SEMS = ("logits_done", "gates_ready", "gates_turned", "gatesT_ready", "bias_done", "bias_added", "route_centred",
            "route_exp", "hidden_ready", "hidden_ready_v", "sig_ready", "sig_gated")
MOE_STAGE_SEMS = ("unit_free", "unit_done", "down_free", "down_done", "bias_scaled")


def moe_semaphores(sem, stages):
    common = [sem("moe_" + n) for n in MOE_SEMS]
    out = {}
    for st in stages:
        names = out[st] = Net()
        (names.logits_done, names.gates_ready, names.gates_turned, names.gatesT_ready, names.bias_done, names.bias_added,
         names.route_centred, names.route_exp, names.hidden_ready, names.hidden_ready_v, names.sig_ready,
         names.sig_gated) = common
        names.unit_free, names.unit_done, names.down_free, names.down_done, names.bias_scaled = (
            sem(f"{st}_{n}") for n in MOE_STAGE_SEMS)
    return out



MID = SEQ // 2 - 1


def l2a_gate(g, s):
    return g.a[:, 16 * s + 0:16 * s + 16, :].rearrange("p t d -> p (t d)")


def l2a_scores(g, s):
    return g.scores_sb[s][:, :]


def l2a_pe(g, pe):
    w = lambda name: g.w("L2A", name)

    def group(t, s, i):
        n, j = g.n0["L2A"] + t + 1, t + 1
        front_pe(g, pe, s, n)
        yield
        pe.wait_ge(g.xT_ready, n)
        pe.matmul(g.ps[s][0:GR, 0, :], w("gk1"), g.xT[s][:, :], start=True, stop=True).then_inc(g.l_low_done, 1)
        yield
        pe.wait_ge(g.l_low_ready, j)
        for c in range(2):
            ins = pe.matmul(g.ps[s][:, c, :], w("gk2")[0:GR, c * P:(c + 1) * P], g.oT[s][0:GR, :], start=True, stop=True)
        ins.then_inc(g.l_gk_done, 1)
        yield
        pe.wait_ge(g.l_gk_read, j)
        for i in range(4):
            ins = pe.matmul(g.ps[s][:, i, :], w("qk")[:, i * D:(i + 1) * D], g.xT[s][:, :], start=True, stop=True)
        ins.then_inc(g.l_qk_done, 1)
        yield
        pe.wait_ge(g.l_qk_ready, j)
        for i in range(GT):
            ins = pe.matmul(g.ps[s][:, i, :], g.xT[s][:, i * P:(i + 1) * P], w("v"), start=True, stop=True)
        ins.then_inc(g.l_v_done, 1)
        yield
        pe.wait_ge(g.l_v_ready, j)
        for i in range(GT):
            ins = pe.matmul(g.ps[s][:, i, :], g.xT[s][:, i * P:(i + 1) * P], w("g"), start=True, stop=True)
        ins.then_inc(g.l_g_done, 1)
        yield
        pe.wait_ge(g.const_loaded, 16)
        pe.wait_ge(g.l_silu_ready, j)
        for sq in range(2):
            for c in range(2):
                for tile in range(GT):
                    for par in range(2):
                        rows, cols = slice(64 * par, 64 * par + 64), slice(tile * P + sq * SEQ, tile * P + sq * SEQ + SEQ)
                        at = (tile * 2 + c) * SEQ
                        ins = pe.matmul(g.ps[s][64 * sq:64 * sq + 64, par, at:at + SEQ], g.qk[s][rows, 2 + c, cols],
                                        g.qk[s][rows, c, cols], start=True, stop=True)
        ins.then_inc(g.l_scores_done, 1)
        yield
        pe.wait_ge(g.const_loaded, 16)
        pe.wait_ge(g.l_scores_ready, j)
        for tile in range(GT):
            for h in range(GH):
                for sq in range(2):
                    rows = slice(64 * sq, 64 * sq + 64)
                    at = (h % 2) * 512 + (tile * 2 + h // 2) * SEQ
                    ins = pe.matmul(g.ps[s][rows, tile, h * GV:(h + 1) * GV], l2a_scores(g, s)[rows, at:at + SEQ],
                                    g.pt[s][rows, tile * 512 + h * GV:tile * 512 + (h + 1) * GV], start=True, stop=True)
        ins.then_inc(g.l_o_done, 1)
        yield
        pe.wait_ge(g.l_og_ready, j)
        og = l2a_gate(g, s)
        for h in range(GH):
            for tile in range(GT):
                at = tile * 512 + h * GV
                ins = pe.transpose(g.ps[s][:, h, tile * P:(tile + 1) * P], og[:, at:at + GV], g.c("ident"))
        ins.then_inc(g.l_og_turned, 1)
        yield
        pe.wait_ge(g.l_ogT_ready_a, j)
        pe.wait_ge(g.l_ogT_ready_v, j)
        for tile in range(GT):
            for h in range(GH):
                ins = pe.matmul(g.ps[s][:, 3, tile * P:(tile + 1) * P], g.qk[s][:, h, tile * P:(tile + 1) * P],
                                w("wo")[:, h * D:(h + 1) * D], start=(h == 0), stop=(h == GH - 1))
        ins.then_inc(g.l_out_done, 1)

    pairs(pe, g.groups, group)


def l2a_act(g, a):
    def group(t, s, i):
        n, j = g.n0["L2A"] + t + 1, t + 1
        front_act(g, a, s, n)
        yield
        a.wait_ge(g.l_low_done, j)
        a.activation(g.oT[s][0:GR, :], g.ps[s][0:GR, 0, :], ACT.Copy).then_inc(g.l_low_ready, 1)
        neg = g.pr[s][:, 1024:2048]
        yield
        a.wait_ge(g.l_gk_read, j)
        a.activation(neg, neg, ACT.Exp).then_inc(g.l_neg_exp, 1)
        yield
        a.wait_ge(g.l_neg_exp, j)
        a.activation(neg, neg, ACT.Ln, bias=1.0).then_inc(g.l_log_ready, 1)
        yield
        a.wait_ge(g.l_sum_ready, j)
        a.activation(g.pr[s][:, 1024:2048], g.pr[s][:, 0:1024], ACT.Exp, scale=1.0 / 16.0).then_inc(g.l_exp_ready, 1)
        yield
        a.wait_ge(g.l_exp_ready, j)
        a.activation(g.pr[s][:, 0:1024], g.pr[s][:, 0:1024], ACT.Exp, scale=-1.0 / 16.0).then_inc(g.l_inverse_ready, 1)
        yield
        a.wait_ge(g.l_v_done, j)
        a.activation(g.pt[s][:, :], g.psf[s], ACT.Copy).then_inc(g.l_v_ready, 1)
        yield
        a.wait_ge(g.l_g_done, j)
        a.activation(l2a_gate(g, s), g.psf[s], ACT.Silu).then_inc(g.l_silu_ready, 1)
        yield
        a.wait_ge(g.l_o_done, j)
        a.activation(g.pr[s][:, :], g.psf[s], ACT.Square).then_inc(g.l_sq_ready, 1)
        yield
        a.wait_ge(g.l_og_turned, j)
        a.activation(g.qk[s][:, 0:2, :], g.ps[s][:, 0:2, :], ACT.Copy).then_inc(g.l_ogT_ready_a, 1)

    pairs(a, g.groups, group)


def l2a_dve(g, v):
    w = lambda name: g.w("L2A", name)
    v.tensor_scalar(w("wo"), w("wo"), w("rms"), None, ALU.mult).then_inc(g.l_fold, 1)
    v.wait_ge(g.l_fold, 1)
    links = slot_links(v, g.slot_link, g.link0["L2A"], LINKS["L2A"])

    def group(t, s, i):
        n, j = g.n0["L2A"] + t + 1, t + 1
        link = links[s]
        link.group(i)
        front_dve(g, v, link, s, t, n)
        z, neg = g.pr[s][:, 0:1024], g.pr[s][:, 1024:2048]
        yield
        v.wait_ge(g.l_gk_done, j)
        for c in range(2):
            ins = v.tensor_scalar(z[:, c * 512:(c + 1) * 512], g.ps[s][:, c, :], w("gkb")[:, c:c + 1], None, ALU.add)
        link(ins)
        v.scalar_tensor_tensor(neg, z, -1.0, z, ALU.mult, ALU.min).then_inc(g.l_gk_read, 1)
        yield
        v.wait_ge(g.l_log_ready, j)
        link(v.scalar_tensor_tensor(z, z, 0.0, neg, ALU.min, ALU.subtract))
        for c in range(2):
            ins = v.tensor_tensor_scan(neg[:, c * 512:(c + 1) * 512], g.c("restart"), z[:, c * 512:(c + 1) * 512], 0.0,
                                       ALU.mult, ALU.add)
        link(ins)
        seqs = lambda ap: ap.rearrange("p (q j) -> p q j", j=SEQ)
        v.tensor_tensor(seqs(z), seqs(neg), seqs(neg)[:, :, MID:MID + 1].to_broadcast([P, 16, SEQ]),
                        ALU.subtract).then_inc(g.l_sum_ready, 1)
        yield
        v.wait_ge(g.l_qk_done, j)
        v.wait_ge(g.l_inverse_ready, j)
        flat = g.qk[s][:, :, :].rearrange("p a c -> p (a c)")
        v.scalar_tensor_tensor(flat[:, 0:1024], g.psf[s][:, 0:1024], GK ** -0.5, g.pr[s][:, 1024:2048], ALU.mult, ALU.mult)
        v.tensor_tensor(flat[:, 1024:2048], g.psf[s][:, 1024:2048], g.pr[s][:, 0:1024], ALU.mult).then_inc(g.l_qk_ready, 1)
        yield
        v.wait_ge(g.l_scores_done, j)
        v.tensor_tensor(seqs(l2a_scores(g, s)), seqs(g.psf[s][:, 0:1024]),
                        g.c("upper").unsqueeze(1).to_broadcast([P, 16, SEQ]), ALU.mult).then_inc(g.l_scores_ready, 1)
        og = l2a_gate(g, s)
        yield
        v.wait_ge(g.l_sq_ready, j)
        link(v.tensor_tensor(og, g.psf[s], og, ALU.mult))
        link(v.tensor_reduce(g.rm[s][:, 0:16], g.pr[s][:, :].rearrange("p (r e) -> p r e", e=GV), AX.X, ALU.add))
        rsqrt_dve(g, v, link, s, 16, g.rm[s][:, 0:16], 1e-5, 1.0 / GV)
        og3 = og.rearrange("p (r e) -> p r e", e=GV)
        v.tensor_tensor(og3, og3, g.rs[s][:, 0:16].unsqueeze(2).to_broadcast([P, 16, GV]), ALU.mult).then_inc(g.l_og_ready, 1)
        yield
        v.wait_ge(g.l_og_turned, j)
        v.tensor_copy(g.qk[s][:, 2:4, :], g.ps[s][:, 2:4, :]).then_inc(g.l_ogT_ready_v, 1)
        yield
        v.wait_ge(g.l_out_done, j)
        h = g.h[:, bass.ds(t * GT, GT), :]
        v.tensor_tensor(h, g.ps[s][:, 3, :].rearrange("p (t d) -> p t d", d=D), h, ALU.add).then_inc(g.slot_free, 1)
        link.end()

    pairs(v, g.groups, group)


STEPS = TOK
CH = 8
FACTOR = CH ** 3 + CH ** 2 + CH + 1
CHUNKS = [(c * P, min(P, FACTOR - c * P)) for c in range((FACTOR + P - 1) // P)]
TOK_COLS = {"w": (0, len(CHUNKS) * CH * D), "b": (len(CHUNKS) * CH * D, D)}
TOK_WIDTH = TOK_COLS["b"][0] + D
FACTOR_LINKS, TOK_LINKS = 5, 5 + CH - 1
TOK_CHUNK = 9


def steps_loop(eng, body):
    with eng.Fori(0, STEPS // 2) as i:
        body(i * 2, 0, True)
        body(i * 2 + 1, 1, True)
    body(STEPS - 1, 0, False)


def factor_sb(g, s):
    return g.qk[s][:, :, :].rearrange("p a c -> p (a c)")[:, 0:FACTOR]


def tok_pe(g, pe):
    at, n = TOK_COLS["w"]
    w = g.w_big[:, at:at + n].rearrange("p (k c) -> p k c", k=len(CHUNKS))

    def turn(t, s):
        pe.wait_ge(g.factor_ready, t + 1)
        for k, (at, rows) in enumerate(CHUNKS):
            ins = pe.transpose(g.psf[s][0:rows, k * P:(k + 1) * P], factor_sb(g, s)[:, at:at + rows], g.c("ident"))
        ins.then_inc(g.factor_turned, 1)

    def step(t, s, following):
        if following:
            turn(t + 1, 1 - s)
        pe.wait_ge(g.factorT_ready, t + 1)
        pe.wait_ge(g.token_ready, t + 1)
        for k, (at, rows) in enumerate(CHUNKS):
            for half in range(2):
                ins = pe.matmul(g.ps[s][:, 2 + half, :], g.pr[s][0:rows, k * P:(k + 1) * P],
                                w[0:rows, k, half * 512:(half + 1) * 512], start=(k == 0), stop=(k == len(CHUNKS) - 1))
        ins.then_inc(g.product_done, 1)

    turn(0, 0)
    steps_loop(pe, step)


def tok_act(g, a):
    last = CHUNKS[-1][1]

    def step(t, s, following):
        full = (len(CHUNKS) - 1) * P
        a.wait_ge(g.factor_turned, t + 1)
        a.activation(g.pr[s][:, 0:full], g.psf[s][:, 0:full], ACT.Copy)
        a.activation(g.pr[s][0:last, full:full + P], g.psf[s][0:last, full:full + P], ACT.Copy).then_inc(g.factorT_ready, 1)

    steps_loop(a, step)


def tok_dve(g, v):
    x = g.t2[0][:, :, :].rearrange("p t d -> p (t d)")
    parts = {1: g.t2[1][:, :, :].rearrange("p t d -> p (t d)"), 2: g.xT[0][:, :], 3: g.xT[1][:, :],
             4: g.xn[0][:, :, :].rearrange("p t d -> p (t d)")}
    s1, s2, s3 = g.small[0][:, 0:CH], g.small[0][:, CH:CH + CH ** 2], g.oT[0][:, :]
    n = STEPS * CH
    start = Link(v, g.moe_link, 0, 4)
    start.group(0)
    v.wait_ge(g.x_loaded, 16)
    v.sem_inc(g.token_ready, 2)
    start(v.tensor_tensor(parts[1][:, 0:n], x[:, CH:CH + n], x[:, 0:n], ALU.subtract))
    for k in range(2, 5):
        ins = v.tensor_scalar(parts[k][:, 0:n], parts[1][:, 0:n], 1.0 / k, None, ALU.mult)
    start(ins)
    v.memset(s1, 0.0)
    v.memset(s2, 0.0)
    start(v.memset(s3, 0.0))
    for s in range(SLOTS):
        v.memset(factor_sb(g, s)[:, FACTOR - 1:FACTOR], 1.0)
    b0, bn = TOK_COLS["b"]
    start(v.tensor_copy(g.a[:, 0, :], g.w_big[:, b0:b0 + bn]))
    a1, b1 = g.small[1][:, 0:CH], g.small[1][:, CH:2 * CH]
    a2, n2 = g.small[1][:, 16:80], g.small[1][:, 80:144]
    b2 = g.small[1][:, 144:208]
    a3, n3 = g.oT[1][:, :], g.xn[1][:, :, :].rearrange("p t d -> p (t d)")

    def outer(out, left, right, size):
        return v.tensor_tensor(out.rearrange("p (i c) -> p i c", c=CH), left.unsqueeze(2).to_broadcast([P, size, CH]),
                               right.unsqueeze(1).to_broadcast([P, size, CH]), ALU.mult)

    def factors(t, s, link):
        vec = {k: parts[k][:, bass.ds(t * CH, CH)] for k in parts}
        f = factor_sb(g, s)
        m, b, c1 = f[:, 0:512], f[:, 512:576], f[:, 576:584]
        v.tensor_tensor(a1, s1, vec[4], ALU.add)
        v.tensor_tensor(b1, s1, vec[3], ALU.add)
        link(v.tensor_tensor(c1, s1, vec[2], ALU.add))
        outer(a2, a1, vec[3], CH)
        outer(b2, b1, vec[2], CH)
        outer(n2, c1, vec[1], CH)
        link(v.tensor_tensor(s1, s1, vec[1], ALU.add))
        v.tensor_tensor(a2, a2, s2, ALU.add)
        link(v.tensor_tensor(b, b2, s2, ALU.add))
        v.tensor_tensor(s2, s2, n2, ALU.add)
        outer(n3, b, vec[1], CH ** 2)
        link(outer(a3, a2, vec[2], CH ** 2))
        v.tensor_tensor(m, a3, s3, ALU.add).then_inc(g.factor_ready, 1)
        link(v.tensor_tensor(s3, s3, n3, ALU.add))

    def combine(t, s, link):
        token = g.a[:, bass.ds(t + 1, 1), :]
        v.wait_ge(g.token_ready, t + 2)
        v.wait_ge(g.product_done, t + 1)
        for c in range(CH):
            before = g.a[:, bass.ds(t, 1), :] if c == 0 else token
            ins = v.scalar_tensor_tensor(token, g.ps[s][:, 2 + c // 4:3 + c // 4, (c % 4) * D:(c % 4 + 1) * D],
                                         parts[1][:, bass.ds(t * CH + c, 1)], before, ALU.mult, ALU.add)
            if c < CH - 1:
                link(ins)
        ins.then_inc(g.token_ready, 1)

    first = Link(v, g.moe_link, 4, FACTOR_LINKS)
    first.group(0)
    factors(0, 0, first)
    link = Link(v, g.moe_link, 4 + FACTOR_LINKS, TOK_LINKS)

    def step(t, s, following):
        link.group(t)
        if following:
            factors(t + 1, 1 - s, link)
        combine(t, s, link)

    steps_loop(v, step)

PE = {"TOK": tok_pe, **{st: moe_pe(st) for st in MOE}, "L0A": l0a_pe, "L2A": l2a_pe, "L1A": l1a_pe, "L2F": l2f_pe, "L3A": l3a_pe, "L3F": l3f_pe}
ACTS = {"TOK": tok_act, **{st: moe_act(st) for st in MOE}, "L0A": l0a_act, "L2A": l2a_act, "L1A": l1a_act, "L2F": l2f_act, "L3A": l3a_act, "L3F": l3f_act}
DVE = {"TOK": tok_dve, **{st: moe_dve(st) for st in MOE}, "L0A": l0a_dve, "L2A": l2a_dve, "L1A": l1a_dve, "L2F": l2f_dve, "L3A": l3a_dve, "L3F": l3f_dve}


def more_semaphores(g, sem):
    (g.m_down_done, g.m_latent_ready, g.m_latent_turned, g.m_latentT_ready, g.m_q_done, g.m_q_ready, g.m_k_done,
     g.m_k_ready, g.m_v_done, g.m_v_ready) = (sem("m_" + n) for n in (
         "down_done", "latent_ready", "latent_turned", "latentT_ready", "q_done", "q_ready", "k_done", "k_ready",
         "v_done", "v_ready"))
    (g.f_conv_ready, g.f_qk_done, g.f_q_ready, g.f_k_ready, g.f_v_done, g.f_v_ready, g.f_exp_ready) = (
        sem("f_" + n) for n in ("conv_ready", "qk_done", "q_ready", "k_ready", "v_done", "v_ready", "exp_ready"))
    g.w_qk_done, g.w_q_ready, g.w_k_ready, g.w_v_done, g.w_v_ready = (
        sem("w_" + n) for n in ("qk_done", "q_ready", "k_ready", "v_done", "v_ready"))
    g.p_q_done, g.p_k_done, g.p_q_ready, g.p_k_ready, g.p_v_done, g.p_v_ready = (
        sem("p_" + n) for n in ("q_done", "k_done", "q_ready", "k_ready", "v_done", "v_ready"))
    g.moe = moe_semaphores(sem, [st for st in g.stages if st in MOE])
    (g.l_low_done, g.l_low_ready, g.l_gk_done, g.l_gk_read, g.l_log_ready, g.l_sum_ready, g.l_neg_exp, g.l_exp_ready, g.l_inverse_ready, g.l_qk_done,
     g.l_qk_ready, g.l_v_done, g.l_v_ready, g.l_g_done, g.l_silu_ready, g.l_scores_done, g.l_scores_ready, g.l_o_done,
     g.l_sq_ready, g.l_og_ready, g.l_og_turned, g.l_ogT_ready_a, g.l_ogT_ready_v, g.l_out_done, g.l_fold) = (
         sem("l_" + n) for n in (
             "low_done", "low_ready", "gk_done", "gk_read", "log_ready", "sum_ready", "neg_exp", "exp_ready", "inverse_ready", "qk_done", "qk_ready",
             "v_done", "v_ready", "g_done", "silu_ready", "scores_done", "scores_ready", "o_done", "sq_ready", "og_ready",
             "og_turned", "ogT_ready_a", "ogT_ready_v", "out_done", "fold"))
    g.lora_pe, g.lora_dve = sem("lora_pe"), sem("lora_dve")



def audio_tower_kernel(nc, ins, out, batch):
    g = Net()
    stages = STAGES
    g.groups = batch * SEQ // GTOK
    tiles = g.groups * GT
    with ExitStack() as ctx:
        def sb(name, shape):
            return ctx.enter_context(nc.sbuf_tensor(name, shape, F32))

        def sem(name):
            return ctx.enter_context(nc.semaphore(name))

        g.h = sb("h", [P, tiles, D])
        g.a = sb("a", [P, max(tiles, 32), D])
        consts, n_const = columns("const")
        const_sb = sb("const_sb", [P, n_const])
        widths = [columns(st)[1] for st in ATTN_STAGES]
        w_attn = [sb(f"w_attn{i}", [P, max(widths[i::2])]) for i in range(2)]
        g.w_big = sb("w_big", [P, W_BIG])
        g.cs = sb("cs", [P, D])

        def slots(name, shape):
            return [sb(f"{name}{s}", shape) for s in range(SLOTS)]

        g.xn, g.xT = slots("xn", [P, GT, D]), slots("xT", [P, GTOK])
        g.qk, g.v2 = slots("qk", [P, 4, GTOK]), slots("v2", [P, 2 * GT, 4, DH + 1])
        g.pr, g.pt = slots("pr", [P, 4 * GTOK]), slots("pt", [P, 4 * GTOK])
        g.o, g.oT, g.t2 = slots("o", [P, GT, D]), slots("oT", [P, GTOK]), slots("t2", [P, GT, D])
        g.of = [g.o[s][:, :, :].rearrange("p t d -> p (t d)") for s in range(SLOTS)]
        g.stats, g.mv = slots("stats", [P, 16, 6]), slots("mv", [P, 16, 2])
        g.ra, g.rs, g.rq, g.rm = (slots(n, [P, 32]) for n in ("ra", "rs", "rq", "rm"))
        g.scores_sb = slots("scores_sb", [P, 1024])
        g.small, g.gates = slots("small", [P, 256]), slots("gates", [P, GT * EXPERTS])

        g.ps = [ctx.enter_context(nc.psum_tensor(f"ps{s}", [P, 4, 512], F32)) for s in range(SLOTS)]
        g.psf = [g.ps[s][:, :, :].rearrange("p b c -> p (b c)") for s in range(SLOTS)]

        def c(name):
            at, n = consts[name]
            return const_sb[:, at:at + n]

        def w(stage, name):
            cols, _ = columns(stage)
            at, n = cols[name]
            return w_attn[ATTN_STAGES.index(stage) % 2][:, at:at + n]

        def heads(s):
            return g.ps[s][:, 0:2, 0:16 * (DH + 1)].rearrange("p a (b e) -> p a b e", e=DH + 1)

        g.c, g.w, g.heads = c, w, heads
        grouped = [st for st in stages if st != "TOK"]
        g.n0 = {st: i * g.groups for i, st in enumerate(grouped)}
        soft = [st for st in stages if st in ("L0A", "L1A", "L2F", "L3A", "L3F")]
        g.k0 = {st: i * g.groups for i, st in enumerate(soft)}
        g.uncentred = g.groups
        moes = [st for st in stages if st in MOE]
        g.m0 = {st: i * g.groups for i, st in enumerate(moes)}
        g.stages = stages
        g.link0 = {}
        at_slot, at_moe = 0, 4 + STEPS * TOK_LINKS
        for st in grouped:
            if st in MOE:
                g.link0[st] = at_moe
                at_moe += g.groups * MOE[st].links
            else:
                g.link0[st] = at_slot
                at_slot += g.groups // SLOTS * LINKS[st]

        g.const_loaded, g.h_zero, g.h_loaded, g.v2_ones = sem("const_loaded"), sem("h_zero"), sem("h_loaded"), sem("v2_ones")
        g.attn_loaded, g.big_loaded = [sem(f"attn_loaded{i}") for i in range(2)], sem("big_loaded")
        g.slot_free, g.xn_ready, g.xn_transposed, g.xT_ready = (sem(n) for n in (
            "slot_free", "xn_ready", "xn_transposed", "xT_ready"))
        g.slot_link, g.moe_link = [sem(f"slot_link{s}") for s in range(SLOTS)], sem("moe_link")
        g.out_stored = sem("out_stored")
        g.r_qk_done, g.r_q_ready, g.r_k_ready, g.r_v_done, g.r_g_done, g.r_g_ready, g.r_silu_ready = (
            sem("r_" + n) for n in ("qk_done", "q_ready", "k_ready", "v_done", "g_done", "g_ready", "silu_ready"))
        g.r_x1_ready, g.r_x1_turned, g.r_x1T_ready = (sem("r_" + n) for n in ("x1_ready", "x1_turned", "x1T_ready"))
        g.r_fc1_done, g.r_gelu_ready, g.r_z_ready, g.r_fc2_done = (
            sem("r_" + n) for n in ("fc1_done", "gelu_ready", "z_ready", "fc2_done"))
        g.fold_dve, g.fold_pe = sem("fold_dve"), sem("fold_pe")
        g.scores_done, g.centred_ready, g.probs_ready, g.probs_turned, g.pt_ready_a, g.pt_ready_v, g.values_weighed = (
            sem(n) for n in ("scores_done", "centred_ready", "probs_ready", "probs_turned", "pt_ready_a", "pt_ready_v",
                             "values_weighed"))
        g.o_ready, g.o_turned, g.oT_ready, g.out_done = (sem(n) for n in ("o_ready", "o_turned", "oT_ready", "out_done"))
        more_semaphores(g, sem)
        g.wait_carrier = sem("wait_carrier")
        g.x_loaded, g.factor_ready, g.factor_turned, g.factorT_ready, g.product_done, g.token_ready, g.tokens_stored = (
            sem(n) for n in ("x_loaded", "factor_ready", "factor_turned", "factorT_ready", "product_done", "token_ready",
                             "tokens_stored"))
        g.tokens = nc.dram_tensor("tokens", (batch, TOK, D), F32, kind="Internal").ap()

        h_rows = lambda dram: dram.rearrange("(t q) s d -> q s t d", q=2)
        block = ctx.enter_context(nc.Block())

        @block.sync
        def _(sp):
            through = lambda st: SLOTS + g.n0[st] + g.groups

            def load_weights(st):
                if st in ATTN_STAGES:
                    same = [e for e in grouped if e in ATTN_STAGES
                            and ATTN_STAGES.index(e) % 2 == ATTN_STAGES.index(st) % 2]
                    region, loaded = w_attn[ATTN_STAGES.index(st) % 2], g.attn_loaded[ATTN_STAGES.index(st) % 2]
                else:
                    same = [e for e in grouped if e not in ATTN_STAGES]
                    region, loaded = g.w_big, g.big_loaded
                before = same[:same.index(st)] if st in same else []
                if before:
                    sp.wait_ge(g.slot_free, through(before[-1]))
                elif st in MOE:
                    sp.wait_ge(g.token_ready, STEPS + 2)
                sp.dma_start(region[:, 0:ins[st].shape[1]], ins[st]).then_inc(loaded, 16)

            sp.dma_start(g.t2[0][:, :, :].rearrange("p t d -> p (t d)"), ins["x"]).then_inc(g.x_loaded, 16)
            sp.dma_start(const_sb[:, :], ins["const"]).then_inc(g.const_loaded, 16)
            load_weights("TOK")
            load_weights(grouped[0])
            sp.wait_ge(g.h_zero, 1)
            for c in range(STEPS // TOK_CHUNK):
                steps = slice(c * TOK_CHUNK, (c + 1) * TOK_CHUNK)
                sp.wait_ge(g.token_ready, (c + 1) * TOK_CHUNK + 2)
                sp.dma_start(g.tokens[:, steps, :], g.a[:, c * TOK_CHUNK + 1:(c + 1) * TOK_CHUNK + 1, :])\
                  .then_inc(g.tokens_stored, 16)
                sp.wait_ge(g.tokens_stored, 16 * (c + 1))
                for q in range(2):
                    sp.dma_start(g.h[64 * q + c * TOK_CHUNK:64 * q + (c + 1) * TOK_CHUNK, :, :],
                                 h_rows(g.tokens)[q][steps, :, :]).then_inc(g.h_loaded, 16)
            for st in grouped[1:]:
                load_weights(st)
            for part in range(g.groups // 2):
                sp.wait_ge(g.slot_free, SLOTS + g.n0[grouped[-1]] + 2 * (part + 1))
                for q in range(2):
                    rows = slice(2 * part * GT, 2 * (part + 1) * GT)
                    sp.dma_start(h_rows(out)[q][:, rows, :], g.h[64 * q:64 * q + TOK, rows, :]).then_inc(g.out_stored, 16)
            sp.wait_ge(g.out_stored, 16 * g.groups)

        def wait_weights(eng, st):
            if st in ATTN_STAGES:
                i = ATTN_STAGES.index(st) % 2
                eng.wait_ge(g.attn_loaded[i], 16 * (1 + len([e for e in stages[:stages.index(st)] if e in ATTN_STAGES[i::2]])))
            else:
                eng.wait_ge(g.big_loaded, 16 * (1 + len([e for e in stages[:stages.index(st)] if e not in ATTN_STAGES])))

        @block.gpsimd
        def _(pool):
            pool.memset(g.h[:, :, :], 0.0).then_inc(g.h_zero, 1)
            for s in range(SLOTS):
                ins_ = pool.memset(g.v2[s][:, :, :, DH], 1.0)
            ins_.then_inc(g.v2_ones, 1)

        @block.tensor
        def _(pe):
            pe.wait_ge(g.const_loaded, 16)
            pe.wait_ge(g.v2_ones, 1)
            for st in stages:
                wait_weights(pe, st)
                PE[st](g, pe)

        @block.scalar
        def _(a):
            a.wait_ge(g.const_loaded, 16)
            for st in stages:
                wait_weights(a, st)
                ACTS[st](g, a)

        @block.vector
        def _(v):
            v.wait_ge(g.const_loaded, 16)
            v.memset(g.rm[0][:, :], 0.0).then_inc(g.slot_free, SLOTS)
            for st in stages:
                wait_weights(v, st)
                if st == grouped[0]:
                    v.wait_ge(g.h_loaded, 32 * (STEPS // TOK_CHUNK))
                DVE[st](g, v)



def host_more(X, arrays, pack, row, col, pad_heads, swap_pairs):
    import numpy as np
    f32 = np.float32
    W = X["L0_tok_W"]
    w = np.zeros((P, len(CHUNKS), CH, D), f32)
    at = 0
    levels = []
    for size in (1, CH, CH ** 2, CH ** 3):
        levels.append(W[:, at:at + size * CH].reshape(D, size, CH).transpose(1, 2, 0))
        at += size * CH
    rows = np.concatenate(levels[::-1])
    for k, (lo, n) in enumerate(CHUNKS):
        w[:n, k] = rows[lo:lo + n]
    arrays["TOK"] = np.concatenate([w.reshape(P, -1), row(X["L0_tok_b"])], 1)
    x = np.zeros((P, SEQ, CH), f32)
    x[:, :, 0] = np.linspace(0.0, 1.0, SEQ, dtype=f32)
    x[:, :, 1:] = X["x"]
    arrays["x"] = x.reshape(P, -1)
    L = lambda n: X["L1_attn_" + n]
    rope = lambda wt: pad_heads(wt, 2, DH)
    arrays["L1A"] = pack("L1A", {
        "down": np.concatenate([L("W_dq"), L("W_dkv")], 1),
        "qa": merge(pad_heads(L("W_uq")), rope(L("W_qr")), DH, 2), "qb": rope(swap_pairs(L("W_qr"))),
        "kn": pad_heads(L("W_ukv")[:, :D]), "ka": rope(L("W_kr")), "kb": rope(swap_pairs(L("W_kr"))),
        "v": L("W_ukv")[:, D:], "wo": L("W_o").T, "qg": L("q_ln_g")[:, None], "qbias": L("q_ln_b")[:, None],
        "kg": L("kv_ln_g")[:, None], "kbias": L("kv_ln_b")[:, None]})
    L = lambda n: X["L2_attn_" + n]
    arrays["L2A"] = pack("L2A", {
        "qk": np.concatenate([L("Wq"), L("Wk")], 1), "gk1": L("Wgk1"), "gk2": L("Wgk2"),
        "gkb": L("bgk2").reshape(2, P).T, "v": L("Wv"), "g": L("Wg"),
        "wo": L("Wo").reshape(GH, GV, D).transpose(1, 0, 2), "rms": L("rms_w")[:, None]})
    L = lambda n: X["L2_ffn_" + n]
    wq, wk, wv = (L("qkv_w")[i * D:(i + 1) * D].T for i in range(3))
    bq, bk, bv = (L("qkv_b")[i * D:(i + 1) * D] for i in range(3))
    arrays["L2F"] = pack("L2F", {
        "qk": np.concatenate([pad_heads(wq), pad_heads(wk)], 1), "v": wv, "wo": L("wo_w").T,
        "conv": L("pos_w")[:, 0, :], "convb": L("pos_b")[:, None],
        "qkb": np.concatenate([pad_heads(bq[None]).reshape(2, P), pad_heads(bk[None]).reshape(2, P)]).T,
        "bv": bv[:, None], "bo": row(L("wo_b"))})
    L = lambda n: X["L3_attn_" + n]
    third = lambda wt, i: wt[:, i * D:(i + 1) * D]
    heads = lambda wt: np.concatenate([pad_heads(third(wt, 0)), pad_heads(third(wt, 1))], 1)
    arrays["L3A"] = pack("L3A", {
        "qk": heads(L("w_qkv")), "v": third(L("w_qkv"), 2), "wo": L("w_out"), "la": L("lora_A_qkv").T,
        "lbqk": heads(L("lora_B_qkv")), "lbv": third(L("lora_B_qkv"), 2), "loa": L("lora_A_out").T,
        "lob": L("lora_B_out"), "bo": row(L("b_out"))})
    L = lambda n: X["L3_ffn_" + n]
    arrays["L3F"] = pack("L3F", {
        "qk": np.concatenate([pad_heads(L("wq")), pad_heads(L("wk"))], 1),
        "qkr": np.concatenate([pad_heads(swap_pairs(L("wq"))), pad_heads(swap_pairs(L("wk")))], 1),
        "v": L("wv"), "wo": L("wo"), "nw": L("attn_norm_w")[:, None]})
    by_rows = lambda a: a.reshape(EXPERTS, -1, P, a.shape[-1]).transpose(2, 0, 1, 3)
    biases = lambda a: a.reshape(-1, P).T

    def mixture(stage, parts):
        m = MOE[stage]
        a = np.zeros((P, m.width), f32)
        for name, (at, n) in m.cols.items():
            part = parts[name].reshape(parts[name].shape[0], -1)
            assert part.shape[1] == n, (name, part.shape, n)
            a[:part.shape[0], at:at + n] = part
        arrays[stage] = a

    L = lambda n: X["L0_ffn_" + n]
    mixture("L0M", {"up": by_rows(L("gate_up_proj")), "down": by_rows(L("down_proj")), "router": L("router_w"),
                    "rb": row(L("router_b")), "ub": biases(L("gate_up_proj_bias")), "db": L("down_proj_bias"),
                    "sb": biases(L("gate_up_proj_bias"))})
    L = lambda n: X["L1_ffn_" + n]
    mixture("L1M", {"up": by_rows(L("w1")), "down": by_rows(L("w2")), "router": L("gate_w"), "rb": row(L("gate_b")),
                    "ub": biases(L("b1")), "db": L("b2")})
    L = lambda n: X["L3_ffn_" + n]
    mixture("L3M", {"up": by_rows(L("w1")), "down": by_rows(L("w2")), "router": L("router_w"),
                    "nw": L("ffn_norm_w")[:, None]})


def merge(base, other, at, width):
    a = base.reshape(base.shape[0], HEADS, 32).copy()
    a[:, :, at:at + width] = other.reshape(base.shape[0], HEADS, 32)[:, :, at:at + width]
    return a.reshape(base.shape)


def host_arrays(X):
    import numpy as np
    f32 = np.float32

    def pack(stage, parts):
        cols, total = columns(stage)
        assert set(parts) == set(cols), set(parts) ^ set(cols)
        a = np.zeros((P, total), f32)
        for name, part in parts.items():
            at, n = cols[name]
            part = np.asarray(part)
            part = part.reshape(part.shape[0], -1)
            assert part.shape[1] == n and part.shape[0] <= P, (stage, name, part.shape)
            a[:part.shape[0], at:at + n] = part
        return a

    def row(vec):
        return np.broadcast_to(vec, (P, vec.shape[0]))

    def pad_heads(wt, width=DH, at=0):
        a = np.zeros((wt.shape[0], 2, 4, 32), f32)
        a[..., at:at + width] = wt.reshape(wt.shape[0], 2, 4, width)
        return a.reshape(wt.shape[0], 2 * P)

    def swap_pairs(wt):
        return wt.reshape(wt.shape[0], -1, 2)[:, :, ::-1].reshape(wt.shape)

    arrays = {}
    i = np.arange(SEQ)
    diff = (i[:, None] - i[None, :]).astype(f32)
    decay = np.log(1.0 - 2.0 ** (-5.0 - np.arange(HEADS))).astype(f32)
    dm = np.where(diff[None] >= 0, np.exp(diff[None] * decay[:, None, None]), 0.0)
    dm = (dm / np.sqrt(dm[:, :, :TOK].sum(-1, keepdims=True))).astype(f32)
    causal = np.where(diff >= 0, 0.0, NEG).astype(f32)
    keys = np.broadcast_to(np.where(i < TOK, 0.0, NEG).astype(f32), (SEQ, SEQ))
    ang = i.astype(f32)
    mc, ms = np.ones((P, SEQ), f32), np.zeros((P, SEQ), f32)
    rc, rsn = np.zeros((P, SEQ), f32), np.zeros((P, SEQ), f32)
    for r in range(4):
        for e in range(2):
            mc[32 * r + DH + e] = np.cos(ang)
            ms[32 * r + DH + e] = np.sin(ang) * (-1 if e == 0 else 1)
        for m in range(DH):
            a_m = ang * f32(1.0 / 10000.0 ** ((m - m % 2) / DH))
            rc[32 * r + m] = np.cos(a_m)
            rsn[32 * r + m] = np.sin(a_m) * (-1 if m % 2 == 0 else 1)
    restart = np.ones((P, GTOK), f32)
    restart[:, ::SEQ] = 0.0
    two = lambda t: np.concatenate([t, t], 0)
    arrays["const"] = pack("const", {
        "ident": np.eye(P, dtype=f32), "ones": np.ones((P, P), f32),
        "dm": two(dm.reshape(2, 4, SEQ, SEQ).transpose(2, 1, 0, 3).reshape(SEQ, HEADS * SEQ)), "causal": two(causal), "keys": two(keys),
        "upper": two((diff.T >= 0).astype(f32)), "restart": restart,
        "mla_cos": mc, "mla_sin": ms, "rope_cos": rc, "rope_sin": rsn})
    col = lambda vec: vec.reshape(-1, P).T
    L = lambda n: X["L0_attn_" + n]
    bv = np.zeros((2, 64, 64), f32)
    bv[:] = L("bv").reshape(2, 1, 64)
    fc2 = np.ones((P, 4, 129), f32)
    fc2[:, :, :D] = L("fc2_w").T.reshape(4, P, D).transpose(1, 0, 2)
    arrays["L0A"] = pack("L0A", {
        "qk": np.concatenate([pad_heads(L("wq").T), pad_heads(L("wk").T)], 1), "v": L("wv").T,
        "g": L("wg").T, "wo": L("wo").T, "fc1": L("fc1_w").T, "fc2": fc2,
        "qkb": np.concatenate([pad_heads(L("bq")[None]).reshape(2, P), pad_heads(L("bk")[None]).reshape(2, P)]).T,
        "bv": bv.reshape(P, 64), "bg": row(L("bg")), "bo": row(L("bo")), "n0g": row(L("n0_g")), "n0b": row(L("n0_b")),
        "n1g": row(L("n1_g")), "n1b": row(L("n1_b")), "fc1b": col(L("fc1_b")), "fc2b": row(L("fc2_b")),
        "fg": col(L("ln_ffn_g")), "fb": col(L("ln_ffn_b"))})
    host_more(X, arrays, pack, row, col, pad_heads, swap_pairs)
    return arrays


STAGES = ("TOK", "L0A", "L0M", "L1A", "L1M", "L2A", "L2F", "L3A", "L3F", "L3M")


def kernel(**inputs):
    import numpy as np
    import concourse.bacc as bacc
    from concourse.bass_utils import run_bass_kernel_spmd

    nc = bacc.Bacc("TRN2", target_bir_lowering=False, num_devices=1)
    arrays = {name: np.ascontiguousarray(a) for name, a in host_arrays({k: np.asarray(v) for k, v in inputs.items()}).items()}
    batch = inputs["x"].shape[0]
    ins = {name: nc.dram_tensor("in_" + name, a.shape, mybir.dt.from_np(a.dtype), kind="ExternalInput").ap()
           for name, a in arrays.items()}
    out = nc.dram_tensor("out", (batch, TOK, D), F32, kind="ExternalOutput").ap()
    audio_tower_kernel(nc, ins, out, batch)
    return run_bass_kernel_spmd(nc, [{"in_" + name: a for name, a in arrays.items()}], core_ids=[0]).results[0]["out"]
```

```python
from contextlib import ExitStack

import concourse.bass as bass
from concourse import mybir

ALU = mybir.AluOpType
ACT = mybir.ActivationFunctionType
AX = mybir.AxisListType
F32 = mybir.dt.float32
I32 = mybir.dt.int32

P = 128
D = 128
HEADS = 8
DH = D // HEADS
TOK = 63
SEQ = 64
GT = 4
GTOK = GT * P
SLOTS = 2
EXPERTS = 8
NEG = -3.0e38
PICKED = -3.3e38
FFN = 4 * D
QP, KVP = 64, 85
GH, GK, GV, GR = 4, 64, 128, 16

LAYOUT = {
    "const": [("ident", P), ("ones", P), ("dm", HEADS * SEQ), ("causal", SEQ), ("upper", SEQ), ("live", 1),
              ("restart", GTOK), ("mla_q", SEQ), ("mla_k", SEQ), ("rope_cos", SEQ), ("rope_sin", SEQ), ("rope_k", SEQ)],
    "L0A": [("qk", 4 * D), ("v", D), ("g", D), ("wo", D), ("fc1", FFN), ("fc2", 4 * 129), ("qkb", 4), ("bv", 64),
            ("bg", D), ("bo", D), ("n0g", D), ("n0b", D), ("n1g", D), ("n1b", D), ("fc1b", 4), ("fc2b", D),
            ("fg", 4), ("fb", 4)],
    "L1A": [("down", QP + KVP), ("q", 2 * D), ("kn", 2 * D), ("kr", 2 * D), ("v", D),
            ("wo", D), ("qg", 1), ("qbias", 1), ("kg", 1), ("kbias", 1)],
    "L2A": [("qk", 4 * D), ("gk1", GR), ("gk2", 2 * D), ("gkb", 2), ("v", GH * GV), ("g", GH * GV), ("wo", GH * D),
            ("rms", 1)],
    "L2F": [("qk", 4 * D), ("v", D), ("wo", D), ("conv", 3), ("convb", 1), ("qkb", 4), ("bv", 1), ("bo", D)],
    "L3A": [("qk", 4 * D), ("v", D), ("wo", D), ("la", D), ("lbqk", 4 * D), ("lbv", D), ("loa", D), ("lob", D),
            ("bo", D)],
    "L3F": [("qk", 4 * D), ("qr", 2 * D), ("v", D), ("wo", D), ("nw", 1)],
}
LINKS = {"L0A": 90, "L1A": 31, "L2A": 31, "L2F": 24, "L3A": 18, "L3F": 36}
SCHEDULE = {
    "L0A": (22, "01101000000111101001010110100101001011100101011101"),
    "L1A": (7, "1000110110001110101101110111010100100011000100"),
    "L2A": (19, "0101000010100100100011111010101011010111101011001100"),
    "L2F": (14, "1010101100101010110101110010010101000101"),
    "L3A": (7, "01000101010101001101011010110011001011"),
    "L3F": (8, "011010101011010011011110110100011010010000"),
}
ATTN_STAGES = ("L0A", "L1A", "L2A", "L2F", "L3A", "L3F")


def columns(stage):
    at, out = 0, {}
    for name, n in LAYOUT[stage]:
        out[name] = (at, n)
        at += n
    return out, at


class Net:
    pass


class Link:

    def __init__(self, eng, sem, base, per_group):
        self.eng, self.sem, self.base, self.per_group, self.k = eng, sem, base, per_group, 0

    def group(self, t):
        self.first = self.base + t * self.per_group
        if self.k == self.per_group:
            self.k = 0

    def __call__(self, ins, own=None):
        self.k += 1
        ins.then_inc(self.sem, 1)
        self.eng.wait_ge(self.sem, self.first + self.k)
        if own is not None:
            self.eng.sem_inc(own, 1)

    def later(self, ins):
        self.k += 1
        ins.then_inc(self.sem, 1)
        awaited = self.first + self.k
        yield
        self.eng.wait_ge(self.sem, awaited)

    def end(self):
        assert self.k == self.per_group, ("links in a group:", self.k)


def slot_links(eng, sems, base, per_group):
    return [Link(eng, sems[s], base, per_group) for s in range(SLOTS)]


def pairs(g, eng, body, cut, order):
    groups, levels = g.groups, order.count("0")

    def turn(i, step0, before, first, last):
        level0, level1, after = 0, cut, None
        rest, parts = last - first, levels - cut
        for slot in order:
            if slot == "0":
                step0(level0)
                level0 += 1
                continue
            if level1 < levels:
                part = level1 - cut
                for level in range(first + part * rest // parts, first + (part + 1) * rest // parts):
                    before(level)
            else:
                if after is None:
                    after = body(i * SLOTS + 1, 1, i)
                after(level1 - levels)
            level1 += 1

    before, first, last = g.tails.pop(eng, (None, 0, 0))
    turn(0, body(0, 0, 0), before, first, last)
    if groups > SLOTS:
        with eng.Fori(1, groups // SLOTS) as i:
            before = body(i * SLOTS - 1, 1, i - 1)
            turn(i, body(i * SLOTS, 0, i), before, cut, levels)
    g.tails[eng] = (body(groups - 1, 1, groups // SLOTS - 1), cut, levels)


def end_tail(g, eng):
    step, first, last = g.tails.pop(eng, (None, 0, 0))
    for level in range(first, last):
        step(level)



RSQRT_LINKS = 12


def rsqrt_steps(g, v, link, s, width, src, eps, scale=1.0):
    a, y, q = g.ra[s][:, 0:width], g.rs[s][:, 0:width], g.rq[s][:, 0:width]
    yield from link.later(v.tensor_scalar(a, src, scale, eps, ALU.mult, ALU.add))
    yield from link.later(v.tensor_scalar(y.bitcast(I32), a.bitcast(I32), 1, None, ALU.arith_shift_right))
    yield from link.later(v.tensor_scalar(y.bitcast(I32), y.bitcast(I32), -1.0, float(0x5F3759DF), ALU.mult, ALU.add))
    for _ in range(3):
        yield from link.later(v.tensor_tensor(q, y, y, ALU.mult))
        yield from link.later(v.scalar_tensor_tensor(q, q, -0.5, a, ALU.mult, ALU.mult))
        yield from link.later(v.scalar_tensor_tensor(y, q, 1.5, y, ALU.add, ALU.mult))


def rsqrt_dve(g, v, link, s, width, src, eps, scale=1.0):
    for _ in rsqrt_steps(g, v, link, s, width, src, eps, scale):
        pass


NORM_LINKS = RSQRT_LINKS + 2


def norm_steps(g, v, link, s, parts, eps):
    for i, part in enumerate(parts):
        ins = v.bn_stats(g.stats[s][:, i, :], part)
    yield from link.later(ins)
    v.sem_inc(g.wait_carrier, 1)
    for i in range(len(parts)):
        ins = v.bn_aggr(g.mv[s][:, i, :], g.stats[s][:, i, :])
    yield from link.later(ins)
    yield from rsqrt_steps(g, v, link, s, len(parts), g.mv[s][:, 0:len(parts), 1], eps)


def norm_dve(g, v, link, s, parts, eps):
    for _ in norm_steps(g, v, link, s, parts, eps):
        pass


def normalise_dve(g, v, s, parts, outs):
    for i, (part, out) in enumerate(zip(parts, outs)):
        ins = v.tensor_scalar(out, part, g.mv[s][:, i, 0:1], g.rs[s][:, i:i + 1], ALU.subtract, ALU.mult)
    return ins


FRONT_LINKS = NORM_LINKS


def front_dve(g, v, link, s, t, n):
    v.wait_ge(g.const_loaded, 16)
    v.wait_ge(g.slot_free, n)
    norm_dve(g, v, link, s, [g.h[:, bass.ds(t * GT + i, 1), :] for i in range(GT)], 1e-5)
    for i in range(GT):
        ins = v.tensor_scalar(g.xn[s][:, i:i + 1, :], g.h[:, bass.ds(t * GT + i, 1), :],
                              g.mv[s][:, i, 0:1], g.rs[s][:, i:i + 1], ALU.subtract, ALU.mult)
    ins.then_inc(g.xn_ready, 1)



def front_pe(g, pe, s, n):
    pe.wait_ge(g.const_loaded, 16)
    pe.wait_ge(g.xn_ready, n)
    for i in range(GT):
        ins = pe.transpose(g.ps[s][:, 0, i * P:(i + 1) * P], g.xn[s][:, i, :], g.c("ident"))
    ins.then_inc(g.xn_transposed, 1)


def front_act(g, a, s, n):
    a.wait_ge(g.xn_transposed, n)
    a.activation(g.xT[s][:, :], g.ps[s][:, 0, :], ACT.Copy).then_inc(g.xT_ready, 1)


def project_qk_pe(g, pe, s, w, first=0, count=4):
    for i in range(first, first + count):
        ins = pe.matmul(g.ps[s][:, i, :], w[:, i * D:(i + 1) * D], g.xT[s][:, :], start=True, stop=True)
    return ins


def values_pe(g, pe, s, w, xT, k=P):
    for q in range(2 * GT):
        for par in range(2):
            ins = pe.matmul(g.ps[s][64 * par:64 * par + 64, 0, q * 64:(q + 1) * 64], xT[0:k, q * SEQ:(q + 1) * SEQ],
                            w[0:k, par * 64:(par + 1) * 64], start=True, stop=True)
    return ins


def scores_pe(g, pe, s):
    for hh in range(2):
        for sq in range(2):
            for tile in range(GT):
                for r in range(4):
                    rows, cols = slice(32 * r, 32 * r + 32), slice(tile * P + sq * SEQ, tile * P + sq * SEQ + SEQ)
                    at = tile * P + hh * SEQ
                    ins = pe.matmul(g.ps[s][64 * sq:64 * sq + 64, r, at:at + SEQ],
                                    g.qk[s][rows, hh, cols], g.qk[s][rows, 2 + hh, cols], start=True, stop=True)
    return ins


def turn_probs_pe(g, pe, s, k):
    for r in range(4):
        if r % 2 == 0:
            pe.wait_ge(g.probs_ready, k * 2 - 1 + r // 2)
        for tile in range(GT):
            c = r * 512 + tile * P
            ins = pe.transpose(g.ps[s][:, r, tile * P:(tile + 1) * P], g.pr[s][:, c:c + P], g.c("ident"))
        if r % 2 == 1:
            ins.then_inc(g.probs_turned, 1)


def weigh_values_pe(g, pe, s):
    for sq in range(2):
        for r in range(4):
            for tile in range(GT):
                c, p = tile * 256 + r * 2 * (DH + 1), r * 512 + tile * P + sq * SEQ
                ins = pe.matmul(g.psf[s][64 * sq:64 * sq + 64, c:c + 2 * (DH + 1)], g.pt[s][:, p:p + SEQ],
                                g.v2[s][:, 2 * tile + sq, r, :, :].rearrange("p a e -> p (a e)"), start=True, stop=True)
    return ins


def turn_out_pe(g, pe, s, src):
    for i in range(GT):
        ins = pe.transpose(g.ps[s][:, 2, i * P:(i + 1) * P], src(i), g.c("ident"))
    return ins


def o_tile(g, s):
    return lambda i: g.o[s][:, i, :]


def project_out_pe(g, pe, s, w):
    for i in range(GT):
        ins = pe.matmul(g.ps[s][:, 3, i * P:(i + 1) * P], g.oT[s][:, i * P:(i + 1) * P], w, start=True, stop=True)
    return ins


ATTEND_LEVELS = 12


def attend_pe(g, pe, s, k, ready, wo, level):
    if level == 0:
        for sem, n in ready:
            pe.wait_ge(sem, n)
        scores_pe(g, pe, s).then_inc(g.scores_done, 1)
    if level == 4:
        turn_probs_pe(g, pe, s, k)
    if level == 6:
        pe.wait_ge(g.pt_ready_a, k)
        pe.wait_ge(g.pt_ready_v, k)
        pe.sem_inc(g.wait_carrier_pe, 1)
        weigh_values_pe(g, pe, s).then_inc(g.values_weighed, 1)
    if level == 8:
        pe.wait_ge(g.o_ready, k)
        turn_out_pe(g, pe, s, o_tile(g, s)).then_inc(g.o_turned, 1)
    if level == 10:
        pe.wait_ge(g.oT_ready, k)
        project_out_pe(g, pe, s, wo).then_inc(g.out_done, 1)


def turned_probs_act(g, a, s, k):
    a.wait_ge(g.probs_turned, k * 2 - 1)
    a.activation(g.pt[s][:, 0:1024], g.psf[s][:, 0:1024], ACT.Copy).then_inc(g.pt_ready_a, 1)


def turned_probs_dve(g, v, s, k):
    v.wait_ge(g.probs_turned, k * 2)
    v.tensor_copy(g.pt[s][:, 1024:2048], g.psf[s][:, 1024:2048]).then_inc(g.pt_ready_v, 1)


def softmax_dve(g, v, link, s, k, scale, mask):
    v.wait_ge(g.scores_done, k)
    rows = g.pr[s].rearrange("p (r j) -> p r j", j=SEQ)
    link(v.scalar_tensor_tensor(rows, g.psf[s].rearrange("p (r j) -> p r j", j=SEQ), scale,
                                mask.unsqueeze(1).to_broadcast([P, 32, SEQ]), ALU.mult, ALU.add))
    link(v.tensor_reduce(g.rm[s][:, 0:32], rows, AX.X, ALU.max))
    for half in (slice(0, 16), slice(16, 32)):
        v.tensor_tensor(rows[:, half, :], rows[:, half, :], g.rm[s][:, half].unsqueeze(2).to_broadcast([P, 16, SEQ]),
                        ALU.subtract).then_inc(g.centred_ready, 1)


SOFTMAX_LINKS = 2


def scale_heads_dve(g, v, s):
    for a in range(2):
        ins = v.tensor_tensor(
            g.o[s][:, :, 64 * a:64 * a + 64].rearrange("p t (r e) -> p t r e", e=DH),
            g.heads(s)[:, :, a::2, 0:DH],
            g.rm[s][:, 0:32].rearrange("p (t b) -> p t b", t=GT)[:, :, a::2].unsqueeze(3).to_broadcast([P, GT, 4, DH]),
            ALU.mult)
    return ins


def divide_dve(g, v, link, s, k):
    v.wait_ge(g.values_weighed, k)
    link(v.reciprocal(g.rm[s][:, 0:32].rearrange("p (t b) -> p t b", t=GT), g.heads(s)[:, :, :, DH]))
    scale_heads_dve(g, v, s).then_inc(g.o_ready, 1)


DIVIDE_LINKS = 1


def add_out_dve(g, v, s, t, k, bias=None, link=None):
    v.wait_ge(g.out_done, k)
    out = g.ps[s][:, 3, :].rearrange("p (t d) -> p t d", d=D)
    if bias is not None:
        link(v.tensor_tensor(g.t2[s][:, :, :], out, bias.unsqueeze(1).to_broadcast([P, GT, D]), ALU.add))
        out = g.t2[s][:, :, :]
    h = g.h[:, bass.ds(t * GT, GT), :]
    v.tensor_tensor(h, out, h, ALU.add).then_inc(g.slot_free, 1)



def l0a_fold_dve(g, v):
    v.wait_ge(g.attn_loaded[0], 16)
    v.wait_ge(g.slot_free, g.n0["L0A"] + SLOTS)
    fc2 = g.w("L0A", "fc2").rearrange("p (k d) -> p k d", d=129)
    for k in range(4):
        ins = v.tensor_scalar(g.pr[0][:, k * P:(k + 1) * P], g.c("ones"), g.w("L0A", "fb")[:, k:k + 1], None, ALU.mult)
    ins.then_inc(g.fold_dve, 1)
    v.wait_ge(g.fold_pe, 1)
    b = g.w("L0A", "fc2b")
    v.tensor_tensor(b, b, g.ps[0][:, 0, 0:D], ALU.add).then_inc(g.fold_dve, 1)
    for k in range(4):
        ins = v.tensor_scalar(fc2[:, k, 0:D], fc2[:, k, 0:D], g.w("L0A", "fg")[:, k:k + 1], None, ALU.mult)
    ins.then_inc(g.fold_dve, 1)
    v.wait_ge(g.fold_pe, 2)
    v.tensor_copy(g.cs[:, :], g.ps[0][:, 1, 0:D]).then_inc(g.fold_dve, 1)
    v.wait_ge(g.fold_dve, 4)


def l0a_fold_pe(g, pe):
    fc2 = g.w("L0A", "fc2").rearrange("p (k d) -> p k d", d=129)
    pe.wait_ge(g.fold_dve, 1)
    for k in range(4):
        ins = pe.matmul(g.ps[0][:, 0, 0:D], g.pr[0][:, k * P:(k + 1) * P], fc2[:, k, 0:D], start=(k == 0), stop=(k == 3))
    ins.then_inc(g.fold_pe, 1)
    pe.wait_ge(g.fold_dve, 3)
    for k in range(4):
        ins = pe.matmul(g.ps[0][:, 1, 0:D], g.c("ones"), fc2[:, k, 0:D], start=(k == 0), stop=(k == 3))
    ins.then_inc(g.fold_pe, 1)
    pe.wait_ge(g.fold_dve, 4)


def l0a_pe(g, pe):
    w = lambda name: g.w("L0A", name)
    fc2 = w("fc2").rearrange("p (k d) -> p k d", d=129)
    l0a_fold_pe(g, pe)

    def group(t, s, i):
        n = g.n0["L0A"] + t + 1
        k = t + 1

        def step(level):
            if level == 1:
                front_pe(g, pe, s, n)
            if level == 3:
                pe.wait_ge(g.xT_ready, n)
                project_qk_pe(g, pe, s, w("qk")).then_inc(g.r_qk_done, 1)
            if level == 5:
                pe.wait_ge(g.r_q_ready, k)
                values_pe(g, pe, s, w("v"), g.xT[s]).then_inc(g.r_v_done, 1)
                for i in range(GT):
                    ins = pe.matmul(g.ps[s][:, 1, i * P:(i + 1) * P], g.xT[s][:, i * P:(i + 1) * P], w("g"), start=True, stop=True)
                ins.then_inc(g.r_g_done, 1)
            if level == 7:
                pe.wait_ge(g.r_g_ready, k)
                pe.wait_ge(g.r_k_ready, k)
                scores_pe(g, pe, s).then_inc(g.scores_done, 1)
            if level == 9:
                turn_probs_pe(g, pe, s, k)
            if level == 11:
                pe.wait_ge(g.pt_ready_a, k)
                pe.wait_ge(g.pt_ready_v, k)
                pe.sem_inc(g.wait_carrier_pe, 1)
                weigh_values_pe(g, pe, s).then_inc(g.values_weighed, 1)
            if level == 13:
                pe.wait_ge(g.o_ready, k)
                turn_out_pe(g, pe, s, o_tile(g, s)).then_inc(g.o_turned, 1)
            if level == 15:
                pe.wait_ge(g.oT_ready, k)
                project_out_pe(g, pe, s, w("wo")).then_inc(g.out_done, 1)
            if level == 17:
                pe.wait_ge(g.r_x1_ready, k)
                turn_out_pe(g, pe, s, lambda i: g.o[s][:, i, :]).then_inc(g.r_x1_turned, 1)
            if level == 19:
                pe.wait_ge(g.r_x1T_ready, k)
                for i in range(4):
                    ins = pe.matmul(g.ps[s][:, i, :], w("fc1")[:, i * D:(i + 1) * D], g.xT[s][:, :], start=True, stop=True)
                ins.then_inc(g.r_fc1_done, 1)
            if level == 21:
                pe.wait_ge(g.r_gelu_ready, k)
                for i in range(GT):
                    for c in range(4):
                        pe.matmul(g.psf[s][:, 256 * i:256 * i + 129], g.pr[s][:, c * 512 + i * P:c * 512 + (i + 1) * P],
                                  fc2[:, c, :], start=(c == 0), stop=(c == 3))
            if level == 23:
                pe.wait_ge(g.r_z_ready, k)
                for i in range(GT):
                    ins = pe.matmul(g.psf[s][:, 256 * i + 129:256 * i + 130], g.pt[s][:, i * P:(i + 1) * P],
                                    g.c("ones")[:, 0:1], start=True, stop=True)
                ins.then_inc(g.r_fc2_done, 1)

        return step

    pairs(g, pe, group, *SCHEDULE["L0A"])


def l0a_act(g, a):
    w = lambda name: g.w("L0A", name)

    def group(t, s, i):
        n = g.n0["L0A"] + t + 1
        k = t + 1

        def step(level):
            if level == 2:
                front_act(g, a, s, n)
            if level == 4:
                a.wait_ge(g.r_qk_done, k)
                for i in range(2):
                    ins = a.activation(g.qk[s][:, i, :], g.ps[s][:, i, :], ACT.Identity, bias=w("qkb")[:, i:i + 1])
                ins.then_inc(g.r_q_ready, 1)
            if level == 7:
                a.wait_ge(g.r_g_ready, k)
                a.activation(g.t2[s][:, :, :], g.t2[s][:, :, :], ACT.Silu).then_inc(g.r_silu_ready, 1)
            if level == 10:
                turned_probs_act(g, a, s, k)
            if level == 14:
                a.wait_ge(g.o_turned, k)
                a.activation(g.oT[s][:, :], g.ps[s][:, 2, :], ACT.Copy).then_inc(g.oT_ready, 1)
            if level == 18:
                a.wait_ge(g.r_x1_turned, k)
                a.activation(g.xT[s][:, :], g.ps[s][:, 2, :], ACT.Copy).then_inc(g.r_x1T_ready, 1)
            if level == 20:
                a.wait_ge(g.r_fc1_done, k)
                for i in range(4):
                    ins = a.activation(g.pr[s][:, i * 512:(i + 1) * 512], g.ps[s][:, i, :], ACT.Gelu, bias=w("fc1b")[:, i:i + 1])
                ins.then_inc(g.r_gelu_ready, 1)
            if level == 21:
                a.wait_ge(g.r_gelu_ready, k)
                a.activation(g.pt[s][:, :], g.pr[s][:, :], ACT.Square).then_inc(g.r_squares_ready, 1)

        return step

    pairs(g, a, group, *SCHEDULE["L0A"])


def l0a_pool(g, pool):
    def group(t, s, i):
        k = t + 1

        def step(level):
            if level == 22:
                pool.wait_ge(g.r_squares_ready, k)
                pool.tensor_tensor(g.pt[s][:, 0:1024], g.pt[s][:, 0:1024], g.pt[s][:, 1024:2048], ALU.add)\
                    .then_inc(g.r_squares_half, 1)
                pool.wait_ge(g.r_squares_half, k)
                pool.tensor_tensor(g.pt[s][:, 0:512], g.pt[s][:, 0:512], g.pt[s][:, 512:1024], ALU.add).then_inc(g.r_z_ready, 1)

        return step

    pairs(g, pool, group, *SCHEDULE["L0A"])


def l0a_dve(g, v):
    w = lambda name: g.w("L0A", name)
    l0a_fold_dve(g, v)
    links = slot_links(v, g.slot_link, g.link0["L0A"], LINKS["L0A"])

    def group(t, s, i):
        n = g.n0["L0A"] + t + 1
        k = t + 1
        link = links[s]
        link.group(i)
        row = lambda name: w(name).unsqueeze(1).to_broadcast([P, GT, D])
        o, xn, t2 = g.o[s][:, :, :], g.xn[s][:, :, :], g.t2[s][:, :, :]
        split = lambda ap: ap.rearrange("p (r t c) -> p r t c", r=4, t=GT)
        den = g.rm[s][:, 0:32]
        den4, sums = den.rearrange("p (t b) -> p t b", t=GT), g.heads(s)[:, :, :, DH]
        oh = g.of[s].rearrange("p (r e) -> p r e", e=DH)
        per_head = lambda ap: ap.unsqueeze(2).to_broadcast([P, 32, DH])
        sq = g.pr[s][:, 0:512].rearrange("p (r e) -> p r e", e=DH)
        z = g.psf[s][:, 0:1024].rearrange("p (t c) -> p t c", c=256)
        mean, sq4 = g.rm[s][:, 0:4], g.rm[s][:, 4:8]
        h = g.h[:, bass.ds(t * GT, GT), :]

        def step(level):
            if level == 0:
                front_dve(g, v, link, s, t, n)
            if level == 4:
                v.wait_ge(g.r_qk_done, k)
                for i in range(2, 4):
                    ins = v.tensor_scalar(g.qk[s][:, i, :], g.ps[s][:, i, :], w("qkb")[:, i:i + 1], DH ** -0.5, ALU.add, ALU.mult)
                ins.then_inc(g.r_k_ready, 1)
            if level == 6:
                v.wait_ge(g.r_v_done, k)
                for a in range(2):
                    rows = slice(64 * a, 64 * a + 64)
                    bias = w("bv")[rows, :].rearrange("p (h e) -> p h e", e=DH).unsqueeze(1).to_broadcast([64, 8, 4, DH])
                    ins = v.tensor_tensor(g.v2[s][rows, :, :, a, 0:DH],
                                          g.ps[s][rows, 0, :].rearrange("p (q h e) -> p q h e", q=8, e=DH), bias, ALU.add)
                link(ins)
                v.wait_ge(g.r_g_done, k)
                v.tensor_tensor(t2, g.ps[s][:, 1, :].rearrange("p (t d) -> p t d", d=D), row("bg"), ALU.add).then_inc(g.r_g_ready, 1)
            if level == 8:
                v.wait_ge(g.scores_done, k)
                for half in (slice(0, 2), slice(2, 4)):
                    v.tensor_tensor(split(g.pr[s][:, :])[:, half], split(g.psf[s])[:, half],
                                    g.c("dm").rearrange("p (r c) -> p r c", r=4)[:, half].unsqueeze(2)
                                    .to_broadcast([P, 2, GT, 2 * SEQ]), ALU.add).then_inc(g.probs_ready, 1)
            if level == 10:
                turned_probs_dve(g, v, s, k)
            if level == 12:
                v.wait_ge(g.values_weighed, k)
                link(v.tensor_scalar(den4, sums, 1.0, None, ALU.max))
                link(v.scalar_tensor_tensor(den4, sums, -1.0, den4, ALU.mult, ALU.max))
                link(v.reciprocal(den, den))
                link(scale_heads_dve(g, v, s))
                link(v.tensor_reduce(g.rm[s][:, 0:32], oh, AX.X, ALU.add))
                link(v.scalar_tensor_tensor(oh, per_head(g.rm[s][:, 0:32]), -1.0 / DH, oh, ALU.mult, ALU.add))
                link(v.tensor_tensor(sq, oh, oh, ALU.mult))
                link(v.tensor_reduce(g.rm[s][:, 0:32], sq, AX.X, ALU.add))
                rsqrt_dve(g, v, link, s, 32, g.rm[s][:, 0:32], 1e-6, 1.0 / DH)
                link(v.tensor_tensor(oh, oh, per_head(g.rs[s][:, 0:32]), ALU.mult))
                v.wait_ge(g.r_silu_ready, k)
                v.tensor_tensor(o, o, t2, ALU.mult).then_inc(g.o_ready, 1)
            if level == 16:
                v.wait_ge(g.out_done, k)
                link(v.tensor_tensor(t2, g.ps[s][:, 3, :].rearrange("p (t d) -> p t d", d=D), row("bo"), ALU.add))
                link(v.tensor_tensor(xn, xn, t2, ALU.add))
                norm_dve(g, v, link, s, [g.xn[s][:, i, :] for i in range(GT)], 1e-5)
                link(normalise_dve(g, v, s, [g.xn[s][:, i, :] for i in range(GT)], [g.xn[s][:, i, :] for i in range(GT)]))
                link(v.tensor_tensor(xn, xn, row("n0g"), ALU.mult))
                v.tensor_tensor(o, xn, row("n0b"), ALU.add).then_inc(g.r_x1_ready, 1)
            if level == 24:
                v.wait_ge(g.r_fc2_done, k)
                link(v.tensor_scalar(g.rm[s][:, 0:8].rearrange("p (a t) -> p t a", a=2), z[:, :, 128:130], 1.0 / FFN, None, ALU.mult))
                link(v.tensor_tensor(g.rm[s][:, 8:12], mean, mean, ALU.mult))
                link(v.tensor_tensor(sq4, sq4, g.rm[s][:, 8:12], ALU.subtract))
                rsqrt_dve(g, v, link, s, 4, sq4, 1e-6)
                link(v.scalar_tensor_tensor(mean, mean, -1.0, g.rs[s][:, 0:4], ALU.mult, ALU.mult))
                for i in range(GT):
                    ins = v.scalar_tensor_tensor(g.t2[s][:, i, :], g.cs[:, :], mean[:, i:i + 1], w("fc2b"), ALU.mult, ALU.add)
                link(ins)
                for i in range(GT):
                    ins = v.scalar_tensor_tensor(g.t2[s][:, i, :], z[:, i, 0:D], g.rs[s][:, i:i + 1], g.t2[s][:, i, :], ALU.mult, ALU.add)
                link(ins)
                link(v.tensor_tensor(t2, t2, o, ALU.add))
                norm_dve(g, v, link, s, [g.t2[s][:, i, :] for i in range(GT)], 1e-5)
                link(normalise_dve(g, v, s, [g.t2[s][:, i, :] for i in range(GT)], [g.t2[s][:, i, :] for i in range(GT)]))
                link(v.tensor_tensor(t2, t2, row("n1g"), ALU.mult))
                link(v.tensor_tensor(t2, t2, row("n1b"), ALU.add))
                v.tensor_tensor(h, t2, h, ALU.add).then_inc(g.slot_free, 1)
                link.end()

        return step

    pairs(g, v, group, *SCHEDULE["L0A"])



def values_act(g, a, s):
    for half in range(2):
        rows = slice(64 * half, 64 * half + 64)
        ins = a.activation(g.v2[s][rows, :, :, half, 0:DH],
                           g.ps[s][rows, 0, :].rearrange("p (q h e) -> p q h e", q=2 * GT, e=DH), ACT.Copy)
    return ins


def attend_act(g, a, s, k, bias=None, turn_out=True, masked_after=None, keys=SEQ, scale=1.0, level=0):
    if level == 2:
        for half in range(2):
            a.wait_ge(g.centred_ready, (k - g.uncentred) * 2 - 1 + half)
            rows = g.pr[s][:, 1024 * half:1024 * half + 1024].rearrange("p (r j) -> p r j", j=SEQ)[:, :, 0:keys]
            a.activation(rows, rows, ACT.Exp, scale=scale)\
                .then_inc(masked_after if masked_after is not None else g.probs_ready, 1)
    if level == 5:
        turned_probs_act(g, a, s, k)
    if level == 9 and turn_out:
        a.wait_ge(g.o_turned, k)
        if bias is None:
            ins = a.activation(g.oT[s][:, :], g.ps[s][:, 2, :], ACT.Copy)
        else:
            ins = a.activation(g.oT[s][:, :], g.ps[s][:, 2, :], ACT.Identity, bias=bias)
        ins.then_inc(g.oT_ready, 1)


def times_table_dve(g, v, s, half, banks, table):
    return v.tensor_tensor(g.qk[s][:, half:half + 2, :].rearrange("p a (q j) -> p (a q) j", j=SEQ),
                           g.ps[s][:, banks:banks + 2, :].rearrange("p a (q j) -> p (a q) j", j=SEQ),
                           table.unsqueeze(1).to_broadcast([P, 16, SEQ]), ALU.mult)



def l1a_pe(g, pe):
    w = lambda name: g.w("L1A", name)

    def group(t, s, i):
        n, j, k = g.n0["L1A"] + t + 1, t + 1, g.k0["L1A"] + t + 1
        cq, ckv = g.of[s][0:QP, :], g.oT[s][0:KVP, :]

        def step(level):
            if level == 1:
                front_pe(g, pe, s, n)
            if level == 3:
                pe.wait_ge(g.xT_ready, n)
                for i in range(GT):
                    ins = pe.matmul(g.psf[s][:, 256 * i:256 * i + QP + KVP], g.xT[s][:, i * P:(i + 1) * P], w("down"),
                                    start=True, stop=True)
                ins.then_inc(g.m_down_done, 1)
            if level == 5:
                pe.wait_ge(g.m_latent_ready, j)
                for i in range(GT):
                    at = i * (QP + KVP)
                    pe.transpose(g.ps[s][0:KVP, 1, i * P:(i + 1) * P], g.pr[s][:, at + QP:at + QP + KVP], g.c("ident"))
                    ins = pe.transpose(g.ps[s][0:QP, 0, i * P:(i + 1) * P], g.pr[s][:, at:at + QP], g.c("ident"))
                ins.then_inc(g.m_latent_turned, 1)
            if level == 7:
                pe.wait_ge(g.m_latentT_ready, j)
                for i in range(2):
                    cols = slice(i * D, (i + 1) * D)
                    pe.matmul(g.ps[s][:, i, :], w("q")[0:QP, cols], cq, start=True, stop=True)
                    pe.matmul(g.ps[s][:, 2 + i, :], w("kn")[0:KVP, cols], ckv, start=True, stop=False)
                    ins = pe.matmul(g.ps[s][:, 2 + i, :], w("kr")[:, cols], g.xT[s][:, :], start=False, stop=True)
                ins.then_inc(g.m_qk_done, 1)
            if level == 9:
                pe.wait_ge(g.m_qk_ready, j)
                values_pe(g, pe, s, w("v"), g.oT[s], KVP).then_inc(g.m_v_done, 1)
            attend_pe(g, pe, s, k, [(g.m_v_ready, j)], w("wo"), level=level - 11)

        return step

    pairs(g, pe, group, *SCHEDULE["L1A"])


def l1a_act(g, a):
    w = lambda name: g.w("L1A", name)

    def group(t, s, i):
        n, j, k = g.n0["L1A"] + t + 1, t + 1, g.k0["L1A"] + t + 1

        def step(level):
            if level == 2:
                front_act(g, a, s, n)
            if level == 6:
                a.wait_ge(g.m_latent_turned, j)
                a.activation(g.of[s][0:QP, :], g.ps[s][0:QP, 0, :], ACT.Identity, bias=w("qbias")[0:QP, :], scale=w("qg")[0:QP, :])
                a.activation(g.oT[s][0:KVP, :], g.ps[s][0:KVP, 1, :], ACT.Identity, bias=w("kbias")[0:KVP, :],
                             scale=w("kg")[0:KVP, :]).then_inc(g.m_latentT_ready, 1)
            if level == 10:
                a.wait_ge(g.m_v_done, j)
                values_act(g, a, s).then_inc(g.m_v_ready, 1)
            attend_act(g, a, s, k, level=level - 11)

        return step

    pairs(g, a, group, *SCHEDULE["L1A"])


def l1a_dve(g, v):
    links = slot_links(v, g.slot_link, g.link0["L1A"], LINKS["L1A"])

    def group(t, s, i):
        n, j, k = g.n0["L1A"] + t + 1, t + 1, g.k0["L1A"] + t + 1
        link = links[s]
        link.group(i)
        parts = [g.psf[s][:, 256 * i + lo:256 * i + hi] for lo, hi in ((0, QP), (QP, QP + KVP)) for i in range(GT)]
        outs = [g.pr[s][:, 149 * i + lo:149 * i + hi] for lo, hi in ((0, QP), (QP, QP + KVP)) for i in range(GT)]

        def step(level):
            if level == 0:
                front_dve(g, v, link, s, t, n)
            if level == 4:
                v.wait_ge(g.const_loaded, 16)
                v.wait_ge(g.m_down_done, j)
                norm_dve(g, v, link, s, parts, 1e-5)
                normalise_dve(g, v, s, parts, outs).then_inc(g.m_latent_ready, 1)
            if level == 8:
                v.wait_ge(g.m_qk_done, j)
                times_table_dve(g, v, s, 0, 0, g.c("mla_q"))
                times_table_dve(g, v, s, 2, 2, g.c("mla_k")).then_inc(g.m_qk_ready, 1)
            if level == 12:
                softmax_dve(g, v, link, s, k, float(DH + 2) ** -0.5, g.c("causal"))
            if level == 16:
                turned_probs_dve(g, v, s, k)
            if level == 18:
                divide_dve(g, v, link, s, k)
            if level == 22:
                add_out_dve(g, v, s, t, k)
                link.end()

        return step

    pairs(g, v, group, *SCHEDULE["L1A"])



def l2f_pe(g, pe):
    w = lambda name: g.w("L2F", name)

    def group(t, s, i):
        n, j, k = g.n0["L2F"] + t + 1, t + 1, g.k0["L2F"] + t + 1

        def step(level):
            if level == 1:
                front_pe(g, pe, s, n)
            if level == 4:
                pe.wait_ge(g.f_conv_ready, j)
                project_qk_pe(g, pe, s, w("qk")).then_inc(g.f_qk_done, 1)
            if level == 6:
                pe.wait_ge(g.f_q_ready, j)
                values_pe(g, pe, s, w("v"), g.xT[s]).then_inc(g.f_v_done, 1)
            attend_pe(g, pe, s, k, [(g.f_v_ready, j), (g.f_k_ready, j)], w("wo"), level=level - 8)

        return step

    pairs(g, pe, group, *SCHEDULE["L2F"])


def l2f_act(g, a):
    w = lambda name: g.w("L2F", name)

    def group(t, s, i):
        n, j, k = g.n0["L2F"] + t + 1, t + 1, g.k0["L2F"] + t + 1

        def step(level):
            if level == 2:
                front_act(g, a, s, n)
            if level == 5:
                a.wait_ge(g.f_qk_done, j)
                for i in range(2):
                    ins = a.activation(g.qk[s][:, i, :], g.ps[s][:, i, :], ACT.Identity, bias=w("qkb")[:, i:i + 1])
                ins.then_inc(g.f_q_ready, 1)
                for i in range(2, 4):
                    ins = a.activation(g.qk[s][:, i, :], g.ps[s][:, i, :], ACT.Identity, bias=w("qkb")[:, i:i + 1])
                ins.then_inc(g.f_k_ready, 1)
            if level == 7:
                a.wait_ge(g.f_v_done, j)
                values_act(g, a, s).then_inc(g.f_v_ready, 1)
            attend_act(g, a, s, k, bias=w("bv"), masked_after=g.f_exp_ready, keys=TOK,
                       scale=float(D) ** -0.5, level=level - 8)

        return step

    pairs(g, a, group, *SCHEDULE["L2F"])


def l2f_dve(g, v):
    w = lambda name: g.w("L2F", name)
    links = slot_links(v, g.slot_link, g.link0["L2F"], LINKS["L2F"])

    def group(t, s, i):
        n, j, k = g.n0["L2F"] + t + 1, t + 1, g.k0["L2F"] + t + 1
        link = links[s]
        link.group(i)
        x, y = g.xT[s], g.t2[s][:, :, :].rearrange("p t d -> p (t d)")
        rows = lambda ap: ap.rearrange("p (r j) -> p r j", j=SEQ)
        score, left = rows(g.pr[s][:, :]), rows(g.pt[s][:, :])
        best = g.small[s][:, :].rearrange("p (r e) -> p r e", e=8)
        raw = rows(g.psf[s])

        def step(level):
            if level == 0:
                front_dve(g, v, link, s, t, n)
            if level == 3:
                v.wait_ge(g.xT_ready, n)
                link(v.memset(x[:, :].rearrange("p (q j) -> p q j", j=SEQ)[:, :, TOK:SEQ], 0.0))
                link(v.scalar_tensor_tensor(y, x[:, :], w("conv")[:, 1:2], x[:, :], ALU.mult, ALU.add))
                link(v.scalar_tensor_tensor(y[:, 1:], x[:, 0:GTOK - 1], w("conv")[:, 0:1], y[:, 1:], ALU.mult, ALU.add))
                link(v.scalar_tensor_tensor(y[:, 0:GTOK - 1], x[:, 1:], w("conv")[:, 2:3], y[:, 0:GTOK - 1], ALU.mult, ALU.add))
                v.tensor_scalar(x[:, :], y, w("convb"), None, ALU.add).then_inc(g.f_conv_ready, 1)
            if level == 9:
                v.wait_ge(g.scores_done, k)
                v.sem_inc(g.wait_carrier, 1)
                source = raw
                for turn in range(2):
                    for r in range(32):
                        ins = v.max(best[:, r, :], source[:, r, 0:TOK])
                    link(ins, g.wait_carrier)
                    if turn == 0:
                        v.tensor_copy(g.rm[s][:, 0:32], best[:, :, 0])
                    for r in range(32):
                        ins = v.match_replace(left[:, r, 0:TOK], best[:, r, :], source[:, r, 0:TOK], PICKED)
                    link(ins, g.wait_carrier)
                    source = left
                v.memset(score[:, :, TOK:SEQ], 0.0)
                for half in (slice(0, 16), slice(16, 32)):
                    v.tensor_tensor(score[:, half, 0:TOK], raw[:, half, 0:TOK],
                                    g.rm[s][:, half].unsqueeze(2).to_broadcast([P, 16, TOK]),
                                    ALU.subtract).then_inc(g.centred_ready, 1)
            if level == 11:
                for half in range(2):
                    v.wait_ge(g.f_exp_ready, j * 2 - 1 + half)
                    rows16 = slice(16 * half, 16 * half + 16)
                    v.scalar_tensor_tensor(score[:, rows16, 0:TOK], left[:, rows16, 0:TOK], 0.5 * (NEG + PICKED),
                                           score[:, rows16, 0:TOK], ALU.is_lt, ALU.mult).then_inc(g.probs_ready, 1)
            if level == 13:
                turned_probs_dve(g, v, s, k)
            if level == 15:
                divide_dve(g, v, link, s, k)
            if level == 19:
                add_out_dve(g, v, s, t, k, w("bo"), link)
                link.end()

        return step

    pairs(g, v, group, *SCHEDULE["L2F"])



def l3a_fold_pe(g, pe):
    w = lambda name: g.w("L3A", name)
    pe.wait_ge(g.slot_free, g.n0["L3A"] + 1)
    pe.matmul(g.ps[0][:, 0, :], w("la")[0:8, :], w("lbqk")[0:8, :], start=True, stop=True)
    pe.matmul(g.ps[0][:, 1, 0:D], w("la")[0:8, :], w("lbv")[0:8, :], start=True, stop=True)
    pe.matmul(g.ps[0][:, 2, 0:D], w("loa")[0:8, :], w("lob")[0:8, :], start=True, stop=True).then_inc(g.lora_pe, 1)
    pe.wait_ge(g.lora_dve, 1)


def l3a_fold_dve(g, v):
    v.wait_ge(g.lora_pe, 1)
    for bank, name in enumerate(("qk", "v", "wo")):
        w = g.w("L3A", name)
        ins = v.scalar_tensor_tensor(w, g.ps[0][:, bank, 0:w.shape[1]], 0.25, w, ALU.mult, ALU.add)
    ins.then_inc(g.lora_dve, 1)


def l3a_pe(g, pe):
    w = lambda name: g.w("L3A", name)
    l3a_fold_pe(g, pe)

    def group(t, s, i):
        n, j, k = g.n0["L3A"] + t + 1, t + 1, g.k0["L3A"] + t + 1

        def step(level):
            if level == 1:
                front_pe(g, pe, s, n)
            if level == 3:
                pe.wait_ge(g.xT_ready, n)
                project_qk_pe(g, pe, s, w("qk")).then_inc(g.w_qk_done, 1)
            if level == 5:
                pe.wait_ge(g.w_q_ready, j)
                pe.matmul(g.ps[s][:, 1, 0:2 * GT], w("v"), g.xT[s][:, 0:GTOK:SEQ], start=True, stop=True)
                values_pe(g, pe, s, w("v"), g.xT[s]).then_inc(g.w_v_done, 1)
            attend_pe(g, pe, s, k, [(g.w_v_ready, j), (g.w_k_ready, j)], w("wo"), level=level - 7)

        return step

    pairs(g, pe, group, *SCHEDULE["L3A"])


def l3a_act(g, a):
    def group(t, s, i):
        n, j, k = g.n0["L3A"] + t + 1, t + 1, g.k0["L3A"] + t + 1

        def step(level):
            if level == 2:
                front_act(g, a, s, n)
            if level == 4:
                a.wait_ge(g.w_qk_done, j)
                a.activation(g.qk[s][:, 0:2, :], g.ps[s][:, 0:2, :], ACT.Copy).then_inc(g.w_q_ready, 1)
            if level == 6:
                a.wait_ge(g.w_v_done, j)
                a.activation(g.small[s][:, 0:2 * GT], g.ps[s][:, 1, 0:2 * GT], ACT.Copy)
                values_act(g, a, s).then_inc(g.w_v_ready, 1)
            attend_act(g, a, s, k, turn_out=False, level=level - 7)

        return step

    pairs(g, a, group, *SCHEDULE["L3A"])


def l3a_dve(g, v):
    w = lambda name: g.w("L3A", name)
    l3a_fold_dve(g, v)
    links = slot_links(v, g.slot_link, g.link0["L3A"], LINKS["L3A"])

    def group(t, s, i):
        n, j, k = g.n0["L3A"] + t + 1, t + 1, g.k0["L3A"] + t + 1
        link = links[s]
        link.group(i)
        split = lambda ap: ap.rearrange("p (q j) -> p q j", j=SEQ)

        def step(level):
            if level == 0:
                front_dve(g, v, link, s, t, n)
            if level == 4:
                v.wait_ge(g.w_qk_done, j)
                v.tensor_copy(g.qk[s][:, 2:4, :], g.ps[s][:, 2:4, :]).then_inc(g.w_k_ready, 1)
            if level == 8:
                softmax_dve(g, v, link, s, k, DH ** -0.5, g.c("causal"))
            if level == 12:
                turned_probs_dve(g, v, s, k)
            if level == 14:
                divide_dve(g, v, link, s, k)
            if level == 16:
                v.wait_ge(g.o_turned, k)
                v.tensor_tensor(split(g.oT[s][:, :]), split(g.ps[s][:, 2, :]),
                                g.small[s][:, 0:2 * GT].unsqueeze(2).to_broadcast([P, 2 * GT, SEQ]), ALU.add).then_inc(g.oT_ready, 1)
            if level == 18:
                add_out_dve(g, v, s, t, k, w("bo"), link)
                link.end()

        return step

    pairs(g, v, group, *SCHEDULE["L3A"])



def rms_dve(g, v, link, s):
    for i in range(GT):
        ins = v.bn_stats(g.stats[s][:, i, :], g.xn[s][:, i, :])
    link(ins, g.wait_carrier)
    for i in range(GT):
        ins = v.bn_aggr(g.mv[s][:, i, :], g.stats[s][:, i, :])
    link(ins)
    link(v.tensor_tensor(g.rm[s][:, 0:GT], g.mv[s][:, 0:GT, 0], g.mv[s][:, 0:GT, 0], ALU.mult))
    link(v.tensor_tensor(g.rm[s][:, 0:GT], g.rm[s][:, 0:GT], g.mv[s][:, 0:GT, 1], ALU.add))
    rsqrt_dve(g, v, link, s, GT, g.rm[s][:, 0:GT], 1e-5)


def l3f_pe(g, pe):
    w = lambda name: g.w("L3F", name)

    def group(t, s, i):
        n, j, k = g.n0["L3F"] + t + 1, t + 1, g.k0["L3F"] + t + 1

        def step(level):
            if level == 1:
                pe.wait_ge(g.const_loaded, 16)
                pe.wait_ge(g.xn_ready, n)
                for i in range(GT):
                    ins = pe.transpose(g.ps[s][:, 0, i * P:(i + 1) * P], g.t2[s][:, i, :], g.c("ident"))
                ins.then_inc(g.xn_transposed, 1)
            if level == 3:
                pe.wait_ge(g.xT_ready, n)
                for i in range(2):
                    cols = slice(i * D, (i + 1) * D)
                    pe.matmul(g.ps[s][:, i, :], w("qk")[:, cols], g.xT[s][:, :], start=True, stop=True)
                    ins = pe.matmul(g.ps[s][:, 2 + i, :], w("qr")[:, cols], g.xT[s][:, :], start=True, stop=True)
                ins.then_inc(g.p_q_done, 1)
            if level == 5:
                pe.wait_ge(g.p_q_ready, j)
                project_qk_pe(g, pe, s, w("qk"), 2, 2).then_inc(g.p_k_done, 1)
            if level == 7:
                pe.wait_ge(g.p_k_ready, j)
                values_pe(g, pe, s, w("v"), g.xT[s]).then_inc(g.p_v_done, 1)
            attend_pe(g, pe, s, k, [(g.p_v_ready, j)], w("wo"), level=level - 9)

        return step

    pairs(g, pe, group, *SCHEDULE["L3F"])


def l3f_act(g, a):
    w = lambda name: g.w("L3F", name)

    def group(t, s, i):
        n, j, k = g.n0["L3F"] + t + 1, t + 1, g.k0["L3F"] + t + 1

        def step(level):
            if level == 2:
                a.wait_ge(g.xn_transposed, n)
                a.activation(g.xT[s][:, :], g.ps[s][:, 0, :], ACT.Copy, scale=w("nw")).then_inc(g.xT_ready, 1)
            if level == 8:
                a.wait_ge(g.p_v_done, j)
                values_act(g, a, s).then_inc(g.p_v_ready, 1)
            attend_act(g, a, s, k, level=level - 9)

        return step

    pairs(g, a, group, *SCHEDULE["L3F"])


def l3f_dve(g, v):
    links = slot_links(v, g.slot_link, g.link0["L3F"], LINKS["L3F"])

    def group(t, s, i):
        n, j, k = g.n0["L3F"] + t + 1, t + 1, g.k0["L3F"] + t + 1
        link = links[s]
        link.group(i)
        rows = [g.h[:, bass.ds(t * GT + i, 1), :] for i in range(GT)]
        h = g.h[:, bass.ds(t * GT, GT), :]

        def step(level):
            if level == 0:
                v.wait_ge(g.const_loaded, 16)
                v.wait_ge(g.slot_free, n)
                norm_dve(g, v, link, s, rows, 1e-5)
                link(normalise_dve(g, v, s, rows, [g.xn[s][:, i:i + 1, :] for i in range(GT)]))
                rms_dve(g, v, link, s)
                for i in range(GT):
                    ins = v.tensor_scalar(g.t2[s][:, i, :], g.xn[s][:, i, :], g.rs[s][:, i:i + 1], None, ALU.mult)
                ins.then_inc(g.xn_ready, 1)
            if level == 4:
                v.wait_ge(g.p_q_done, j)
                split = lambda ap: ap.rearrange("p (q j) -> p q j", j=SEQ)
                both = lambda table: table.unsqueeze(1).to_broadcast([P, 16, SEQ])
                v.tensor_tensor(split(g.pr[s][:, 0:1024]), split(g.psf[s][:, 0:1024]), both(g.c("rope_cos")), ALU.mult)
                link(v.tensor_tensor(split(g.pr[s][:, 1024:2048]), split(g.psf[s][:, 1024:2048]), both(g.c("rope_sin")), ALU.mult))
                v.tensor_tensor(g.qk[s][:, 0:2, :].rearrange("p a c -> p (a c)"), g.pr[s][:, 0:1024],
                                g.pr[s][:, 1024:2048], ALU.add).then_inc(g.p_q_ready, 1)
            if level == 6:
                v.wait_ge(g.p_k_done, j)
                times_table_dve(g, v, s, 2, 2, g.c("rope_k")).then_inc(g.p_k_ready, 1)
            if level == 10:
                softmax_dve(g, v, link, s, k, DH ** -0.5, g.c("causal"))
            if level == 14:
                turned_probs_dve(g, v, s, k)
            if level == 16:
                divide_dve(g, v, link, s, k)
            if level == 20:
                v.wait_ge(g.out_done, k)
                link(v.tensor_tensor(g.a[:, bass.ds(t * GT, GT), :], g.ps[s][:, 3, :].rearrange("p (t d) -> p t d", d=D),
                                     g.xn[s][:, :, :], ALU.add))
                v.tensor_tensor(h, g.a[:, bass.ds(t * GT, GT), :], h, ALU.add).then_inc(g.slot_free, 1)
                link.end()

        return step

    pairs(g, v, group, *SCHEDULE["L3F"])


class Moe:

    def __init__(self, stage, kind, hidden):
        self.stage, self.kind = stage, kind
        self.up = hidden if kind != "swish" else 2 * hidden
        self.chunks = hidden // P
        self.units = self.up // (2 * P)
        self.links = NORM_LINKS + (2 if kind == "gelu" else 0) + 7
        self.cols = {}
        at = 0
        parts = [("up", EXPERTS * self.up), ("down", EXPERTS * self.chunks * D), ("router", EXPERTS)]
        if kind != "gelu":
            parts += [("rb", EXPERTS), ("ub", EXPERTS * self.up // P), ("db", D)]
        if kind == "swish":
            parts += [("sb", EXPERTS * self.up // P)]
        if kind == "gelu":
            parts += [("nw", 1)]
        for name, n in parts:
            self.cols[name] = (at, n)
            at += n
        self.width = at

    def w(self, g, name):
        at, n = self.cols[name]
        return g.w_big[:, at:at + n]


MOE = {"L0M": Moe("L0M", "swish", 256), "L1M": Moe("L1M", "relu", 256), "L3M": Moe("L3M", "gelu", 512)}
W_BIG = max(m.width for m in MOE.values())
ROUTE = 16
SENTINEL = -1.0e38



def moe_acts(g, e, chunk):
    return g.pr[e % 2][:, chunk * GTOK:(chunk + 1) * GTOK]


def moe_pe(stage):
    m = MOE[stage]

    def program(g, pe):
        sem = g.moe[stage]
        up, down = m.w(g, "up"), m.w(g, "down")
        pe.wait_ge(g.slot_free, g.n0[stage] + SLOTS)

        def turn_x(t, s, first=False):
            n = g.n0[stage] + t + 1
            if not first and m.kind != "gelu":
                pe.wait_ge(sem.gatesT_ready, g.m0[stage] + t)
            pe.wait_ge(g.xn_ready, n)
            for i in range(GT):
                ins = pe.transpose(g.ps[1][:, 2, i * P:(i + 1) * P], g.xn[s][:, i, :], g.c("ident"))
            ins.then_inc(g.xn_transposed, 1)

        def logits(t, s, first=False):
            pe.wait_ge(g.xT_ready, g.n0[stage] + t + 1)
            if not first:
                pe.wait_ge(sem.route_centred, g.m0[stage] + t)
            if not first and m.kind != "gelu":
                pe.wait_ge(sem.bias_added, g.m0[stage] + t)
            for i in range(GT):
                ins = pe.matmul(g.ps[1][:, 3, i * EXPERTS:(i + 1) * EXPERTS], g.xT[s][:, i * P:(i + 1) * P],
                                m.w(g, "router"), start=True, stop=True)
            ins.then_inc(sem.logits_done, 1)

        def turn_gates(t, s):
            pe.wait_ge(sem.gates_ready, g.m0[stage] + t + 1)
            for i in range(GT):
                ins = pe.transpose(g.ps[1][0:EXPERTS, 2, i * P:(i + 1) * P], g.gates[s][:, i * EXPERTS:(i + 1) * EXPERTS],
                                   g.c("ident"))
            ins.then_inc(sem.gates_turned, 1)

        def bias(t, s):
            pe.wait_ge(sem.gatesT_ready, g.m0[stage] + t + 1)
            for i in range(GT):
                ins = pe.matmul(g.ps[1][:, 3, i * P:(i + 1) * P], g.oT[s][0:EXPERTS, i * P:(i + 1) * P],
                                m.w(g, "db")[0:EXPERTS, :], start=True, stop=True)
            ins.then_inc(sem.bias_done, 1)

        def unit(t, s, e, u):
            if m.kind == "relu":
                pe.wait_ge(sem.hidden_ready, t * EXPERTS + e + 1)
                pe.wait_ge(sem.hidden_ready_v, t * EXPERTS + e + 1)
            else:
                pe.wait_ge(sem.unit_free, (t * EXPERTS + e) * m.units + u + 1)
            b = 2 * ((e * m.units + u) % 2)
            for i in range(2):
                c = e * m.up + (i * m.chunks + u if m.kind == "swish" else 2 * u + i) * P
                ins = pe.matmul(g.ps[0][:, b + i, :], up[:, c:c + P], g.xT[s][:, :], start=True, stop=True)
            ins.then_inc(sem.unit_done, 1)

        def down_of(t, s, e):
            if m.kind == "relu":
                pe.wait_ge(sem.hidden_ready, t * EXPERTS + e + 3)
                pe.wait_ge(sem.hidden_ready_v, t * EXPERTS + e + 3)
            else:
                pe.wait_ge(sem.unit_free, (t * EXPERTS + e + 1) * m.units + 2)
            pe.wait_ge(sem.down_free, t * EXPERTS + e + 1)
            for i in range(GT):
                for c in range(m.chunks):
                    at = (e * m.chunks + c) * D
                    ins = pe.matmul(g.ps[1][:, e % 2, i * P:(i + 1) * P], moe_acts(g, e, c)[:, i * P:(i + 1) * P],
                                    down[:, at:at + D], start=(c == 0), stop=(c == m.chunks - 1))
            ins.then_inc(sem.down_done, 1)

        def prepare(t, s):
            turn_x(t, s, True)
            logits(t, s, True)
            if m.kind != "gelu":
                turn_gates(t, s)

        def group(t, s, following):
            for e in range(EXPERTS):
                for u in range(m.units):
                    unit(t, s, e, u)
                    if u == (1 if m.kind == "swish" else 0) and e > 0:
                        down_of(t, s, e - 1)
                if e == 1 and m.kind != "gelu":
                    bias(t, s)
                if following:
                    if e == 4:
                        turn_x(t + 1, 1 - s)
                    if e == 5:
                        logits(t + 1, 1 - s)
            down_of(t, s, EXPERTS - 1)
            if following and m.kind != "gelu":
                turn_gates(t + 1, 1 - s)

        prepare(0, 0)
        moe_groups(pe, g, group)

    return program


def moe_groups(eng, g, group):
    if g.groups > 2:
        with eng.Fori(0, g.groups // 2 - 1) as i:
            group(i * 2, 0, True)
            group(i * 2 + 1, 1, True)
    group(g.groups - 2, 0, True)
    group(g.groups - 1, 1, False)


def moe_act(stage):
    m = MOE[stage]

    def program(g, a):
        sem = g.moe[stage]
        if m.kind == "swish":
            a.wait_ge(sem.bias_scaled, 1)

        def evacuate_x(t, s):
            n = g.n0[stage] + t + 1
            a.wait_ge(g.xn_transposed, n)
            if m.kind == "gelu":
                a.activation(g.xT[s][:, :], g.ps[1][:, 2, :], ACT.Copy, scale=m.w(g, "nw")).then_inc(g.xT_ready, 1)
            else:
                a.activation(g.xT[s][:, :], g.ps[1][:, 2, :], ACT.Copy).then_inc(g.xT_ready, 1)

        def exponentials(t, s):
            a.wait_ge(sem.route_centred, g.m0[stage] + t + 1)
            a.activation(g.gates[s][:, :], g.gates[s][:, :], ACT.Exp).then_inc(sem.route_exp, 1)

        def evacuate_gates(t, s):
            a.wait_ge(sem.gates_turned, g.m0[stage] + t + 1)
            a.activation(g.oT[s][0:EXPERTS, :], g.ps[1][0:EXPERTS, 2, :], ACT.Copy).then_inc(sem.gatesT_ready, 1)

        def unit(t, s, e, u):
            b = 2 * ((e * m.units + u) % 2)
            a.wait_ge(sem.unit_done, (t * EXPERTS + e) * m.units + u + 1)
            if m.kind == "swish":
                at = e * m.up // P + u
                a.activation(g.pt[0][:, (b // 2) * GTOK:(b // 2 + 1) * GTOK], g.ps[0][:, b, :], ACT.Sigmoid, scale=1.702,
                             bias=m.w(g, "sb")[:, at:at + 1]).then_inc(sem.sig_ready, 1)
                return
            if u == 0:
                a.wait_ge(sem.down_done, t * EXPERTS + e + 1)
            if m.kind == "relu":
                at = e * m.up // P
                a.activation(moe_acts(g, e, 0), g.ps[0][:, b, :], ACT.Relu, bias=m.w(g, "ub")[:, at:at + 1])\
                    .then_inc(sem.hidden_ready, 1)
            else:
                ins = a.activation(g.pr[e % 2][:, 2 * u * GTOK:(2 * u + 2) * GTOK],
                                   g.ps[0][:, b:b + 2, :], ACT.Gelu)
                ins.then_inc(sem.unit_free, 1)

        def group(t, s, following):
            for e in range(EXPERTS):
                for u in range(m.units):
                    unit(t, s, e, u)
                if following:
                    if e == 4:
                        evacuate_x(t + 1, 1 - s)
                    if e == 6:
                        exponentials(t + 1, 1 - s)
                    if e == 7 and m.kind != "gelu":
                        evacuate_gates(t + 1, 1 - s)

        evacuate_x(0, 0)
        exponentials(0, 0)
        if m.kind != "gelu":
            evacuate_gates(0, 0)
        moe_groups(a, g, group)

    return program


def moe_dve(stage):
    m = MOE[stage]

    def program(g, v):
        sem = g.moe[stage]
        link = Link(v, g.moe_link, g.link0[stage], m.links)
        v.wait_ge(g.slot_free, g.n0[stage] + SLOTS)
        v.sem_inc(sem.down_free, 2)
        v.sem_inc(sem.down_done, 2)
        if m.kind == "relu":
            v.sem_inc(sem.hidden_ready, 2)
            v.sem_inc(sem.hidden_ready_v, 2)
        else:
            v.sem_inc(sem.unit_free, 2)
        for s in range(SLOTS):
            ins = v.memset(g.small[s][:, 0:192], SENTINEL)
        if m.kind == "swish":
            v.tensor_scalar(m.w(g, "sb"), m.w(g, "ub"), 1.702, None, ALU.mult).then_inc(sem.bias_scaled, 1)
            v.wait_ge(sem.bias_scaled, 1)
            ub = m.w(g, "ub").rearrange("p (e c) -> p e c", e=EXPERTS)[:, :, m.chunks:]
            ins = v.tensor_scalar(ub, ub, 1.0, None, ALU.add)
        ins.then_inc(sem.bias_scaled, 1)
        v.wait_ge(sem.bias_scaled, 2 if m.kind == "swish" else 1)
        source = g.a if m.kind == "gelu" else g.h

        def normalise(t, s):
            v.wait_ge(g.const_loaded, 16)
            rows = [source[:, bass.ds(t * GT + i, 1), :] for i in range(GT)]
            if m.kind != "gelu":
                yield from norm_steps(g, v, link, s, rows, 1e-5)
                ins = normalise_dve(g, v, s, rows, [g.xn[s][:, i:i + 1, :] for i in range(GT)])
            else:
                for i in range(GT):
                    ins = v.bn_stats(g.stats[s][:, i, :], rows[i])
                yield from link.later(ins)
                v.sem_inc(g.wait_carrier, 1)
                for i in range(GT):
                    ins = v.bn_aggr(g.mv[s][:, i, :], g.stats[s][:, i, :])
                yield from link.later(ins)
                yield from link.later(v.tensor_tensor(g.rm[s][:, 0:GT], g.mv[s][:, 0:GT, 0], g.mv[s][:, 0:GT, 0], ALU.mult))
                yield from link.later(v.tensor_tensor(g.rm[s][:, 0:GT], g.rm[s][:, 0:GT], g.mv[s][:, 0:GT, 1], ALU.add))
                yield from rsqrt_steps(g, v, link, s, GT, g.rm[s][:, 0:GT], 1e-5)
                for i in range(GT):
                    ins = v.tensor_scalar(g.xn[s][:, i:i + 1, :], rows[i], g.rs[s][:, i:i + 1], None, ALU.mult)
            ins.then_inc(g.xn_ready, 1)

        def route(t, s):
            lg = g.small[s][:, 0:GT * ROUTE].rearrange("p (t c) -> p t c", t=GT)
            left = g.small[s][:, 64:64 + GT * ROUTE].rearrange("p (t c) -> p t c", t=GT)
            top = g.small[s][:, 128:128 + GT * 8].rearrange("p (t c) -> p t c", t=GT)
            two = g.small[s][:, 160:160 + GT * 8].rearrange("p (t c) -> p t c", t=GT)
            ps = g.ps[1][:, 3, 0:GT * EXPERTS].rearrange("p (t e) -> p t e", t=GT)
            v.wait_ge(sem.logits_done, g.m0[stage] + t + 1)
            if m.kind == "gelu":
                yield from link.later(v.tensor_copy(lg[:, :, 0:EXPERTS], ps))
            else:
                yield from link.later(v.tensor_tensor(lg[:, :, 0:EXPERTS], ps, m.w(g, "rb").unsqueeze(1)
                                                      .to_broadcast([P, GT, EXPERTS]), ALU.add))
            v.sem_inc(g.wait_carrier, 1)
            for i in range(GT):
                ins = v.max(top[:, i, :], lg[:, i, 0:EXPERTS])
            yield from link.later(ins)
            yield from link.later(v.tensor_copy(two[:, :, 0:2], top[:, :, 0:2]))
            v.sem_inc(g.wait_carrier, 1)
            for i in range(GT):
                ins = v.match_replace(left[:, i, 0:14], two[:, i, :], lg[:, i, 0:14], PICKED)
            yield from link.later(ins)
            gates = g.gates[s][:, :].rearrange("p (t e) -> p t e", t=GT)
            v.tensor_tensor(gates, lg[:, :, 0:EXPERTS], top[:, :, 0:1].to_broadcast([P, GT, EXPERTS]),
                            ALU.subtract).then_inc(sem.route_centred, 1)

        def gate(t, s):
            left = g.small[s][:, 64:64 + GT * ROUTE].rearrange("p (t c) -> p t c", t=GT)
            gates = g.gates[s][:, :].rearrange("p (t e) -> p t e", t=GT)
            sums = g.small[s][:, 192:192 + GT]
            v.wait_ge(sem.route_exp, g.m0[stage] + t + 1)
            yield from link.later(v.scalar_tensor_tensor(gates, left[:, :, 0:EXPERTS], 0.5 * (SENTINEL + PICKED), gates, ALU.is_lt, ALU.mult))
            yield from link.later(v.tensor_reduce(sums, gates, AX.X, ALU.add))
            yield from link.later(v.reciprocal(sums, sums))
            v.tensor_tensor(gates, gates, sums.unsqueeze(2).to_broadcast([P, GT, EXPERTS]),
                            ALU.mult).then_inc(sem.gates_ready, 1)
            link.end()

        def unit(t, s, e, u):
            b = 2 * ((e * m.units + u) % 2)
            at = e * m.up // P + u
            if m.kind == "swish":
                sig = g.pt[0][:, (b // 2) * GTOK:(b // 2 + 1) * GTOK]
                v.wait_ge(sem.sig_ready, (t * EXPERTS + e) * m.units + u + 1)
                v.scalar_tensor_tensor(sig, g.ps[0][:, b, :], m.w(g, "ub")[:, at:at + 1], sig,
                                       ALU.add, ALU.mult).then_inc(sem.sig_gated, 1)
                v.wait_ge(sem.sig_gated, (t * EXPERTS + e) * m.units + u + 1)
                if u == 0:
                    v.wait_ge(sem.down_done, t * EXPERTS + e + 1)
                at += m.chunks
                v.scalar_tensor_tensor(moe_acts(g, e, u), g.ps[0][:, b + 1, :], m.w(g, "ub")[:, at:at + 1], sig,
                                       ALU.add, ALU.mult).then_inc(sem.unit_free, 1)
            if m.kind == "relu":
                v.wait_ge(sem.unit_done, t * EXPERTS + e + 1)
                v.wait_ge(sem.down_done, t * EXPERTS + e + 1)
                v.tensor_scalar(moe_acts(g, e, 1), g.ps[0][:, b + 1, :], m.w(g, "ub")[:, at + 1:at + 2], 0.0,
                                ALU.add, ALU.max).then_inc(sem.hidden_ready_v, 1)

        def gather(t, s, e):
            if e == 0:
                v.wait_ge(sem.gates_ready, g.m0[stage] + t + 1)
            if e == 1 and m.kind != "gelu":
                v.wait_ge(sem.bias_added, g.m0[stage] + t + 1)
            v.wait_ge(sem.down_free, t * EXPERTS + e + 2)
            v.wait_ge(sem.down_done, t * EXPERTS + e + 3)
            for i in range(GT):
                row = g.h[:, bass.ds(t * GT + i, 1), :]
                ins = v.scalar_tensor_tensor(row, g.ps[1][:, e % 2:e % 2 + 1, i * P:(i + 1) * P],
                                             g.gates[s][:, i * EXPERTS + e:i * EXPERTS + e + 1], row, ALU.mult, ALU.add)
            ins.then_inc(sem.down_free, 1)

        def add_bias(t, s):
            v.wait_ge(sem.down_free, t * EXPERTS + 3)
            v.wait_ge(sem.bias_done, g.m0[stage] + t + 1)
            h = g.h[:, bass.ds(t * GT, GT), :]
            v.tensor_tensor(h, g.ps[1][:, 3, :].rearrange("p (t d) -> p t d", d=D), h, ALU.add).then_inc(sem.bias_added, 1)

        def advance(steps, count=None):
            for done, _ in enumerate(steps, 1):
                if done == count:
                    return

        def group(t, s, following):
            normalising = routing = gating = iter(())
            if following:
                link.group(t + 1)
                normalising, routing, gating = normalise(t + 1, 1 - s), route(t + 1, 1 - s), gate(t + 1, 1 - s)
            for e in range(EXPERTS):
                for u in range(m.units):
                    unit(t, s, e, u)
                    if e < 3:
                        advance(normalising, -(-5 // m.units))
                if e == 2 and m.kind != "gelu":
                    add_bias(t, s)
                if e > 0:
                    gather(t, s, e - 1)
                if e == 3:
                    advance(normalising)
                if e == 5:
                    advance(routing)
                if e == 7:
                    advance(gating)
            gather(t, s, EXPERTS - 1)
            v.wait_ge(sem.down_free, (t + 1) * EXPERTS + 2)
            v.sem_inc(g.slot_free, 1)

        link.group(0)
        advance(normalise(0, 0))
        advance(route(0, 0))
        advance(gate(0, 0))
        moe_groups(v, g, group)

    return program


MOE_SEMS = ("logits_done", "gates_ready", "gates_turned", "gatesT_ready", "bias_done", "bias_added", "route_centred",
            "route_exp", "hidden_ready", "hidden_ready_v", "sig_ready", "sig_gated")
MOE_STAGE_SEMS = ("unit_free", "unit_done", "down_free", "down_done", "bias_scaled")


def moe_semaphores(sem, stages):
    common = [sem("moe_" + n) for n in MOE_SEMS]
    out = {}
    for st in stages:
        names = out[st] = Net()
        (names.logits_done, names.gates_ready, names.gates_turned, names.gatesT_ready, names.bias_done, names.bias_added,
         names.route_centred, names.route_exp, names.hidden_ready, names.hidden_ready_v, names.sig_ready,
         names.sig_gated) = common
        names.unit_free, names.unit_done, names.down_free, names.down_done, names.bias_scaled = (
            sem(f"{st}_{n}") for n in MOE_STAGE_SEMS)
    return out



MID = SEQ // 2 - 1


def l2a_gate(g, s):
    return g.a[:, 16 * s + 0:16 * s + 16, :].rearrange("p t d -> p (t d)")


def l2a_scores(g, s):
    return g.a[:, 32 + 8 * s:40 + 8 * s, :].rearrange("p t d -> p (t d)")


def l2a_pe(g, pe):
    w = lambda name: g.w("L2A", name)

    def group(t, s, i):
        n, j = g.n0["L2A"] + t + 1, t + 1
        og = l2a_gate(g, s)

        def step(level):
            if level == 1:
                front_pe(g, pe, s, n)
            if level == 3:
                pe.wait_ge(g.xT_ready, n)
                pe.matmul(g.ps[s][0:GR, 0, :], w("gk1"), g.xT[s][:, :], start=True, stop=True).then_inc(g.l_low_done, 1)
            if level == 5:
                pe.wait_ge(g.l_low_ready, j)
                for c in range(2):
                    ins = pe.matmul(g.ps[s][:, c, :], w("gk2")[0:GR, c * P:(c + 1) * P], g.oT[s][0:GR, :], start=True, stop=True)
                ins.then_inc(g.l_gk_done, 1)
            if level == 7:
                pe.wait_ge(g.l_gk_read, j)
                for i in range(4):
                    ins = pe.matmul(g.ps[s][:, i, :], w("qk")[:, i * D:(i + 1) * D], g.xT[s][:, :], start=True, stop=True)
                ins.then_inc(g.l_qk_done, 1)
            if level == 13:
                pe.wait_ge(g.l_qk_ready, j)
                for i in range(GT):
                    ins = pe.matmul(g.ps[s][:, i, :], g.xT[s][:, i * P:(i + 1) * P], w("v"), start=True, stop=True)
                ins.then_inc(g.l_v_done, 1)
            if level == 15:
                pe.wait_ge(g.l_v_ready, j)
                for i in range(GT):
                    ins = pe.matmul(g.ps[s][:, i, :], g.xT[s][:, i * P:(i + 1) * P], w("g"), start=True, stop=True)
                ins.then_inc(g.l_g_done, 1)
            if level == 17:
                pe.wait_ge(g.l_silu_ready, j)
                pe.sem_inc(g.wait_carrier_pe, 1)
                for sq in range(2):
                    for c in range(2):
                        for tile in range(GT):
                            for par in range(2):
                                rows, cols = slice(64 * par, 64 * par + 64), slice(tile * P + sq * SEQ, tile * P + sq * SEQ + SEQ)
                                at = (tile * 2 + c) * SEQ
                                ins = pe.matmul(g.ps[s][64 * sq:64 * sq + 64, par, at:at + SEQ], g.qk[s][rows, 2 + c, cols],
                                                g.qk[s][rows, c, cols], start=True, stop=True)
                ins.then_inc(g.l_scores_done, 1)
            if level == 19:
                pe.wait_ge(g.l_scores_ready, j)
                pe.sem_inc(g.wait_carrier_pe, 1)
                for tile in range(GT):
                    for h in range(GH):
                        for sq in range(2):
                            rows = slice(64 * sq, 64 * sq + 64)
                            at = (h % 2) * 512 + (tile * 2 + h // 2) * SEQ
                            ins = pe.matmul(g.ps[s][rows, tile, h * GV:(h + 1) * GV], l2a_scores(g, s)[rows, at:at + SEQ],
                                            g.pt[s][rows, tile * 512 + h * GV:tile * 512 + (h + 1) * GV], start=True, stop=True)
                ins.then_inc(g.l_o_done, 1)
            if level == 22:
                pe.wait_ge(g.l_og_ready, j)
                for h in range(GH):
                    for tile in range(GT):
                        at = tile * 512 + h * GV
                        ins = pe.transpose(g.ps[s][:, h, tile * P:(tile + 1) * P], og[:, at:at + GV], g.c("ident"))
                ins.then_inc(g.l_og_turned, 1)
            if level == 24:
                pe.wait_ge(g.l_ogT_ready_a, j)
                pe.wait_ge(g.l_ogT_ready_v, j)
                for tile in range(GT):
                    for h in range(GH):
                        ins = pe.matmul(g.ps[s][:, 3, tile * P:(tile + 1) * P], g.qk[s][:, h, tile * P:(tile + 1) * P],
                                        w("wo")[:, h * D:(h + 1) * D], start=(h == 0), stop=(h == GH - 1))
                ins.then_inc(g.l_out_done, 1)

        return step

    pairs(g, pe, group, *SCHEDULE["L2A"])


def l2a_act(g, a):
    def group(t, s, i):
        n, j = g.n0["L2A"] + t + 1, t + 1
        neg = g.pr[s][:, 1024:2048]

        def step(level):
            if level == 2:
                front_act(g, a, s, n)
            if level == 4:
                a.wait_ge(g.l_low_done, j)
                a.activation(g.oT[s][0:GR, :], g.ps[s][0:GR, 0, :], ACT.Copy).then_inc(g.l_low_ready, 1)
            if level == 7:
                a.wait_ge(g.l_gk_read, j)
                a.activation(neg, neg, ACT.Exp).then_inc(g.l_neg_exp, 1)
            if level == 8:
                a.wait_ge(g.l_neg_exp, j)
                a.activation(neg, neg, ACT.Ln, bias=1.0).then_inc(g.l_log_ready, 1)
            if level == 10:
                a.wait_ge(g.l_sum_ready, j)
                a.activation(g.pr[s][:, 1024:2048], g.pr[s][:, 0:1024], ACT.Exp, scale=1.0 / 16.0).then_inc(g.l_exp_ready, 1)
            if level == 11:
                a.wait_ge(g.l_exp_ready, j)
                a.activation(g.pr[s][:, 0:1024], g.pr[s][:, 0:1024], ACT.Exp, scale=-1.0 / 16.0).then_inc(g.l_inverse_ready, 1)
            if level == 14:
                a.wait_ge(g.l_v_done, j)
                a.activation(g.pt[s][:, :], g.psf[s], ACT.Copy).then_inc(g.l_v_ready, 1)
            if level == 16:
                a.wait_ge(g.l_g_done, j)
                a.activation(l2a_gate(g, s), g.psf[s], ACT.Silu).then_inc(g.l_silu_ready, 1)
            if level == 20:
                a.wait_ge(g.l_o_done, j)
                a.activation(g.pr[s][:, :], g.psf[s], ACT.Square).then_inc(g.l_sq_ready, 1)
            if level == 23:
                a.wait_ge(g.l_og_turned, j)
                a.activation(g.qk[s][:, 0:2, :], g.ps[s][:, 0:2, :], ACT.Copy).then_inc(g.l_ogT_ready_a, 1)

        return step

    pairs(g, a, group, *SCHEDULE["L2A"])


def l2a_dve(g, v):
    w = lambda name: g.w("L2A", name)
    v.tensor_scalar(w("wo"), w("wo"), w("rms"), None, ALU.mult).then_inc(g.l_fold, 1)
    v.wait_ge(g.l_fold, 1)
    links = slot_links(v, g.slot_link, g.link0["L2A"], LINKS["L2A"])

    def group(t, s, i):
        n, j = g.n0["L2A"] + t + 1, t + 1
        link = links[s]
        link.group(i)
        z, neg = g.pr[s][:, 0:1024], g.pr[s][:, 1024:2048]
        seqs = lambda ap: ap.rearrange("p (q j) -> p q j", j=SEQ)
        flat = g.qk[s][:, :, :].rearrange("p a c -> p (a c)")
        og = l2a_gate(g, s)
        og3 = og.rearrange("p (r e) -> p r e", e=GV)
        h = g.h[:, bass.ds(t * GT, GT), :]

        def step(level):
            if level == 0:
                front_dve(g, v, link, s, t, n)
            if level == 6:
                v.wait_ge(g.l_gk_done, j)
                for c in range(2):
                    ins = v.tensor_scalar(z[:, c * 512:(c + 1) * 512], g.ps[s][:, c, :], w("gkb")[:, c:c + 1], None, ALU.add)
                link(ins)
                v.scalar_tensor_tensor(neg, z, -1.0, z, ALU.mult, ALU.min).then_inc(g.l_gk_read, 1)
            if level == 9:
                v.wait_ge(g.l_log_ready, j)
                link(v.scalar_tensor_tensor(z, z, 0.0, neg, ALU.min, ALU.subtract))
                for c in range(2):
                    ins = v.tensor_tensor_scan(neg[:, c * 512:(c + 1) * 512], g.c("restart"), z[:, c * 512:(c + 1) * 512], 0.0,
                                               ALU.mult, ALU.add)
                link(ins)
                v.tensor_tensor(seqs(z), seqs(neg), seqs(neg)[:, :, MID:MID + 1].to_broadcast([P, 16, SEQ]),
                                ALU.subtract).then_inc(g.l_sum_ready, 1)
            if level == 12:
                v.wait_ge(g.l_qk_done, j)
                v.wait_ge(g.l_inverse_ready, j)
                v.scalar_tensor_tensor(flat[:, 0:1024], g.psf[s][:, 0:1024], GK ** -0.5, g.pr[s][:, 1024:2048], ALU.mult, ALU.mult)
                v.tensor_tensor(flat[:, 1024:2048], g.psf[s][:, 1024:2048], g.pr[s][:, 0:1024], ALU.mult).then_inc(g.l_qk_ready, 1)
            if level == 18:
                v.wait_ge(g.l_scores_done, j)
                v.tensor_tensor(seqs(l2a_scores(g, s)), seqs(g.psf[s][:, 0:1024]),
                                g.c("upper").unsqueeze(1).to_broadcast([P, 16, SEQ]), ALU.mult).then_inc(g.l_scores_ready, 1)
            if level == 21:
                v.wait_ge(g.l_sq_ready, j)
                link(v.tensor_tensor(og, g.psf[s], og, ALU.mult))
                link(v.tensor_reduce(g.rm[s][:, 0:16], g.pr[s][:, :].rearrange("p (r e) -> p r e", e=GV), AX.X, ALU.add))
                rsqrt_dve(g, v, link, s, 16, g.rm[s][:, 0:16], 1e-5, 1.0 / GV)
                v.tensor_tensor(og3, og3, g.rs[s][:, 0:16].unsqueeze(2).to_broadcast([P, 16, GV]), ALU.mult).then_inc(g.l_og_ready, 1)
            if level == 23:
                v.wait_ge(g.l_og_turned, j)
                v.tensor_copy(g.qk[s][:, 2:4, :], g.ps[s][:, 2:4, :]).then_inc(g.l_ogT_ready_v, 1)
            if level == 25:
                v.wait_ge(g.l_out_done, j)
                v.tensor_tensor(h, g.ps[s][:, 3, :].rearrange("p (t d) -> p t d", d=D), h, ALU.add).then_inc(g.slot_free, 1)
                link.end()

        return step

    pairs(g, v, group, *SCHEDULE["L2A"])


STEPS = TOK
CH = 8
FACTOR = CH ** 3 + CH ** 2 + CH + 1
CHUNKS = [(c * P, min(P, FACTOR - c * P)) for c in range((FACTOR + P - 1) // P)]
TOK_COLS = {"w": (0, len(CHUNKS) * CH * D), "b": (len(CHUNKS) * CH * D, D)}
TOK_WIDTH = TOK_COLS["b"][0] + D
START_LINKS, FACTOR_LINKS, COMBINE_LINKS = 4, 5, CH - 1
TOK_CHUNK = 9


def steps_loop(eng, body):
    with eng.Fori(0, (STEPS - 3) // 2) as i:
        body(i * 2, 0, 2)
        body(i * 2 + 1, 1, 2)
    for t in range(STEPS - 3, STEPS):
        body(t, t % 2, min(2, STEPS - 1 - t))


def factor_sb(g, s):
    return g.qk[s][:, :, :].rearrange("p a c -> p (a c)")[:, 0:FACTOR]


def tok_pe(g, pe):
    at, n = TOK_COLS["w"]
    w = g.w_big[:, at:at + n].rearrange("p (k c) -> p k c", k=len(CHUNKS))

    def turn(t, s):
        pe.wait_ge(g.factor_ready, t + 1)
        for k, (at, rows) in enumerate(CHUNKS):
            ins = pe.transpose(g.psf[s][0:rows, k * P:(k + 1) * P], factor_sb(g, s)[:, at:at + rows], g.c("ident"))
        ins.then_inc(g.factor_turned, 1)

    def step(t, s, after):
        if after:
            turn(t + 1, 1 - s)
        pe.wait_ge(g.factorT_ready, t + 1)
        pe.wait_ge(g.token_ready, t + 1)
        for k, (at, rows) in enumerate(CHUNKS):
            for half in range(2):
                ins = pe.matmul(g.ps[s][:, 2 + half, :], g.pr[s][0:rows, k * P:(k + 1) * P],
                                w[0:rows, k, half * 512:(half + 1) * 512], start=(k == 0), stop=(k == len(CHUNKS) - 1))
        ins.then_inc(g.product_done, 1)

    turn(0, 0)
    steps_loop(pe, step)


def tok_act(g, a):
    last = CHUNKS[-1][1]

    def step(t, s, after):
        full = (len(CHUNKS) - 1) * P
        a.wait_ge(g.factor_turned, t + 1)
        a.activation(g.pr[s][:, 0:full], g.psf[s][:, 0:full], ACT.Copy)
        a.activation(g.pr[s][0:last, full:full + P], g.psf[s][0:last, full:full + P], ACT.Copy).then_inc(g.factorT_ready, 1)

    steps_loop(a, step)


def tok_dve(g, v):
    x = g.t2[0][:, :, :].rearrange("p t d -> p (t d)")
    parts = {1: g.t2[1][:, :, :].rearrange("p t d -> p (t d)"), 2: g.xT[0][:, :], 3: g.xT[1][:, :],
             4: g.xn[0][:, :, :].rearrange("p t d -> p (t d)")}
    s1, s2, s3 = g.small[0][:, 0:CH], g.small[0][:, CH:CH + CH ** 2], g.oT[0][:, :]
    n = STEPS * CH
    start = Link(v, g.moe_link, 0, START_LINKS)
    start.group(0)
    v.wait_ge(g.x_loaded, 16)
    v.sem_inc(g.token_ready, 2)
    start(v.tensor_tensor(parts[1][:, 0:n], x[:, CH:CH + n], x[:, 0:n], ALU.subtract))
    for k in range(2, 5):
        ins = v.tensor_scalar(parts[k][:, 0:n], parts[1][:, 0:n], 1.0 / k, None, ALU.mult)
    start(ins)
    v.memset(s1, 0.0)
    v.memset(s2, 0.0)
    start(v.memset(s3, 0.0))
    for s in range(SLOTS):
        v.memset(factor_sb(g, s)[:, FACTOR - 1:FACTOR], 1.0)
    b0, bn = TOK_COLS["b"]
    start(v.tensor_copy(g.a[:, 0, :], g.w_big[:, b0:b0 + bn]))
    a1, b1 = g.small[1][:, 0:CH], g.small[1][:, CH:2 * CH]
    a2, n2 = g.small[1][:, 16:80], g.small[1][:, 80:144]
    b2 = g.small[1][:, 144:208]
    a3, n3 = g.oT[1][:, :], g.xn[1][:, :, :].rearrange("p t d -> p (t d)")

    def outer(out, left, right, size):
        return v.tensor_tensor(out.rearrange("p (i c) -> p i c", c=CH), left.unsqueeze(2).to_broadcast([P, size, CH]),
                               right.unsqueeze(1).to_broadcast([P, size, CH]), ALU.mult)

    def factors(t, s, link):
        vec = {k: parts[k][:, bass.ds(t * CH, CH)] for k in parts}
        f = factor_sb(g, s)
        m, b, c1 = f[:, 0:512], f[:, 512:576], f[:, 576:584]
        v.tensor_tensor(a1, s1, vec[4], ALU.add)
        v.tensor_tensor(b1, s1, vec[3], ALU.add)
        link(v.tensor_tensor(c1, s1, vec[2], ALU.add))
        outer(a2, a1, vec[3], CH)
        outer(b2, b1, vec[2], CH)
        outer(n2, c1, vec[1], CH)
        link(v.tensor_tensor(s1, s1, vec[1], ALU.add))
        v.tensor_tensor(a2, a2, s2, ALU.add)
        link(v.tensor_tensor(b, b2, s2, ALU.add))
        v.tensor_tensor(s2, s2, n2, ALU.add)
        outer(n3, b, vec[1], CH ** 2)
        link(outer(a3, a2, vec[2], CH ** 2))
        v.tensor_tensor(m, a3, s3, ALU.add).then_inc(g.factor_ready, 1)
        link(v.tensor_tensor(s3, s3, n3, ALU.add))

    def combine(t, s, link):
        token = g.a[:, bass.ds(t + 1, 1), :]
        v.wait_ge(g.token_ready, t + 2)
        v.wait_ge(g.product_done, t + 1)
        for c in range(CH):
            before = g.a[:, bass.ds(t, 1), :] if c == 0 else token
            ins = v.scalar_tensor_tensor(token, g.ps[s][:, 2 + c // 4:3 + c // 4, (c % 4) * D:(c % 4 + 1) * D],
                                         parts[1][:, bass.ds(t * CH + c, 1)], before, ALU.mult, ALU.add)
            if c < CH - 1:
                link(ins)
        ins.then_inc(g.token_ready, 1)

    ahead, link = Link(v, g.factor_link, 0, FACTOR_LINKS), Link(v, g.moe_link, START_LINKS, COMBINE_LINKS)
    for t in range(2):
        ahead.group(t)
        factors(t, t, ahead)

    def step(t, s, after):
        if after == 2:
            v.wait_ge(g.factor_turned, t + 1)
            ahead.group(t + 2)
            factors(t + 2, s, ahead)
        link.group(t)
        combine(t, s, link)

    steps_loop(v, step)
PE = {"TOK": tok_pe, **{st: moe_pe(st) for st in MOE}, "L0A": l0a_pe, "L2A": l2a_pe, "L1A": l1a_pe, "L2F": l2f_pe, "L3A": l3a_pe, "L3F": l3f_pe}
ACTS = {"TOK": tok_act, **{st: moe_act(st) for st in MOE}, "L0A": l0a_act, "L2A": l2a_act, "L1A": l1a_act, "L2F": l2f_act, "L3A": l3a_act, "L3F": l3f_act}
DVE = {"TOK": tok_dve, **{st: moe_dve(st) for st in MOE}, "L0A": l0a_dve, "L2A": l2a_dve, "L1A": l1a_dve, "L2F": l2f_dve, "L3A": l3a_dve, "L3F": l3f_dve}


def more_semaphores(g, sem):
    g.m_down_done, g.m_latent_ready, g.m_latent_turned, g.m_latentT_ready, g.m_qk_done, g.m_qk_ready, g.m_v_done, g.m_v_ready = (
        sem("m_" + n) for n in ("down_done", "latent_ready", "latent_turned", "latentT_ready", "qk_done", "qk_ready",
                                "v_done", "v_ready"))
    (g.f_conv_ready, g.f_qk_done, g.f_q_ready, g.f_k_ready, g.f_v_done, g.f_v_ready, g.f_exp_ready) = (
        sem("f_" + n) for n in ("conv_ready", "qk_done", "q_ready", "k_ready", "v_done", "v_ready", "exp_ready"))
    g.w_qk_done, g.w_q_ready, g.w_k_ready, g.w_v_done, g.w_v_ready = (
        sem("w_" + n) for n in ("qk_done", "q_ready", "k_ready", "v_done", "v_ready"))
    g.p_q_done, g.p_k_done, g.p_q_ready, g.p_k_ready, g.p_v_done, g.p_v_ready = (
        sem("p_" + n) for n in ("q_done", "k_done", "q_ready", "k_ready", "v_done", "v_ready"))
    g.moe = moe_semaphores(sem, [st for st in g.stages if st in MOE])
    (g.l_low_done, g.l_low_ready, g.l_gk_done, g.l_gk_read, g.l_log_ready, g.l_sum_ready, g.l_neg_exp, g.l_exp_ready, g.l_inverse_ready, g.l_qk_done,
     g.l_qk_ready, g.l_v_done, g.l_v_ready, g.l_g_done, g.l_silu_ready, g.l_scores_done, g.l_scores_ready, g.l_o_done,
     g.l_sq_ready, g.l_og_ready, g.l_og_turned, g.l_ogT_ready_a, g.l_ogT_ready_v, g.l_out_done, g.l_fold) = (
         sem("l_" + n) for n in (
             "low_done", "low_ready", "gk_done", "gk_read", "log_ready", "sum_ready", "neg_exp", "exp_ready", "inverse_ready", "qk_done", "qk_ready",
             "v_done", "v_ready", "g_done", "silu_ready", "scores_done", "scores_ready", "o_done", "sq_ready", "og_ready",
             "og_turned", "ogT_ready_a", "ogT_ready_v", "out_done", "fold"))
    g.lora_pe, g.lora_dve = sem("lora_pe"), sem("lora_dve")



def audio_tower_kernel(nc, ins, out, batch):
    g = Net()
    stages = STAGES
    g.groups = batch * SEQ // GTOK
    tiles = g.groups * GT
    with ExitStack() as ctx:
        def sb(name, shape):
            return ctx.enter_context(nc.sbuf_tensor(name, shape, F32))

        def sem(name):
            return ctx.enter_context(nc.semaphore(name))

        g.h = sb("h", [P, tiles, D])
        g.a = sb("a", [P, max(tiles, 48), D])
        consts, n_const = columns("const")
        const_sb = sb("const_sb", [P, n_const])
        widths = [columns(st)[1] for st in ATTN_STAGES]
        w_attn = [sb(f"w_attn{i}", [P, max(widths[i::2])]) for i in range(2)]
        g.w_big = sb("w_big", [P, W_BIG])
        g.cs = sb("cs", [P, D])

        def slots(name, shape):
            return [sb(f"{name}{s}", shape) for s in range(SLOTS)]

        g.xn, g.xT = slots("xn", [P, GT, D]), slots("xT", [P, GTOK])
        g.qk, g.v2 = slots("qk", [P, 4, GTOK]), slots("v2", [P, 2 * GT, 4, 2, DH + 1])
        g.pr, g.pt = slots("pr", [P, 4 * GTOK]), slots("pt", [P, 4 * GTOK])
        g.o, g.oT, g.t2 = slots("o", [P, GT, D]), slots("oT", [P, GTOK]), slots("t2", [P, GT, D])
        g.of = [g.o[s][:, :, :].rearrange("p t d -> p (t d)") for s in range(SLOTS)]
        g.stats, g.mv = slots("stats", [P, 16, 6]), slots("mv", [P, 16, 2])
        g.ra, g.rs, g.rq, g.rm = (slots(n, [P, 32]) for n in ("ra", "rs", "rq", "rm"))
        g.small, g.gates = slots("small", [P, 256]), slots("gates", [P, GT * EXPERTS])

        g.ps = [ctx.enter_context(nc.psum_tensor(f"ps{s}", [P, 4, 512], F32)) for s in range(SLOTS)]
        g.psf = [g.ps[s][:, :, :].rearrange("p b c -> p (b c)") for s in range(SLOTS)]

        def c(name):
            at, n = consts[name]
            return const_sb[:, at:at + n]

        def w(stage, name):
            cols, _ = columns(stage)
            at, n = cols[name]
            return w_attn[ATTN_STAGES.index(stage) % 2][:, at:at + n]

        def heads(s):
            return g.psf[s][:, 0:1024].rearrange("p (t c) -> p t c", t=GT)[:, :, 0:8 * (DH + 1)]\
                    .rearrange("p t (b e) -> p t b e", e=DH + 1)

        g.c, g.w, g.heads = c, w, heads
        grouped = [st for st in stages if st != "TOK"]
        g.n0 = {st: i * g.groups for i, st in enumerate(grouped)}
        soft = [st for st in stages if st in ("L0A", "L1A", "L2F", "L3A", "L3F")]
        g.k0 = {st: i * g.groups for i, st in enumerate(soft)}
        g.uncentred = g.groups
        moes = [st for st in stages if st in MOE]
        g.m0 = {st: i * g.groups for i, st in enumerate(moes)}
        g.stages, g.tails = stages, {}
        g.link0 = {}
        at_slot, at_moe = 0, START_LINKS + STEPS * COMBINE_LINKS
        for st in grouped:
            if st in MOE:
                g.link0[st] = at_moe
                at_moe += g.groups * MOE[st].links
            else:
                g.link0[st] = at_slot
                at_slot += g.groups // SLOTS * LINKS[st]

        g.const_loaded, g.h_zero, g.h_loaded, g.v2_ones = sem("const_loaded"), sem("h_zero"), sem("h_loaded"), sem("v2_ones")
        g.attn_loaded, g.big_loaded = [sem(f"attn_loaded{i}") for i in range(2)], sem("big_loaded")
        g.slot_free, g.xn_ready, g.xn_transposed, g.xT_ready = (sem(n) for n in (
            "slot_free", "xn_ready", "xn_transposed", "xT_ready"))
        g.slot_link, g.moe_link = [sem(f"slot_link{s}") for s in range(SLOTS)], sem("moe_link")
        g.out_stored = sem("out_stored")
        g.r_qk_done, g.r_q_ready, g.r_k_ready, g.r_v_done, g.r_g_done, g.r_g_ready, g.r_silu_ready = (
            sem("r_" + n) for n in ("qk_done", "q_ready", "k_ready", "v_done", "g_done", "g_ready", "silu_ready"))
        g.r_x1_ready, g.r_x1_turned, g.r_x1T_ready = (sem("r_" + n) for n in ("x1_ready", "x1_turned", "x1T_ready"))
        g.r_fc1_done, g.r_gelu_ready, g.r_squares_ready, g.r_squares_half, g.r_z_ready, g.r_fc2_done = (
            sem("r_" + n) for n in ("fc1_done", "gelu_ready", "squares_ready", "squares_half", "z_ready", "fc2_done"))
        g.fold_dve, g.fold_pe = sem("fold_dve"), sem("fold_pe")
        g.scores_done, g.centred_ready, g.probs_ready, g.probs_turned, g.pt_ready_a, g.pt_ready_v, g.values_weighed = (
            sem(n) for n in ("scores_done", "centred_ready", "probs_ready", "probs_turned", "pt_ready_a", "pt_ready_v",
                             "values_weighed"))
        g.o_ready, g.o_turned, g.oT_ready, g.out_done = (sem(n) for n in ("o_ready", "o_turned", "oT_ready", "out_done"))
        more_semaphores(g, sem)
        g.wait_carrier, g.wait_carrier_pe = sem("wait_carrier"), sem("wait_carrier_pe")
        g.factor_link = sem("factor_link")
        g.x_loaded, g.factor_ready, g.factor_turned, g.factorT_ready, g.product_done, g.token_ready, g.tokens_stored = (
            sem(n) for n in ("x_loaded", "factor_ready", "factor_turned", "factorT_ready", "product_done", "token_ready",
                             "tokens_stored"))
        g.tokens = nc.dram_tensor("tokens", (batch, TOK, D), F32, kind="Internal").ap()

        h_rows = lambda dram: dram.rearrange("(t q) s d -> q s t d", q=2)
        block = ctx.enter_context(nc.Block())

        @block.sync
        def _(sp):
            through = lambda st: SLOTS + g.n0[st] + g.groups

            def load_weights(st):
                if st in ATTN_STAGES:
                    same = [e for e in grouped if e in ATTN_STAGES
                            and ATTN_STAGES.index(e) % 2 == ATTN_STAGES.index(st) % 2]
                    region, loaded = w_attn[ATTN_STAGES.index(st) % 2], g.attn_loaded[ATTN_STAGES.index(st) % 2]
                else:
                    same = [e for e in grouped if e not in ATTN_STAGES]
                    region, loaded = g.w_big, g.big_loaded
                before = same[:same.index(st)] if st in same else []
                if before:
                    sp.wait_ge(g.slot_free, through(before[-1]))
                elif st in MOE:
                    sp.wait_ge(g.token_ready, STEPS + 2)
                sp.dma_start(region[:, 0:ins[st].shape[1]], ins[st]).then_inc(loaded, 16)

            sp.dma_start(g.t2[0][:, :, :].rearrange("p t d -> p (t d)"), ins["x"]).then_inc(g.x_loaded, 16)
            sp.dma_start(const_sb[:, :], ins["const"]).then_inc(g.const_loaded, 16)
            load_weights("TOK")
            load_weights(grouped[0])
            sp.wait_ge(g.h_zero, 1)
            for c in range(STEPS // TOK_CHUNK):
                steps = slice(c * TOK_CHUNK, (c + 1) * TOK_CHUNK)
                sp.wait_ge(g.token_ready, (c + 1) * TOK_CHUNK + 2)
                sp.dma_start(g.tokens[:, steps, :], g.a[:, c * TOK_CHUNK + 1:(c + 1) * TOK_CHUNK + 1, :])\
                  .then_inc(g.tokens_stored, 16)
                sp.wait_ge(g.tokens_stored, 16 * (c + 1))
                for q in range(2):
                    sp.dma_start(g.h[64 * q + c * TOK_CHUNK:64 * q + (c + 1) * TOK_CHUNK, :, :],
                                 h_rows(g.tokens)[q][steps, :, :]).then_inc(g.h_loaded, 16)
            for st in grouped[1:]:
                load_weights(st)
            for part in range(g.groups // 2):
                sp.wait_ge(g.slot_free, SLOTS + g.n0[grouped[-1]] + 2 * (part + 1))
                for q in range(2):
                    rows = slice(2 * part * GT, 2 * (part + 1) * GT)
                    sp.dma_start(h_rows(out)[q][:, rows, :], g.h[64 * q:64 * q + TOK, rows, :]).then_inc(g.out_stored, 16)
            sp.wait_ge(g.out_stored, 16 * g.groups)

        def wait_weights(eng, st):
            if st in ATTN_STAGES:
                i = ATTN_STAGES.index(st) % 2
                eng.wait_ge(g.attn_loaded[i], 16 * (1 + len([e for e in stages[:stages.index(st)] if e in ATTN_STAGES[i::2]])))
            else:
                eng.wait_ge(g.big_loaded, 16 * (1 + len([e for e in stages[:stages.index(st)] if e not in ATTN_STAGES])))

        @block.gpsimd
        def _(pool):
            pool.memset(g.h[:, :, :], 0.0).then_inc(g.h_zero, 1)
            for s in range(SLOTS):
                ins_ = pool.memset(g.v2[s][:, :, :, :, :], 0.0)
            ins_.then_inc(g.v2_ones, 1)
            pool.wait_ge(g.v2_ones, 1)
            pool.wait_ge(g.const_loaded, 16)
            for s in range(SLOTS):
                for half in range(2):
                    rows = slice(64 * half, 64 * half + 64)
                    ins_ = pool.tensor_copy(g.v2[s][rows, :, :, half, DH],
                                            c("live")[rows, :].unsqueeze(2).to_broadcast([64, 2 * GT, 4]))
            ins_.then_inc(g.v2_ones, 1)
            l0a_pool(g, pool)
            end_tail(g, pool)

        @block.tensor
        def _(pe):
            pe.wait_ge(g.const_loaded, 16)
            pe.wait_ge(g.v2_ones, 2)
            for st in stages:
                if st in MOE:
                    end_tail(g, pe)
                wait_weights(pe, st)
                PE[st](g, pe)
            end_tail(g, pe)

        @block.scalar
        def _(a):
            a.wait_ge(g.const_loaded, 16)
            for st in stages:
                if st in MOE:
                    end_tail(g, a)
                wait_weights(a, st)
                ACTS[st](g, a)
            end_tail(g, a)

        @block.vector
        def _(v):
            v.wait_ge(g.const_loaded, 16)
            v.memset(g.rm[0][:, :], 0.0).then_inc(g.slot_free, SLOTS)
            for st in stages:
                if st in MOE:
                    end_tail(g, v)
                wait_weights(v, st)
                if st == grouped[0]:
                    v.wait_ge(g.h_loaded, 32 * (STEPS // TOK_CHUNK))
                DVE[st](g, v)
            end_tail(g, v)



MLA_Q, MLA_K = [0, 0, 1, 1, 1, 1, 0, 0], [0, 1, 0, 1, 1, 0, 1, 0]
ROPE_Q, ROPE_Q_OTHER, ROPE_K = [0, 0, 1, 1], [1, 1, 0, 0], [0, 1, 1, 0]

def host_more(X, arrays, pack, row, col, pad_heads, swap_pairs):
    import numpy as np
    f32 = np.float32
    W = X["L0_tok_W"]
    w = np.zeros((P, len(CHUNKS), CH, D), f32)
    at = 0
    levels = []
    for size in (1, CH, CH ** 2, CH ** 3):
        levels.append(W[:, at:at + size * CH].reshape(D, size, CH).transpose(1, 2, 0))
        at += size * CH
    rows = np.concatenate(levels[::-1])
    for k, (lo, n) in enumerate(CHUNKS):
        w[:n, k] = rows[lo:lo + n]
    arrays["TOK"] = np.concatenate([w.reshape(P, -1), row(X["L0_tok_b"])], 1)
    x = np.zeros((P, SEQ, CH), f32)
    x[:, :, 0] = np.linspace(0.0, 1.0, SEQ, dtype=f32)
    x[:, :, 1:] = X["x"]
    arrays["x"] = x.reshape(P, -1)
    L = lambda n: X["L1_attn_" + n]
    picked = lambda wt, order: pad_heads(wt.reshape(wt.shape[0], HEADS, 2)[:, :, order].reshape(wt.shape[0], -1), 8, DH)
    arrays["L1A"] = pack("L1A", {
        "down": np.concatenate([L("W_dq"), L("W_dkv")], 1),
        "q": merge(pad_heads(L("W_uq")), picked(L("W_qr"), MLA_Q), DH, 8),
        "kn": pad_heads(L("W_ukv")[:, :D]), "kr": picked(L("W_kr"), MLA_K),
        "v": L("W_ukv")[:, D:], "wo": L("W_o").T, "qg": L("q_ln_g")[:, None], "qbias": L("q_ln_b")[:, None],
        "kg": L("kv_ln_g")[:, None], "kbias": L("kv_ln_b")[:, None]})
    L = lambda n: X["L2_attn_" + n]
    arrays["L2A"] = pack("L2A", {
        "qk": np.concatenate([L("Wq"), L("Wk")], 1), "gk1": L("Wgk1"), "gk2": L("Wgk2"),
        "gkb": L("bgk2").reshape(2, P).T, "v": L("Wv"), "g": L("Wg"),
        "wo": L("Wo").reshape(GH, GV, D).transpose(1, 0, 2), "rms": L("rms_w")[:, None]})
    L = lambda n: X["L2_ffn_" + n]
    wq, wk, wv = (L("qkv_w")[i * D:(i + 1) * D].T for i in range(3))
    bq, bk, bv = (L("qkv_b")[i * D:(i + 1) * D] for i in range(3))
    arrays["L2F"] = pack("L2F", {
        "qk": np.concatenate([pad_heads(wq), pad_heads(wk)], 1), "v": wv, "wo": L("wo_w").T,
        "conv": L("pos_w")[:, 0, :], "convb": L("pos_b")[:, None],
        "qkb": np.concatenate([pad_heads(bq[None]).reshape(2, P), pad_heads(bk[None]).reshape(2, P)]).T,
        "bv": bv[:, None], "bo": row(L("wo_b"))})
    L = lambda n: X["L3_attn_" + n]
    third = lambda wt, i: wt[:, i * D:(i + 1) * D]
    heads = lambda wt: np.concatenate([pad_heads(third(wt, 0)), pad_heads(third(wt, 1))], 1)
    arrays["L3A"] = pack("L3A", {
        "qk": heads(L("w_qkv")), "v": third(L("w_qkv"), 2), "wo": L("w_out"), "la": L("lora_A_qkv").T,
        "lbqk": heads(L("lora_B_qkv")), "lbv": third(L("lora_B_qkv"), 2), "loa": L("lora_A_out").T,
        "lob": L("lora_B_out"), "bo": row(L("b_out"))})
    L = lambda n: X["L3_ffn_" + n]
    picked = lambda wt, order: pad_heads(
        wt.reshape(wt.shape[0], -1, 2)[:, :, order].reshape(wt.shape[0], -1), 2 * DH)
    arrays["L3F"] = pack("L3F", {
        "qk": np.concatenate([picked(L("wq"), ROPE_Q), picked(L("wk"), ROPE_K)], 1),
        "qr": picked(L("wq"), ROPE_Q_OTHER),
        "v": L("wv"), "wo": L("wo"), "nw": L("attn_norm_w")[:, None]})
    by_rows = lambda a: a.reshape(EXPERTS, -1, P, a.shape[-1]).transpose(2, 0, 1, 3)
    biases = lambda a: a.reshape(-1, P).T

    def mixture(stage, parts):
        m = MOE[stage]
        a = np.zeros((P, m.width), f32)
        for name, (at, n) in m.cols.items():
            part = parts[name].reshape(parts[name].shape[0], -1)
            assert part.shape[1] == n, (name, part.shape, n)
            a[:part.shape[0], at:at + n] = part
        arrays[stage] = a

    L = lambda n: X["L0_ffn_" + n]
    mixture("L0M", {"up": by_rows(L("gate_up_proj")), "down": by_rows(L("down_proj")), "router": L("router_w"),
                    "rb": row(L("router_b")), "ub": biases(L("gate_up_proj_bias")), "db": L("down_proj_bias"),
                    "sb": biases(L("gate_up_proj_bias"))})
    L = lambda n: X["L1_ffn_" + n]
    mixture("L1M", {"up": by_rows(L("w1")), "down": by_rows(L("w2")), "router": L("gate_w"), "rb": row(L("gate_b")),
                    "ub": biases(L("b1")), "db": L("b2")})
    L = lambda n: X["L3_ffn_" + n]
    mixture("L3M", {"up": by_rows(L("w1")), "down": by_rows(L("w2")), "router": L("router_w"),
                    "nw": L("ffn_norm_w")[:, None]})


def merge(base, other, at, width):
    a = base.reshape(base.shape[0], HEADS, 32).copy()
    a[:, :, at:at + width] = other.reshape(base.shape[0], HEADS, 32)[:, :, at:at + width]
    return a.reshape(base.shape)


def host_arrays(X):
    import numpy as np
    f32 = np.float32

    def pack(stage, parts):
        cols, total = columns(stage)
        assert set(parts) == set(cols), set(parts) ^ set(cols)
        a = np.zeros((P, total), f32)
        for name, part in parts.items():
            at, n = cols[name]
            part = np.asarray(part)
            part = part.reshape(part.shape[0], -1)
            assert part.shape[1] == n and part.shape[0] <= P, (stage, name, part.shape)
            a[:part.shape[0], at:at + n] = part
        return a

    def row(vec):
        return np.broadcast_to(vec, (P, vec.shape[0]))

    def pad_heads(wt, width=DH, at=0):
        a = np.zeros((wt.shape[0], 2, 4, 32), f32)
        a[..., at:at + width] = wt.reshape(wt.shape[0], 2, 4, width)
        return a.reshape(wt.shape[0], 2 * P)

    def swap_pairs(wt):
        return wt.reshape(wt.shape[0], -1, 2)[:, :, ::-1].reshape(wt.shape)

    arrays = {}
    i = np.arange(SEQ)
    diff = (i[:, None] - i[None, :]).astype(f32)
    decay = np.log(1.0 - 2.0 ** (-5.0 - np.arange(HEADS))).astype(f32)
    dm = np.where(diff[None] >= 0, np.exp(diff[None] * decay[:, None, None]), 0.0)
    dm = (dm / np.sqrt(dm[:, :, :TOK].sum(-1, keepdims=True))).astype(f32)
    causal = np.where(diff >= 0, 0.0, NEG).astype(f32)
    ang = i.astype(f32)
    mla_q, mla_k = np.ones((P, SEQ), f32), np.ones((P, SEQ), f32)
    rc, rsn, rk = np.zeros((P, SEQ), f32), np.zeros((P, SEQ), f32), np.zeros((P, SEQ), f32)
    for r in range(4):
        cos, sin = np.cos(ang), np.sin(ang)
        mla_q[32 * r + DH:32 * r + DH + 8] = [cos, cos, -sin, -sin, cos, cos, sin, sin]
        mla_k[32 * r + DH:32 * r + DH + 8] = [cos, -sin, cos, -sin, cos, sin, cos, sin]
        for m in range(DH // 2):
            turn = ang * f32(1.0 / 10000.0 ** (2 * m / DH))
            cos, sin, at = np.cos(turn), np.sin(turn), 32 * r + 4 * m
            rc[at:at + 4] = [cos, cos, cos, cos]
            rsn[at:at + 4] = [-sin, -sin, sin, sin]
            rk[at:at + 4] = [cos, -sin, cos, sin]
    restart = np.ones((P, GTOK), f32)
    restart[:, ::SEQ] = 0.0
    two = lambda t: np.concatenate([t, t], 0)
    arrays["const"] = pack("const", {
        "ident": np.eye(P, dtype=f32), "ones": np.ones((P, P), f32),
        "dm": two(dm.reshape(2, 4, SEQ, SEQ).transpose(2, 1, 0, 3).reshape(SEQ, HEADS * SEQ)), "causal": two(causal),
        "live": two((i < TOK).astype(f32)[:, None]), "upper": two((diff.T >= 0).astype(f32)), "restart": restart,
        "mla_q": mla_q, "mla_k": mla_k, "rope_cos": rc, "rope_sin": rsn, "rope_k": rk})
    col = lambda vec: vec.reshape(-1, P).T
    L = lambda n: X["L0_attn_" + n]
    bv = np.zeros((2, 64, 64), f32)
    bv[:, :TOK] = L("bv").reshape(2, 1, 64)
    fc2 = np.ones((P, 4, 129), f32)
    fc2[:, :, :D] = L("fc2_w").T.reshape(4, P, D).transpose(1, 0, 2)
    arrays["L0A"] = pack("L0A", {
        "qk": np.concatenate([pad_heads(L("wq").T), pad_heads(L("wk").T)], 1), "v": L("wv").T,
        "g": L("wg").T, "wo": L("wo").T, "fc1": L("fc1_w").T, "fc2": fc2,
        "qkb": np.concatenate([pad_heads(L("bq")[None]).reshape(2, P), pad_heads(L("bk")[None]).reshape(2, P)]).T,
        "bv": bv.reshape(P, 64), "bg": row(L("bg")), "bo": row(L("bo")), "n0g": row(L("n0_g")), "n0b": row(L("n0_b")),
        "n1g": row(L("n1_g")), "n1b": row(L("n1_b")), "fc1b": col(L("fc1_b")), "fc2b": row(L("fc2_b")),
        "fg": col(L("ln_ffn_g")), "fb": col(L("ln_ffn_b"))})
    host_more(X, arrays, pack, row, col, pad_heads, swap_pairs)
    return arrays


STAGES = ("TOK", "L0A", "L0M", "L1A", "L1M", "L2A", "L2F", "L3A", "L3F", "L3M")


def kernel(**inputs):
    import numpy as np
    import concourse.bacc as bacc
    from concourse.bass_utils import run_bass_kernel_spmd

    nc = bacc.Bacc("TRN2", target_bir_lowering=False, num_devices=1)
    arrays = {name: np.ascontiguousarray(a) for name, a in host_arrays({k: np.asarray(v) for k, v in inputs.items()}).items()}
    batch = inputs["x"].shape[0]
    ins = {name: nc.dram_tensor("in_" + name, a.shape, mybir.dt.from_np(a.dtype), kind="ExternalInput").ap()
           for name, a in arrays.items()}
    out = nc.dram_tensor("out", (batch, TOK, D), F32, kind="ExternalOutput").ap()
    audio_tower_kernel(nc, ins, out, batch)
    return run_bass_kernel_spmd(nc, [{"in_" + name: a for name, a in arrays.items()}], core_ids=[0]).results[0]["out"]
```
